# Optimizing a Trainium2 kernel written in Bass

```python
import numpy as np
import jax
import jax.numpy as jnp

def _softmax(x, axis=-1):
    return jax.nn.softmax(x, axis=axis)

def _gelu(x):
    return jax.nn.gelu(x, approximate=True)

def _silu(x):
    return jax.nn.silu(x)

def _sigmoid(x):
    return jax.nn.sigmoid(x)

def _layernorm(x, axis=-1, eps=1e-05):
    m = jnp.mean(x, axis=axis, keepdims=True)
    v = jnp.var(x, axis=axis, keepdims=True)
    return (x - m) / jnp.sqrt(v + eps)

def _scatter_add(tgt, idx, src, axis=0):
    return tgt.at[idx].add(src)

def _segment_sum(src, seg, n):
    return jax.ops.segment_sum(src, seg, n)
kernel_name = 'mk_gnn_resnorm_d4_gnn_r32_0d4022'

def setup_inputs(seed: int=0):
    np.random.seed(seed)
    _w = jnp.asarray

    def _rec_inputs():
        import jax
        import jax.numpy as jnp
        _gk = jax.random.key(seed)
        x = -0.000202 + 1 * jax.random.normal(jax.random.fold_in(_gk, 1), (3125, 64), jnp.float32)
        src = jax.random.randint(jax.random.fold_in(_gk, 2), (100000,), 0, 3125, jnp.int32)
        dst = jax.random.randint(jax.random.fold_in(_gk, 3), (100000,), 0, 3125, jnp.int32)
        _o = jnp.argsort(dst, stable=True)
        src = src[_o]
        dst = dst[_o]
        edge_attr_2 = 0.000452788 + 0.999756 * jax.random.normal(jax.random.fold_in(_gk, 11), (100000, 2), jnp.float32)
        edge_attr_64 = -9.77346e-05 + 0.999888 * jax.random.normal(jax.random.fold_in(_gk, 12), (100000, 64), jnp.float32)
        edge_type_4 = jax.random.randint(jax.random.fold_in(_gk, 14), (100000,), 0, 4, jnp.int32)
        return (x, src, dst, edge_attr_2, edge_attr_64, edge_type_4)
    x, src, dst, edge_attr_2, edge_attr_64, edge_type_4 = _rec_inputs()

    def _L0_gnn_setup():
        import jax, jax.numpy as jnp
        import numpy as np
        N_NODES = 3125
        N_EDGES = 50000
        IN_DIM = 64
        HID_DIM = 64
        OUT_DIM = 64

        def _gin_conv(h, src, dst, W, b, num_nodes):
            agg = jax.ops.segment_sum(h[src], dst, num_segments=num_nodes)
            return jax.nn.relu((h + agg) @ W + b)
        key = jax.random.key(seed)
        k_x, k_e, k_w1, k_b1, k_w2, k_b2 = jax.random.split(key, 6)
        x = jax.random.normal(k_x, (N_NODES, IN_DIM), dtype=jnp.float32)
        edge_index = jax.random.randint(k_e, (2, N_EDGES), 0, N_NODES, dtype=jnp.int64)
        W1 = jax.random.normal(k_w1, (IN_DIM, HID_DIM), dtype=jnp.float32) / np.sqrt(IN_DIM)
        b1 = jax.random.normal(k_b1, (HID_DIM,), dtype=jnp.float32) * 0.01
        W2 = jax.random.normal(k_w2, (HID_DIM, OUT_DIM), dtype=jnp.float32) / np.sqrt(HID_DIM)
        b2 = jax.random.normal(k_b2, (OUT_DIM,), dtype=jnp.float32) * 0.01
        return {'x': x, 'edge_index': edge_index, 'W1': W1, 'b1': b1, 'W2': W2, 'b2': b2}
    _L0_gnn_all = _L0_gnn_setup()
    _L0_gnn_in = {k: v for k, v in _L0_gnn_all.items() if k in ('W1', 'b1', 'W2', 'b2')}
    del _L0_gnn_all

    def _L1_gnn_setup():
        import jax, jax.numpy as jnp
        import numpy as np
        N_NODES = 3125
        N_EDGES = 1250000
        D_FEAT = 64

        def _aggregate(x, src, dst, num_nodes):
            return jax.ops.segment_sum(x[src], dst, num_segments=num_nodes)
        key = jax.random.key(seed)
        kx, ke = jax.random.split(key)
        x = jax.random.normal(kx, (N_NODES, D_FEAT), dtype=jnp.float32)
        edge_index = jax.random.randint(ke, (2, N_EDGES), 0, N_NODES, dtype=jnp.int64)
        return {'x': x, 'edge_index': edge_index}
    _L1_gnn_all = _L1_gnn_setup()
    _L1_gnn_in = {k: v for k, v in _L1_gnn_all.items() if k in ()}
    del _L1_gnn_all

    def _L2_gnn_setup():
        import jax, jax.numpy as jnp
        import numpy as np
        N = 50000
        E = 25000
        C = 64
        SPACEDIM = 2
        LN_EPS = 1e-05

        def _mlp(x, Wh, bh, Wo, bo, ln_w, ln_b):
            for i in range(Wh.shape[0]):
                x = jax.nn.relu(x @ Wh[i] + bh[i])
            x = x @ Wo + bo
            mu = jnp.mean(x, axis=-1, keepdims=True)
            var = jnp.var(x, axis=-1, keepdims=True)
            return (x - mu) * jax.lax.rsqrt(var + LN_EPS) * ln_w + ln_b
        key = jax.random.key(seed)
        ks = jax.random.split(key, 16)
        s = 1.0 / np.sqrt(C)
        inp = {'x': jax.random.normal(ks[0], (N, C), jnp.float32), 'e': jax.random.normal(ks[1], (E, C), jnp.float32), 'nvec': jax.random.normal(ks[2], (E, SPACEDIM), jnp.float32), 'edge_index': jax.random.randint(ks[3], (2, E), 0, N, jnp.int64), 'flux_Wh': jax.random.normal(ks[4], (3, C, C), jnp.float32) * s, 'flux_bh': jax.random.normal(ks[5], (3, C), jnp.float32) * s, 'flux_Wo': jax.random.normal(ks[6], (C, C * SPACEDIM), jnp.float32) * s, 'flux_bo': jax.random.normal(ks[7], (C * SPACEDIM,), jnp.float32) * s, 'flux_ln_w': jnp.ones((C * SPACEDIM,), jnp.float32), 'flux_ln_b': jnp.zeros((C * SPACEDIM,), jnp.float32), 'a_Wh': jax.random.normal(ks[8], (3, C, C), jnp.float32) * s, 'a_bh': jax.random.normal(ks[9], (3, C), jnp.float32) * s, 'a_Wo': jax.random.normal(ks[10], (C, C), jnp.float32) * s, 'a_bo': jax.random.normal(ks[11], (C,), jnp.float32) * s, 'a_ln_w': jnp.ones((C,), jnp.float32), 'a_ln_b': jnp.zeros((C,), jnp.float32)}
        return inp
    _L2_gnn_all = _L2_gnn_setup()
    _L2_gnn_in = {k: v for k, v in _L2_gnn_all.items() if k in ('flux_Wh', 'flux_bh', 'flux_Wo', 'flux_bo', 'flux_ln_w', 'flux_ln_b', 'a_Wh', 'a_bh', 'a_Wo', 'a_bo', 'a_ln_w', 'a_ln_b')}
    del _L2_gnn_all

    def _L3_gnn_setup():
        import jax, jax.numpy as jnp
        import numpy as np
        DIM = 64
        NUM_HEADS = 4
        HEAD_DIM = DIM // NUM_HEADS
        SCALE = HEAD_DIM ** (-0.5)
        NUM_EDGE_TYPES = 4
        N = 3125
        E = 1250000
        key = jax.random.key(seed)
        ks = jax.random.split(key, 12)
        s = 1.0 / np.sqrt(DIM)
        inp = {'x': jax.random.normal(ks[0], (N, DIM), dtype=jnp.float32), 'edge_index': jax.random.randint(ks[1], (2, E), 0, N, dtype=jnp.int64 if jax.config.read('jax_enable_x64') else jnp.int32), 'edge_type': jax.random.randint(ks[2], (E,), 0, NUM_EDGE_TYPES), 'num_nodes': N, 'Wq': jax.random.uniform(ks[3], (DIM, DIM), jnp.float32, -s, s), 'bq': jax.random.uniform(ks[4], (DIM,), jnp.float32, -s, s), 'Wk': jax.random.uniform(ks[5], (DIM, DIM), jnp.float32, -s, s), 'bk': jax.random.uniform(ks[6], (DIM,), jnp.float32, -s, s), 'Wv': jax.random.uniform(ks[7], (DIM, DIM), jnp.float32, -s, s), 'bv': jax.random.uniform(ks[8], (DIM,), jnp.float32, -s, s), 'Wo': jax.random.uniform(ks[9], (DIM, DIM), jnp.float32, -s, s), 'bo': jax.random.uniform(ks[10], (DIM,), jnp.float32, -s, s), 'edge_bias': jax.random.normal(ks[11], (NUM_EDGE_TYPES, NUM_HEADS), dtype=jnp.float32)}
        return inp
    _L3_gnn_all = _L3_gnn_setup()
    _L3_gnn_in = {k: v for k, v in _L3_gnn_all.items() if k in ('Wq', 'bq', 'Wk', 'bk', 'Wv', 'bv', 'Wo', 'bo', 'edge_bias')}
    del _L3_gnn_all
    return {'x': x, 'src': src, 'dst': dst, 'edge_attr_2': edge_attr_2, 'edge_attr_64': edge_attr_64, 'edge_type_4': edge_type_4, 'L0_gnn_W1': _L0_gnn_in['W1'], 'L0_gnn_b1': _L0_gnn_in['b1'], 'L0_gnn_W2': _L0_gnn_in['W2'], 'L0_gnn_b2': _L0_gnn_in['b2'], 'L2_gnn_flux_Wh': _L2_gnn_in['flux_Wh'], 'L2_gnn_flux_bh': _L2_gnn_in['flux_bh'], 'L2_gnn_flux_Wo': _L2_gnn_in['flux_Wo'], 'L2_gnn_flux_bo': _L2_gnn_in['flux_bo'], 'L2_gnn_flux_ln_w': _L2_gnn_in['flux_ln_w'], 'L2_gnn_flux_ln_b': _L2_gnn_in['flux_ln_b'], 'L2_gnn_a_Wh': _L2_gnn_in['a_Wh'], 'L2_gnn_a_bh': _L2_gnn_in['a_bh'], 'L2_gnn_a_Wo': _L2_gnn_in['a_Wo'], 'L2_gnn_a_bo': _L2_gnn_in['a_bo'], 'L2_gnn_a_ln_w': _L2_gnn_in['a_ln_w'], 'L2_gnn_a_ln_b': _L2_gnn_in['a_ln_b'], 'L3_gnn_Wq': _L3_gnn_in['Wq'], 'L3_gnn_bq': _L3_gnn_in['bq'], 'L3_gnn_Wk': _L3_gnn_in['Wk'], 'L3_gnn_bk': _L3_gnn_in['bk'], 'L3_gnn_Wv': _L3_gnn_in['Wv'], 'L3_gnn_bv': _L3_gnn_in['bv'], 'L3_gnn_Wo': _L3_gnn_in['Wo'], 'L3_gnn_bo': _L3_gnn_in['bo'], 'L3_gnn_edge_bias': _L3_gnn_in['edge_bias']}

def reference(x, src, dst, edge_attr_2, edge_attr_64, edge_type_4, L0_gnn_W1, L0_gnn_b1, L0_gnn_W2, L0_gnn_b2, L2_gnn_flux_Wh, L2_gnn_flux_bh, L2_gnn_flux_Wo, L2_gnn_flux_bo, L2_gnn_flux_ln_w, L2_gnn_flux_ln_b, L2_gnn_a_Wh, L2_gnn_a_bh, L2_gnn_a_Wo, L2_gnn_a_bo, L2_gnn_a_ln_w, L2_gnn_a_ln_b, L3_gnn_Wq, L3_gnn_bq, L3_gnn_Wk, L3_gnn_bk, L3_gnn_Wv, L3_gnn_bv, L3_gnn_Wo, L3_gnn_bo, L3_gnn_edge_bias):
    import jax
    import jax.numpy as jnp

    def _L0_gnn_ref(x, edge_index, W1, b1, W2, b2):
        import jax, jax.numpy as jnp
        import numpy as np
        N_NODES = 3125
        N_EDGES = 50000
        IN_DIM = 64
        HID_DIM = 64
        OUT_DIM = 64

        def _gin_conv(h, src, dst, W, b, num_nodes):
            agg = jax.ops.segment_sum(h[src], dst, num_segments=num_nodes)
            return jax.nn.relu((h + agg) @ W + b)
        n = x.shape[0]
        src, dst = (edge_index[0], edge_index[1])
        h = _gin_conv(x, src, dst, W1, b1, n)
        h = jax.nn.relu(h)
        out = _gin_conv(h, src, dst, W2, b2, n)
        return out

    def _L1_gnn_ref(x, edge_index):
        import jax, jax.numpy as jnp
        import numpy as np
        N_NODES = 3125
        N_EDGES = 1250000
        D_FEAT = 64

        def _aggregate(x, src, dst, num_nodes):
            return jax.ops.segment_sum(x[src], dst, num_segments=num_nodes)
        num_nodes = x.shape[0]
        src, dst = (edge_index[0], edge_index[1])
        h = _aggregate(x, src, dst, num_nodes)
        h = jax.nn.relu(h)
        h = _aggregate(h, src, dst, num_nodes)
        return h

    def _L2_gnn_ref(x, e, nvec, edge_index, flux_Wh, flux_bh, flux_Wo, flux_bo, flux_ln_w, flux_ln_b, a_Wh, a_bh, a_Wo, a_bo, a_ln_w, a_ln_b):
        import jax, jax.numpy as jnp
        import numpy as np
        N = 50000
        E = 25000
        C = 64
        SPACEDIM = 2
        LN_EPS = 1e-05

        def _mlp(x, Wh, bh, Wo, bo, ln_w, ln_b):
            for i in range(Wh.shape[0]):
                x = jax.nn.relu(x @ Wh[i] + bh[i])
            x = x @ Wo + bo
            mu = jnp.mean(x, axis=-1, keepdims=True)
            var = jnp.var(x, axis=-1, keepdims=True)
            return (x - mu) * jax.lax.rsqrt(var + LN_EPS) * ln_w + ln_b
        src = edge_index[0]
        dst = edge_index[1]
        x_send = x[src]
        x_recv = x[dst]
        n_e = x_send.shape[0]
        c = x.shape[1]
        fs = _mlp(x_send, flux_Wh, flux_bh, flux_Wo, flux_bo, flux_ln_w, flux_ln_b)
        fr = _mlp(x_recv, flux_Wh, flux_bh, flux_Wo, flux_bo, flux_ln_w, flux_ln_b)
        flux_send = jnp.einsum('ecd,ed->ec', fs.reshape(n_e, c, SPACEDIM), nvec)
        flux_recv = jnp.einsum('ecd,ed->ec', fr.reshape(n_e, c, SPACEDIM), nvec)
        a_ws = _mlp((x_send + x_recv) * 0.5, a_Wh, a_bh, a_Wo, a_bo, a_ln_w, a_ln_b)
        flux = 0.5 * (flux_send + flux_recv) - 0.5 * a_ws * (x_send - x_recv)
        agg = jax.ops.segment_sum(flux, dst, num_segments=x.shape[0])
        return x + agg

    def _L3_gnn_ref(x, edge_index, edge_type, num_nodes, Wq, bq, Wk, bk, Wv, bv, Wo, bo, edge_bias):
        import jax, jax.numpy as jnp
        import numpy as np
        DIM = 64
        NUM_HEADS = 4
        HEAD_DIM = DIM // NUM_HEADS
        SCALE = HEAD_DIM ** (-0.5)
        NUM_EDGE_TYPES = 4
        N = 3125
        E = 1250000
        Q = (x @ Wq.T + bq).reshape(-1, NUM_HEADS, HEAD_DIM)
        K = (x @ Wk.T + bk).reshape(-1, NUM_HEADS, HEAD_DIM)
        V = (x @ Wv.T + bv).reshape(-1, NUM_HEADS, HEAD_DIM)
        src, tgt = (edge_index[0], edge_index[1])
        scores = jnp.sum(Q[tgt] * K[src], axis=-1) * SCALE + edge_bias[edge_type]
        seg_max = jax.ops.segment_max(scores, tgt, num_segments=num_nodes)
        seg_max = jnp.maximum(seg_max, -1000000000.0)
        exp_scores = jnp.exp(scores - seg_max[tgt])
        seg_sum = jax.ops.segment_sum(exp_scores, tgt, num_segments=num_nodes)
        attn = exp_scores / (seg_sum[tgt] + 1e-12)
        weighted = V[src] * attn[..., None]
        out = jax.ops.segment_sum(weighted, tgt, num_segments=num_nodes)
        out = out.reshape(num_nodes, DIM)
        return out @ Wo.T + bo
    edge_index = jnp.stack([src, dst])
    x = _layernorm(x + _L0_gnn_ref(x, edge_index, L0_gnn_W1, L0_gnn_b1, L0_gnn_W2, L0_gnn_b2), axis=-1)
    x = _layernorm(x + _L1_gnn_ref(x, edge_index), axis=-1)
    x = _layernorm(x + _L2_gnn_ref(x, edge_attr_64, edge_attr_2, edge_index, L2_gnn_flux_Wh, L2_gnn_flux_bh, L2_gnn_flux_Wo, L2_gnn_flux_bo, L2_gnn_flux_ln_w, L2_gnn_flux_ln_b, L2_gnn_a_Wh, L2_gnn_a_bh, L2_gnn_a_Wo, L2_gnn_a_bo, L2_gnn_a_ln_w, L2_gnn_a_ln_b), axis=-1)
    x = _layernorm(x + _L3_gnn_ref(x, edge_index, edge_type_4, 3125, L3_gnn_Wq, L3_gnn_bq, L3_gnn_Wk, L3_gnn_bk, L3_gnn_Wv, L3_gnn_bv, L3_gnn_Wo, L3_gnn_bo, L3_gnn_edge_bias), axis=-1)
    return x

_drawn_inputs = setup_inputs


def setup_inputs(seed=0):
    import zlib

    import numpy as np

    out = dict(_drawn_inputs(seed))
    spreads = {'L2_gnn_flux_ln_w': (1.0, 0.2),
     'L2_gnn_flux_ln_b': (0.0, 0.1),
     'L2_gnn_a_ln_w': (1.0, 0.6),
     'L2_gnn_a_ln_b': (0.0, 2.0)}
    factors = {'L0_gnn_b1': 8.0,
     'L0_gnn_b2': 200.0,
     'L2_gnn_a_bh': 5.017,
     'L2_gnn_a_bo': 5.624,
     'L3_gnn_bq': 5.543,
     'L3_gnn_bk': 200.0}
    for name, (base, spread) in spreads.items():
        noise = np.random.default_rng([zlib.crc32(name.encode()), seed]).standard_normal(out[name].shape)
        drawn = base * np.exp(spread * noise) if base else spread * noise
        out[name] = jnp.asarray(drawn.astype(out[name].dtype))
    for name, factor in factors.items():
        out[name] = (out[name] * factor).astype(out[name].dtype)
    return out
```

```python
import concourse.bass as bass
from concourse import mybir

F32 = mybir.dt.float32
BF16 = mybir.dt.bfloat16
I32 = mybir.dt.int32
ALU = mybir.AluOpType
ACT = mybir.ActivationFunctionType
X = mybir.AxisListType.X

N = 3125
E = 100000
D = 64
H = 4
HD = D // H
P = 128
NP, NB = 125, 25
G = 8
NG = -(-E // (P * G))
T = NG * G
TK = -(-T // P)
TL = T - (TK - 1) * P
ROWS = T * P
NEG = -3.0e38
EPS = 1e-5
PA = 28
assert ROWS % (P * PA) == 0
WQ = 2 * D
W2 = D + 2
W3 = D + 2 * H


def build(nc, x, src, dst, edge_attr_2, edge_type_4, W1, b1, W2_, b2, fWh, fbh, fWo, fbo, flw, flb,
          aWh, abh, aWo, abo, alw, alb, Wq, bq, Wk, bk, Wv, bv, Wo, bo, edge_bias, out):
    sems = {}

    def sem(name):
        if name not in sems:
            sems[name] = nc.alloc_semaphore(name)
        return sems[name]

    def sb(name, shape, dt=F32):
        return nc.alloc_sbuf_tensor(name, shape, dt)

    class Count:

        def __init__(self, name):
            self.sem, self.n = sem(name), 0

        def by(self, ins, k=1):
            self.n += k
            return ins.then_inc(self.sem, k)

        def all(self, eng):
            eng.wait_ge(self.sem, self.n)

    vec_done, act_done, pool_done = Count("vec_done"), Count("act_done"), Count("pool_done")
    sp_io, pool_io = Count("sp_io"), Count("pool_io")

    def dve(eng, ins):
        vec_done.by(ins)
        vec_done.all(eng)

    def bc(ap, shape):
        return ap.to_broadcast(shape)

    bank = [nc.alloc_psum_tensor(f"bank{i}", [P, 512], F32) for i in range(8)]
    ident = sb("ident", [P, P])
    src_i = sb("src_i", [P, T], I32)
    dst_f = sb("dst_f", [P, T])
    nvec = sb("nvec", [P, T, 2])
    ebias = sb("ebias", [P, T, H])
    xs = sb("xs", [NP, NB, D])
    agg = sb("agg", [NP, NB, D])
    hid = sb("hid", [NP, NB, D])
    idx_last = sb("idx_last", [NP, NB], I32)
    idx_first = sb("idx_first", [NP, NB], I32)
    idx_put = sb("idx_put", [NP, NB], I32)
    idx_head = sb("idx_head", [P, TK], I32)
    midnode = sb("midnode", [P, TK])
    midlast = sb("midlast", [P, TK])
    midsel = sb("midsel", [P, TK, NB, NP], BF16)
    midrow = sb("midrow", [H, T])
    area = sb("area", [P, 4 * G * P + 2 * G * WQ + 4 * G * W3])
    featT = area[0:D + 1, 0:NB * NP]
    hidT = area[0:D + 1, NB * NP:2 * NB * NP]
    scratch = sb("scratch", [P, 8192])

    def carve(o, shape, dt=F32, parts=P):
        n = 1
        for s in shape:
            n *= s
        half = dt is BF16
        v = scratch[0:parts, o:o + (-(-n // 2) if half else n)]
        if dt is not F32:
            v = v.bitcast(dt)[:, 0:n]
        if len(shape) == 2:
            v = v.rearrange("p (a b) -> p a b", a=shape[0])
        if len(shape) == 3:
            v = v.rearrange("p (a b c) -> p a b c", a=shape[0], b=shape[1])
        return v

    def dram(name, shape, dt=F32):
        return nc.dram_tensor(name, shape, dt).ap()

    dst_pad = dram("dst_pad", [T, P], I32)
    ends = dram("ends", [N + 1, 1])
    lastrow = dram("lastrow", [1, T])
    headrow = dram("headrow", [1, T])
    midrow_d = dram("midrow_d", [1, T])
    midlast_d = dram("midlast_d", [1, T])
    table = dram("table", [N, D])
    table2 = dram("table2", [N, 4 * D])
    table2d = dram("table2d", [N, 2 * D])
    put = dram("put", [ROWS, WQ])
    sums = {w: dram(f"sums{w}", [ROWS + 1, w]) for w in (D, W2, W3)}
    nodes = lambda ap: ap.rearrange("(p b) d -> p b d", b=NB)

    def tile_rows(ap):
        return ap[0:ROWS, :].rearrange("(g p j) w -> g p j w", p=P, j=G)[:, 0, :, :]

    raw = {"dst": carve(0, (TK, P), I32), "src": carve(896, (TK, P), I32), "typ": carve(1792, (TK, P), I32)}
    rawf = {"dst": carve(2688, (TK, P)), "src": carve(3584, (TK, P)), "typ": carve(4480, (TK, P))}
    raw_nv = carve(5376, (TK, 2 * P))
    typ_f = carve(7168, (T,))
    eb_b = sb("eb_b", [P, 4 * H])

    full = E // P
    fk, fr = full // P, full % P
    rest = E - full * P

    with nc.Block() as block:
        @block.gpsimd
        def _(pool):
            pool_done.by(pool.memset(ident[:, :], 0.0))
            pool_done.all(pool)
            pool.affine_select(out=ident[:, :], in_=ident[:, :], compare_op=ALU.not_equal, fill=1.0,
                               base=0, pattern=[[-1, P]], channel_multiplier=1)

        @block.vector
        def _(v):
            v.memset(raw["dst"][:, TK - 1, :], N)
            v.memset(raw["src"][:, TK - 1, :], 0)
            v.memset(raw["typ"][:, TK - 1, :], 0)
            v.memset(raw_nv[:, TK - 1, :], 0.0)

    with nc.Block() as block:
        @block.sync
        def _(sp):
            for name, a, w in (("dst", dst, 1), ("src", src, 1), ("typ", edge_type_4, 1), ("nv", edge_attr_2, 2)):
                to = raw_nv if name == "nv" else raw[name]
                flat = a.rearrange("e d -> (e d)") if w == 2 else a
                c = P * w
                sp_io.by(sp.dma_start(to[:, 0:fk, :], flat[0:fk * P * c].rearrange("(k r c) -> r k c", r=P, c=c)), 16)
                sp_io.by(sp.dma_start(to[0:fr, fk, :], flat[fk * P * c:full * c].rearrange("(r c) -> r c", c=c)), 16)
                sp_io.by(sp.dma_start(to[fr:fr + 1, fk, 0:rest * w], flat[full * c:E * w].rearrange("(r c) -> r c", r=1)), 16)
            sp_io.by(sp.dma_start(xs[:, :, :], nodes(x)), 16)
            sp_io.by(sp.dma_start(eb_b[:, :], edge_bias.rearrange("k h -> (k h)").partition_broadcast(P)), 16)
            sp_io.all(sp)

    with nc.Block() as block:
        @block.vector
        def _(v):
            for name in raw:
                v.tensor_copy(rawf[name], raw[name])

        @block.sync
        def _(sp):
            sp_io.by(sp.dma_start(dst_pad[0:(TK - 1) * P, :].rearrange("(k r) c -> r k c", r=P), raw["dst"][:, 0:TK - 1, :]), 16)
            sp_io.by(sp.dma_start(dst_pad[(TK - 1) * P:T, :], raw["dst"][0:TL, TK - 1, :]), 16)
            sp_io.all(sp)

    def turn(sources, place):
        with nc.Block() as block:
            @block.tensor
            def _(pe):
                for i, s in enumerate(sources):
                    pe.transpose(bank[i // 4][:, (i % 4) * P:(i % 4 + 1) * P], s, ident[:, :])

        with nc.Block() as block:
            @block.vector
            def _(v):
                for i in range(len(sources)):
                    to = place(i)
                    w = to.shape[1]
                    v.tensor_copy(to, bank[i // 4][:, (i % 4) * P:(i % 4) * P + w])

    def cols(t):
        return lambda k: t[:, k * P:min((k + 1) * P, T)]

    turn([rawf["dst"][:, k, :] for k in range(TK)], cols(dst_f))
    turn([rawf["src"][:, k, :] for k in range(TK)], cols(src_i))
    turn([rawf["typ"][:, k, :] for k in range(TK)], cols(typ_f))
    for d in range(2):
        turn([raw_nv[:, k, :].rearrange("r (c d) -> r d c", d=2)[:, d, :] for k in range(TK)],
             lambda k: nvec[:, k * P:min((k + 1) * P, T), d])

    with nc.Block() as block:
        @block.sync
        def _(sp):
            sp_io.by(sp.dma_start(lastrow, dst_f[P - 1:P, :]), 16)
            sp_io.by(sp.dma_start(headrow, dst_f[0:1, :]), 16)
            sp_io.all(sp)

        @block.vector
        def _(v):
            mask = carve(0, (T,))
            dve(v, v.memset(ebias[:, :, :], 0.0))
            for k in range(4):
                dve(v, v.tensor_scalar(mask, typ_f, float(k), None, ALU.is_equal))
                for h in range(H):
                    c = k * H + h
                    ins = v.scalar_tensor_tensor(out=ebias[:, :, h], in0=mask, scalar=eb_b[:, c:c + 1],
                                                 in1=ebias[:, :, h], op0=ALU.mult, op1=ALU.add)
                dve(v, ins)

    nodeval = carve(0, (NB,), parts=NP)
    lastb = carve(32, (T,), parts=NP)
    lastH, headH = carve(832, (T,), parts=H), carve(1632, (T,), parts=H)
    five = 5
    cmp5 = carve(2432, (five, T), parts=NP)
    full_tiles = carve(6400, (NB,), parts=NP)
    q_i = carve(6432, (NB,), I32, NP)
    with nc.Block() as block:
        @block.sync
        def _(sp):
            sp_io.by(sp.dma_start(lastb, lastrow.rearrange("a t -> (a t)").partition_broadcast(NP)), 16)
            sp_io.by(sp.dma_start(lastH, lastrow.rearrange("a t -> (a t)").partition_broadcast(H)), 16)
            sp_io.by(sp.dma_start(headH, headrow.rearrange("a t -> (a t)").partition_broadcast(H)), 16)
            sp_io.all(sp)

        @block.gpsimd
        def _(pool):
            pool.iota(nodeval, [[1, NB]], base=0, channel_multiplier=NB, allow_small_or_imprecise_dtypes=True)

    mlH = carve(7300, (T,), parts=H)
    mid_eq = carve(6464, (T - 2,), parts=H)
    with nc.Block() as block:
        @block.vector
        def _(v):
            for q in range(NB // five):
                a = nodeval[:, q * five:(q + 1) * five]
                dve(v, v.tensor_tensor(cmp5, lastb.unsqueeze(1).to_broadcast([NP, five, T]),
                                       a.unsqueeze(2).to_broadcast([NP, five, T]), ALU.is_le))
                dve(v, v.tensor_reduce(full_tiles[:, q * five:(q + 1) * five], cmp5, X, ALU.add))
            dve(v, v.tensor_copy(q_i, full_tiles))
            dve(v, v.tensor_tensor(mid_eq, lastH[:, 0:T - 2], headH[:, 2:T], ALU.is_equal))
            dve(v, v.memset(midrow[:, :], -1.0))
            dve(v, v.tensor_scalar(midrow[:, 1:T - 1], lastH[:, 0:T - 2], 1.0, None, ALU.add))
            dve(v, v.tensor_tensor(midrow[:, 1:T - 1], midrow[:, 1:T - 1], mid_eq, ALU.mult))
            dve(v, v.tensor_scalar(midrow[:, 1:T - 1], midrow[:, 1:T - 1], -1.0, None, ALU.add))
            dve(v, v.tensor_scalar(mlH, midrow[:, :], float(N), None, ALU.is_lt))
            dve(v, v.tensor_scalar(midrow[:, :], midrow[:, :], 1.0, None, ALU.add))
            dve(v, v.tensor_tensor(midrow[:, :], midrow[:, :], mlH, ALU.mult))
            dve(v, v.tensor_scalar(midrow[:, :], midrow[:, :], -1.0, None, ALU.add))
            dve(v, v.memset(mlH, 0.0))
            dve(v, v.tensor_tensor(mlH[:, 0:T - 1], midrow[:, 0:T - 1], midrow[:, 1:T], ALU.not_equal))
            dve(v, v.tensor_scalar(mid_eq, midrow[:, 1:T - 1], 0.0, None, ALU.is_ge))
            dve(v, v.tensor_tensor(mlH[:, 1:T - 1], mlH[:, 1:T - 1], mid_eq, ALU.mult))
            dve(v, v.memset(mlH[:, 0:1], 0.0))

    rows_of = carve(2432, (NB, P), I32, NP)
    with nc.Block() as block:
        @block.gpsimd
        def _(pool):
            for b in range(NB):
                pool_io.by(pool.indirect_dma_start(rows_of[:, b, :], None, dst_pad,
                                                   bass.IndirectOffsetOnAxis(ap=q_i[:, b:b + 1], axis=0)), 16)
            pool_io.all(pool)

        @block.sync
        def _(sp):
            sp_io.by(sp.dma_start(midrow_d, midrow[0:1, :]), 16)
            sp_io.by(sp.dma_start(midlast_d, mlH[0:1, :]), 16)
            sp_io.all(sp)

    cmp_f = carve(6464, (NB,), parts=NP)
    zero1 = carve(6500, (1,), parts=1)
    end_f = carve(6510, (NB,), parts=NP)
    start_f = carve(6540, (NB,), parts=NP)
    with nc.Block() as block:
        @block.vector
        def _(v):
            dve(v, v.tensor_tensor(rows_of, rows_of, nodeval.unsqueeze(2).to_broadcast([NP, NB, P]), ALU.is_le))
            dve(v, v.tensor_reduce(cmp_f, rows_of, X, ALU.add))
            dve(v, v.scalar_tensor_tensor(out=end_f, in0=full_tiles, scalar=float(P), in1=cmp_f, op0=ALU.mult, op1=ALU.add))
            v.memset(zero1, 0.0)
            v.memset(midnode[:, :], -1.0)
            v.memset(midlast[:, :], 0.0)

    def tile_cols(row):
        return row.rearrange("a t -> (a t)")

    with nc.Block() as block:
        @block.sync
        def _(sp):
            sp_io.by(sp.dma_start(ends[1:N + 1, :].rearrange("(p b) a -> p (b a)", b=NB), end_f), 16)
            sp_io.by(sp.dma_start(ends[0:1, :], zero1), 16)
            for to, row in ((midnode, midrow_d), (midlast, midlast_d)):
                flat = tile_cols(row)
                for k in range(TK):
                    n = min(P, T - k * P)
                    sp_io.by(sp.dma_start(to[0:n, k:k + 1], flat[k * P:k * P + n].rearrange("(r a) -> r a", a=1)), 16)
            sp_io.all(sp)

    with nc.Block() as block:
        @block.sync
        def _(sp):
            sp_io.by(sp.dma_start(start_f, ends[0:N, :].rearrange("(p b) a -> p (b a)", b=NB)), 16)
            sp_io.all(sp)

        @block.gpsimd
        def _(pool):
            pool.iota(carve(0, (NB, NP)), [[1, NB], [NB, NP]], base=0, channel_multiplier=0,
                      allow_small_or_imprecise_dtypes=True)

    e_i, t_i, r_i = (carve(6600 + 32 * i, (NB,), I32, NP) for i in range(3))
    tf, has, two, row_f, tl_f = (carve(6700 + 32 * i, (NB,), parts=NP) for i in range(5))

    with nc.Block() as block:
        @block.vector
        def _(v):
            for k in range(TK):
                v.tensor_scalar(midsel[:, k, :, :], carve(0, (NB, NP)), midnode[:, k:k + 1], None, ALU.is_equal)

            def row(edge, keep_tile):
                dve(v, v.tensor_copy(e_i, edge))
                dve(v, v.tensor_scalar(t_i, e_i, 7, None, ALU.arith_shift_right))
                dve(v, v.tensor_copy(keep_tile, t_i))
                dve(v, v.tensor_scalar(r_i, t_i, 7, None, ALU.bitwise_and))
                dve(v, v.tensor_copy(row_f, r_i))
                dve(v, v.tensor_scalar(t_i, e_i, 10, None, ALU.arith_shift_right))
                dve(v, v.tensor_copy(tf, t_i))
                dve(v, v.scalar_tensor_tensor(out=row_f, in0=tf, scalar=float(P * G), in1=row_f, op0=ALU.mult, op1=ALU.add))
                dve(v, v.tensor_scalar(t_i, e_i, 127, None, ALU.bitwise_and))
                dve(v, v.tensor_copy(tf, t_i))
                dve(v, v.scalar_tensor_tensor(out=row_f, in0=tf, scalar=float(G), in1=row_f, op0=ALU.mult, op1=ALU.add))

            def choose(to, mask, other):
                dve(v, v.tensor_scalar(row_f, row_f, float(-other), None, ALU.add))
                dve(v, v.tensor_tensor(row_f, row_f, mask, ALU.mult))
                dve(v, v.tensor_scalar(to, row_f, float(other), None, ALU.add))

            dve(v, v.tensor_tensor(has, end_f, start_f, ALU.is_gt))
            dve(v, v.tensor_scalar(end_f, end_f, -1.0, None, ALU.add))
            row(end_f, tl_f)
            choose(idx_last[:, :], has, ROWS)
            row(start_f, full_tiles)
            dve(v, v.tensor_tensor(two, full_tiles, tl_f, ALU.is_lt))
            dve(v, v.tensor_tensor(two, two, has, ALU.mult))
            choose(idx_first[:, :], two, ROWS)
            row(start_f, full_tiles)
            dve(v, v.tensor_scalar(two, tf, 0.0, None, ALU.is_gt))
            dve(v, v.tensor_tensor(two, two, has, ALU.mult))
            choose(idx_put[:, :], two, 2 * ROWS)

    with nc.Block() as block:
        @block.sync
        def _(sp):
            flat = tile_cols(headrow)
            for k in range(TK):
                n = min(P, T - k * P)
                sp_io.by(sp.dma_start(carve(0, (TK,))[0:n, k:k + 1], flat[k * P:k * P + n].rearrange("(r a) -> r a", a=1)), 16)
            sp_io.all(sp)

        @block.vector
        def _(v):
            v.memset(scratch[:, 4096:8192], 0.0)

    nullrow = sb("nullrow", [1, W3])
    with nc.Block() as block:
        @block.vector
        def _(v):
            dve(v, v.tensor_scalar(idx_head[0:TL, TK - 1:TK], carve(0, (TK,))[0:TL, TK - 1:TK], float(N - 1), None, ALU.min))
            dve(v, v.tensor_scalar(idx_head[:, 0:TK - 1], carve(0, (TK,))[:, 0:TK - 1], float(N - 1), None, ALU.min))
            dve(v, v.memset(nullrow[:, 0:D + H], 0.0))
            dve(v, v.memset(nullrow[:, D + H:W3], NEG))

        @block.sync
        def _(sp):
            flat = put.rearrange("(c p a) w -> c p (a w)", p=P, a=PA)
            for k in range(flat.shape[0]):
                sp_io.by(sp.dma_start(flat[k], scratch[:, 4096:4096 + PA * WQ]), 16)
            sp_io.all(sp)

    with nc.Block() as block:
        @block.sync
        def _(sp):
            for w in sums:
                sp_io.by(sp.dma_start(sums[w][ROWS:ROWS + 1, :], nullrow[:, 0:w] if w == W3 else scratch[0:1, 4096:4096 + w]), 16)
            sp_io.all(sp)

    idx_st = [sb(f"idx_st{u}", [P, G], I32) for u in range(2)]
    at = [0]

    def take(shape, dt=F32):
        n = shape[0] * shape[1]
        v = area[:, at[0]:at[0] + n]
        at[0] += n
        return (v.bitcast(dt) if dt is not F32 else v).rearrange("p (a b) -> p a b", a=shape[0])

    dstrow = [take([G, P], I32) for u in range(2)]
    same = [take([G, P]) for u in range(2)]
    putr = [take([G, WQ]) for u in range(2)]
    vals = [take([G, W3]) for u in range(2)]
    outs = [take([G, W3]).rearrange("p a b -> p (a b)") for u in range(2)]
    gath = [sb(f"gath{u}", [P, G * 4 * D]) for u in range(2)]
    rows32 = [sb(f"rows32_{u}", [G * H, P], I32) for u in range(2)]

    dst_groups = dst_pad.rearrange("(g j) c -> g (j c)", j=G)
    dst_tiles = dst_pad.rearrange("(g j) c -> g j c", j=G)
    put_groups = put.rearrange("(g p j) w -> g p (j w)", p=P, j=G)

    def sums_groups(w):
        return sums[w][0:ROWS, :].rearrange("(g p j) w -> g p (j w)", p=P, j=G)

    def done(g):
        return g + 3

    def free(g):
        return g + 1

    def groups(eng, early, late=None):
        late = late or (lambda g, u, i: None)
        early(0, 0, 0)
        early(1, 1, 0)
        late(0, 0, 0)
        early(2, 0, 1)
        late(1, 1, 0)
        with eng.Fori(1, NG // 2 - 1) as i:
            early(i * 2 + 1, 1, i)
            late(i * 2, 0, i)
            early(i * 2 + 2, 0, i + 1)
            late(i * 2 + 1, 1, i)
        early(NG - 1, 1, NG // 2 - 1)
        late(NG - 2, 0, NG // 2 - 1)
        late(NG - 1, 1, NG // 2 - 1)

    def wait_prior(eng, s, n):
        if not (isinstance(n, int) and n <= 0):
            eng.wait_ge(s, n)

    class Pass:

        def __init__(self, tag, tab, width, w):
            self.tag, self.tab, self.w = tag, tab, w
            self.idx_ready = self.sem("idx_ready")
            self.gathered = [self.sem(f"gathered{u}") for u in range(2)]
            self.gath_used = self.sem("gath_used")
            self.begun = self.sem("begun")
            self.rows_in = [self.sem(f"rows_in{u}") for u in range(2)]
            self.put_in = [self.sem(f"put_in{u}") for u in range(2)]
            self.same_ready = self.sem("same_ready")
            self.summed = self.sem("summed")
            self.out_ready = self.sem("out_ready")
            self.stored = [self.sem(f"stored{u}") for u in range(2)]
            self.rows = [gath[u][:, 0:G * width].rearrange("p (g w) -> p g w", w=width) for u in range(2)]
            self.out = [outs[u][:, 0:G * w] for u in range(2)]

        def sem(self, name):
            return sem(f"{self.tag}_{name}")

        def gather(self, pool):
            def early(g, u, i):
                pool.wait_ge(self.idx_ready, g + 1)
                pool.wait_ge(self.gath_used, free(g))
                pool.sem_inc(self.begun, 1)
                for j in range(G):
                    pool.indirect_dma_start(self.rows[u][:, j, :], None, self.tab,
                                            bass.IndirectOffsetOnAxis(ap=idx_st[u][:, j:j + 1], axis=0)
                                            ).then_inc(self.gathered[u], 16)
            groups(pool, early)

        def load_rows(self, sp, g, u):
            sp.wait_ge(self.same_ready, free(g))
            sp.dma_start(dstrow[u][:, :, :].rearrange("p g c -> p (g c)"),
                         dst_groups[bass.ds(g, 1), :].to_broadcast([P, G * P])).then_inc(self.rows_in[u], 16)

        def load_put(self, sp, g, u, expanded):
            sp.wait_ge(expanded, free(g))
            sp.dma_start(putr[u][:, :, :].rearrange("p g w -> p (g w)"),
                         put_groups[bass.ds(g, 1), :, :].rearrange("a p w -> (a p) w")).then_inc(self.put_in[u], 16)

        def store(self, sp, g, u):
            sp.wait_ge(self.out_ready, g + 1)
            sp.dma_start(sums_groups(self.w)[bass.ds(g, 1), :, :].rearrange("a p w -> (a p) w"), self.out[u]
                         ).then_inc(self.stored[u], 16)

        def all_stored(self, sp):
            for u in range(2):
                sp.wait_ge(self.stored[u], 16 * (NG // 2))

        def stage_idx(self, v, g, u, i):
            wait_prior(v, self.gathered[u], i * (16 * G))
            v.tensor_scalar(idx_st[u][:, :], src_i[:, bass.ds(g * G, G)], 0.0, None, ALU.add).then_inc(self.idx_ready, 1)

        def compare(self, v, g, u, i):
            v.wait_ge(self.rows_in[u], i * 16 + 16)
            v.wait_ge(self.summed, free(g))
            v.tensor_tensor(same[u][:, :, :], dstrow[u][:, :, :],
                            dst_f[:, bass.ds(g * G, G)].unsqueeze(2).to_broadcast([P, G, P]),
                            ALU.is_equal).then_inc(self.same_ready, 1)

    def plain_pass(tag, tab):
        s = Pass(tag, tab, D, D)
        evicted = s.sem("evicted")
        with nc.Block() as block:
            @block.gpsimd
            def _(pool):
                s.gather(pool)

            @block.sync
            def _(sp):
                groups(sp, lambda g, u, i: s.load_rows(sp, g, u), lambda g, u, i: s.store(sp, g, u))
                s.all_stored(sp)

            @block.vector
            def _(v):
                v.sem_inc(s.same_ready, 2)
                v.sem_inc(s.gath_used, 2)

                def early(g, u, i):
                    s.stage_idx(v, g, u, i)
                    s.compare(v, g, u, i)

                def late(g, u, i):
                    v.wait_ge(s.summed, done(g))
                    v.sem_inc(s.gath_used, 1)
                groups(v, early, late)

            @block.tensor
            def _(pe):
                pe.sem_inc(s.summed, 2)

                def early(g, u, i):
                    pe.wait_ge(s.same_ready, done(g))
                    pe.wait_ge(s.gathered[u], i * (16 * G) + 16 * G)
                    pe.wait_ge(evicted, free(g))
                    for j in range(G):
                        mm = pe.matmul(bank[u][:, j * D:(j + 1) * D], same[u][:, j, :], s.rows[u][:, j, :],
                                       start=True, stop=True)
                    mm.then_inc(s.summed, 1)
                groups(pe, early)

            @block.scalar
            def _(act):
                act.sem_inc(evicted, 2)

                def early(g, u, i):
                    act.wait_ge(s.summed, done(g))
                    wait_prior(act, s.stored[u], i * 16)
                    act.copy(s.out[u], bank[u][:, :]).then_inc(s.out_ready, 1)
                    act.wait_ge(s.out_ready, g + 1)
                    act.sem_inc(evicted, 1)
                groups(act, early)

    r_last, r_first = (area[0:NP, i * NB * W3:(i + 1) * NB * W3].rearrange("p (b w) -> p b w", w=W3) for i in range(2))

    def pick(w):
        tmid = carve(0, (TK, w))
        with nc.Block() as block:
            @block.gpsimd
            def _(pool):
                for b in range(NB):
                    for to, idx in ((r_last, idx_last), (r_first, idx_first)):
                        pool_io.by(pool.indirect_dma_start(to[:, b, 0:w], None, sums[w],
                                                           bass.IndirectOffsetOnAxis(ap=idx[:, b:b + 1], axis=0)), 16)
                pool_io.all(pool)

            @block.vector
            def _(v):
                vec_done.by(v.memset(scratch[:, 0:TK * w], 0.0))

            @block.sync
            def _(sp):
                vec_done.all(sp)
                heads = tile_rows(sums[w])
                for k in range(TK):
                    n = min(P, T - k * P) // G
                    sp_io.by(sp.dma_start(tmid[0:n * G, k, :],
                                          heads[k * P // G:k * P // G + n, :, :].rearrange("g j w -> (g j) w")
                                          if False else heads[k * P // G:k * P // G + n, :, :]), 16)
                sp_io.all(sp)
        return tmid

    def per_bank(w):
        return 512 // w

    def mids(tm, w):
        parts = [carve(4096 + i * 512, (TK, w), BF16) for i in range(3)]
        left = carve(2048, (TK, w))
        with nc.Block() as block:
            @block.vector
            def _(v):
                dve(v, v.tensor_copy(parts[0], tm))
                dve(v, v.tensor_tensor(left, tm, parts[0], ALU.subtract))
                dve(v, v.tensor_copy(parts[1], left))
                dve(v, v.tensor_tensor(left, left, parts[1], ALU.subtract))
                dve(v, v.tensor_copy(parts[2], left))

        with nc.Block() as block:
            @block.tensor
            def _(pe):
                n = per_bank(w)
                for b in range(NB):
                    to = bank[b // n][0:NP, (b % n) * w:(b % n + 1) * w]
                    for k in range(TK):
                        for i, part in enumerate(parts):
                            pe.matmul(to, midsel[:, k, b, :], part[:, k, :],
                                      start=(k == 0 and i == 0), stop=(k == TK - 1 and i == 2))

    def by_bank(w):
        n = per_bank(w)
        for c in range(-(-NB // n)):
            m = min(n, NB - c * n)
            yield bank[c][0:NP, 0:m * w].rearrange("p (b w) -> p b w", w=w), c * n, m

    def collect(w):
        tmid = pick(w)
        mids(tmid, w)
        with nc.Block() as block:
            @block.vector
            def _(v):
                dve(v, v.tensor_tensor(r_last[:, :, 0:w], r_last[:, :, 0:w], r_first[:, :, 0:w], ALU.add))
                for view, b, m in by_bank(w):
                    ins = v.tensor_tensor(r_last[:, b:b + m, 0:w], r_last[:, b:b + m, 0:w], view, ALU.add)
                dve(v, ins)
                v.tensor_copy(agg[:, :, :], r_last[:, :, 0:D])

    def turn_nodes(a, to):
        with nc.Block() as block:
            @block.vector
            def _(v):
                v.memset(to[D:D + 1, :], 1.0)

            @block.tensor
            def _(pe):
                for b in range(NB):
                    pe.transpose(bank[b // 4][0:D, (b % 4) * NP:(b % 4 + 1) * NP], a[:, b, :], ident[0:NP, 0:NP])

        with nc.Block() as block:
            @block.vector
            def _(v):
                for c in range(-(-NB // 4)):
                    m = min(4, NB - 4 * c) * NP
                    v.tensor_copy(to[0:D, c * 4 * NP:c * 4 * NP + m], bank[c][0:D, 0:m])

    def project(a, rows, wt, w):
        n = per_bank(w)
        with nc.Block() as block:
            @block.tensor
            def _(pe):
                for b in range(NB):
                    pe.matmul(bank[b // n][0:NP, (b % n) * w:(b % n + 1) * w], a[0:rows, b * NP:(b + 1) * NP], wt,
                              start=True, stop=True)

    st1 = sb("st1", [P, NB])
    st2 = sb("st2", [P, NB])

    def normalize(v, z, wd, tmp):
        shape = [NP, NB, wd]
        dve(v, v.tensor_reduce(st1[0:NP, :], z, X, ALU.add))
        dve(v, v.tensor_scalar(st1[0:NP, :], st1[0:NP, :], 1.0 / wd, None, ALU.mult))
        dve(v, v.tensor_tensor(z, z, st1[0:NP, :].unsqueeze(2).to_broadcast(shape), ALU.subtract))
        dve(v, v.tensor_tensor(tmp, z, z, ALU.mult))
        dve(v, v.tensor_reduce(st2[0:NP, :], tmp, X, ALU.add))
        dve(v, v.tensor_scalar(st2[0:NP, :], st2[0:NP, :], 1.0 / wd, EPS, ALU.mult, ALU.add))

    def layernorm(z, wd, tmp):
        with nc.Block() as block:
            @block.vector
            def _(v):
                normalize(v, z, wd, tmp)

        with nc.Block() as block:
            @block.scalar
            def _(act):
                act.activation(st1[0:NP, :], st2[0:NP, :], ACT.Sqrt)

        with nc.Block() as block:
            @block.vector
            def _(v):
                dve(v, v.reciprocal(st2[0:NP, :], st1[0:NP, :]))
                dve(v, v.tensor_tensor(z, z, st2[0:NP, :].unsqueeze(2).to_broadcast([NP, NB, wd]), ALU.mult))

    tmp64 = carve(0, (NB, D), parts=NP)

    def to_table(tab, a):
        with nc.Block() as block:
            @block.sync
            def _(sp):
                sp_io.by(sp.dma_start(nodes(tab), a), 16)
                sp_io.all(sp)

    w1s, w2s = sb("w1s", [D + 1, D]), sb("w2s", [D + 1, D])
    wts = {n: sb(f"w_{n}", [D + 1, D]) for n in "qkvo"}
    wraw = {n: sb(f"wraw_{n}", [D, D]) for n in "qkvo"}
    fw = [sb(f"fw{i}", [D, D]) for i in range(3)]
    fb = sb("fb", [D, 3])
    fwo = sb("fwo", [D + 1, 2 * D])
    flwb = sb("flwb", [NP, 2 * D])
    flbb = sb("flbb", [NP, 2 * D])
    aw0 = sb("aw0", [D, D])
    abd = [sb(f"abd{i}", [P, P]) for i in range(3)]
    ab = sb("ab", [P, 3])
    abo2 = sb("abo2", [1, P])
    ones1 = sb("ones1", [1, P])
    alwb = sb("alwb", [P, D])
    albb = sb("albb", [P, D])
    abo1 = sb("abo1", [1, D])
    tst = sb("tst", [P, 4])

    with nc.Block() as block:
        @block.vector
        def _(v):
            for a in abd:
                vec_done.by(v.memset(a[:, :], 0.0))

        @block.sync
        def _(sp):
            def load(to, a):
                sp_io.by(sp.dma_start(to, a), 16)

            def row(a):
                return a.rearrange("(a n) -> a n", a=1)

            def col(a):
                return a.rearrange("(n a) -> n a", a=1)

            for to, w, b in ((w1s, W1, b1), (w2s, W2_, b2), (fwo, fWo, fbo)):
                load(to[0:D, :], w)
                load(to[D:D + 1, :], row(b))
            for n, w, b in (("q", Wq, bq), ("k", Wk, bk), ("v", Wv, bv), ("o", Wo, bo)):
                load(wraw[n][:, :], w)
                load(wts[n][D:D + 1, :], row(b))
            for i in range(3):
                load(fw[i][:, :], fWh[i])
                load(fb[:, i:i + 1], col(fbh[i]))
                for c in range(2):
                    load(ab[c * D:(c + 1) * D, i:i + 1], col(abh[i]))
            load(flwb[:, :], flw.partition_broadcast(NP))
            load(flbb[:, :], flb.partition_broadcast(NP))
            load(alwb[:, :], alw.partition_broadcast(P))
            load(albb[:, :], alb.partition_broadcast(P))
            load(aw0[:, :], aWh[0])
            load(abo1[:, :], row(abo))
            vec_done.all(sp)
            for i, w in ((0, aWh[1]), (1, aWh[2]), (2, aWo)):
                for c in range(2):
                    load(abd[i][c * D:(c + 1) * D, c * D:(c + 1) * D], w)
            sp_io.all(sp)

    with nc.Block() as block:
        @block.vector
        def _(v):
            dve(v, v.tensor_scalar(aw0[:, :], aw0[:, :], 0.5, None, ALU.mult))
            for c in range(2):
                a = abd[2][c * D:(c + 1) * D, c * D:(c + 1) * D]
                t = tst[c * D:(c + 1) * D, 0:1]
                dve(v, v.tensor_reduce(t, a, X, ALU.add))
                dve(v, v.tensor_scalar(t, t, 1.0 / D, None, ALU.mult))
                dve(v, v.tensor_scalar(a, a, t, None, ALU.subtract))
            t = tst[0:1, 1:2]
            dve(v, v.tensor_reduce(t, abo1[:, :], X, ALU.add))
            dve(v, v.tensor_scalar(t, t, 1.0 / D, None, ALU.mult))
            for c in range(2):
                dve(v, v.tensor_scalar(abo2[:, c * D:(c + 1) * D], abo1[:, :], t, None, ALU.subtract))
            dve(v, v.tensor_scalar(alwb[:, :], alwb[:, :], -0.5, None, ALU.mult))
            dve(v, v.tensor_scalar(albb[:, :], albb[:, :], -0.5, None, ALU.mult))
            dve(v, v.tensor_scalar(flwb[:, :], flwb[:, :], 0.5, None, ALU.mult))
            dve(v, v.tensor_scalar(flbb[:, :], flbb[:, :], 0.5, None, ALU.mult))
            dve(v, v.memset(ones1[:, :], 1.0))

        @block.tensor
        def _(pe):
            for c, n in enumerate("qkvo"):
                pe.transpose(bank[0][0:D, c * D:(c + 1) * D], wraw[n][:, :], ident[0:D, 0:D])

    with nc.Block() as block:
        @block.vector
        def _(v):
            for c, n in enumerate("qkvo"):
                dve(v, v.tensor_copy(wts[n][0:D, :], bank[0][0:D, c * D:(c + 1) * D]))
            dve(v, v.tensor_scalar(wts["q"][:, :], wts["q"][:, :], HD ** -0.5, None, ALU.mult))

    def gin(source, h, weights):
        plain_pass(source[0], source[1])
        collect(D)
        with nc.Block() as block:
            @block.vector
            def _(v):
                v.tensor_tensor(agg[:, :, :], agg[:, :, :], h, ALU.add)
        turn_nodes(agg, featT)
        project(featT, D + 1, weights[:, :], D)
        with nc.Block() as block:
            @block.scalar
            def _(act):
                for view, b, m in by_bank(D):
                    act.activation(hid[:, b:b + m, :], view, ACT.Relu)

    def residual(a):
        with nc.Block() as block:
            @block.vector
            def _(v):
                v.tensor_tensor(xs[:, :, :], xs[:, :, :], a, ALU.add)
        layernorm(xs[:, :, :], D, tmp64)

    gin(("p0a", x), xs[:, :, :], w1s)
    to_table(table, hid[:, :, :])
    gin(("p0b", table), hid[:, :, :], w2s)
    residual(hid[:, :, :])

    to_table(table, xs[:, :, :])
    plain_pass("p1a", table)
    collect(D)
    with nc.Block() as block:
        @block.vector
        def _(v):
            v.tensor_scalar(hid[:, :, :], agg[:, :, :], 0.0, None, ALU.max)
    to_table(table, hid[:, :, :])
    plain_pass("p1b", table)
    collect(D)
    residual(agg[:, :, :])

    tab = sb("tab", [NP, NB, 2 * D])
    flux = scratch[0:NP, 0:NB * 2 * D].rearrange("p (b w) -> p b w", w=2 * D)
    fsq = scratch[0:NP, NB * 2 * D:2 * NB * 2 * D].rearrange("p (b w) -> p b w", w=2 * D)
    turn_nodes(xs, featT)
    project(featT, D, aw0[:, :], D)
    with nc.Block() as block:
        @block.vector
        def _(v):
            for view, b, m in by_bank(D):
                v.tensor_copy(tab[:, b:b + m, 0:D], view)
            v.tensor_copy(tab[:, :, D:2 * D], xs[:, :, :])
            v.memset(hidT[D:D + 1, :], 1.0)
    CH = 4 * NP
    for layer in range(3):
        ins_, to = (featT, hidT) if layer % 2 == 0 else (hidT, featT)
        with nc.Block() as block:
            @block.tensor
            def _(pe):
                for c in range(-(-NB // 4)):
                    m = min(CH, NB * NP - c * CH)
                    pe.matmul(bank[c][0:D, 0:m], fw[layer][:, :], ins_[0:D, c * CH:c * CH + m], start=True, stop=True)

        with nc.Block() as block:
            @block.scalar
            def _(act):
                for c in range(-(-NB // 4)):
                    m = min(CH, NB * NP - c * CH)
                    act.activation(to[0:D, c * CH:c * CH + m], bank[c][0:D, 0:m], ACT.Relu, bias=fb[:, layer:layer + 1])
    project(hidT, D + 1, fwo[:, :], 2 * D)
    with nc.Block() as block:
        @block.vector
        def _(v):
            for view, b, m in by_bank(2 * D):
                v.tensor_copy(flux[:, b:b + m, :], view)
    layernorm(flux, 2 * D, fsq)
    with nc.Block() as block:
        @block.vector
        def _(v):
            shape = [NP, NB, 2 * D]
            dve(v, v.tensor_tensor(flux, flux, flwb[:, :].unsqueeze(1).to_broadcast(shape), ALU.mult))
            dve(v, v.tensor_tensor(flux, flux, flbb[:, :].unsqueeze(1).to_broadcast(shape), ALU.add))
    fx = sb("fx", [NP, NB, 2 * D])

    def publish(srcs, a, headtab):
        heads = gath[0][:, 0:TK * 2 * D].rearrange("p (k w) -> p k w", w=2 * D)
        with nc.Block() as block:
            @block.sync
            def _(sp):
                for to, s_ in srcs:
                    sp_io.by(sp.dma_start(to, s_), 16)
                sp_io.all(sp)

            @block.gpsimd
            def _(pool):
                for b in range(NB):
                    pool_io.by(pool.indirect_dma_start(put, bass.IndirectOffsetOnAxis(ap=idx_put[:, b:b + 1], axis=0),
                                                       a[:, b, :], None, bounds_check=ROWS - 1, oob_is_err=False), 16)
                pool_io.all(pool)

        with nc.Block() as block:
            @block.gpsimd
            def _(pool):
                for k in range(TK):
                    n = min(P, T - k * P)
                    pool_io.by(pool.indirect_dma_start(heads[0:n, k, :], None, headtab,
                                                       bass.IndirectOffsetOnAxis(ap=idx_head[0:n, k:k + 1], axis=0)), 16)
                pool_io.all(pool)

        with nc.Block() as block:
            @block.sync
            def _(sp):
                rows = tile_rows(put)
                for k in range(TK):
                    n = min(P, T - k * P) // G
                    sp_io.by(sp.dma_start(rows[k * P // G:k * P // G + n, :, :], heads[0:n * G, k, :]), 16)
                sp_io.all(sp)

    publish([(nodes(table2)[:, :, 0:2 * D], tab[:, :, :]), (nodes(table2)[:, :, 2 * D:4 * D], flux),
             (nodes(table2d), tab[:, :, :])], tab, table2d)
    with nc.Block() as block:
        @block.vector
        def _(v):
            v.tensor_copy(fx[:, :, :], flux)

    def flux_pass():
        s = Pass("p2", table2, 4 * D, W2)
        expanded, z_ready, d_ready, f_part, f_ready = (s.sem(n) for n in ("expanded", "z_ready", "d_ready", "f_part", "f_ready"))
        turned, h1, m1, h2, m2, h3, y = (s.sem(n) for n in ("turned", "h1", "m1", "h2", "m2", "h3", "y"))
        squared, var_ready, root, u_ready, chain, v_ready = (s.sem(n) for n in ("squared", "var_ready", "root", "u_ready", "chain", "v_ready"))
        CH_ = 4
        zb = carve(0, (G, D))
        db = [carve(512 + 512 * u, (G, D)) for u in range(2)]
        ft = carve(1536, (G, D, 2))
        fl = [carve(2560 + 512 * u, (G, D)) for u in range(2)]
        h1b, h2b, h3b, sq, ub = (carve(3584 + 512 * k, (512,)) for k in range(5))
        ub = ub.rearrange("p (g d) -> p g d", g=G)
        var, sd, rstd = (carve(6200 + 8 * k, (G,)) for k in range(3))
        wd = [P, G, D]

        def ex(lo):
            return [bank[c][:, :].rearrange("p (g w) -> p g w", g=4)[:, :, lo:lo + D] for c in range(2)]

        with nc.Block() as block:
            @block.gpsimd
            def _(pool):
                s.gather(pool)

            @block.sync
            def _(sp):
                def early(g, u, i):
                    s.load_rows(sp, g, u)
                    s.load_put(sp, g, u, expanded)
                groups(sp, early, lambda g, u, i: s.store(sp, g, u))
                s.all_stored(sp)

            @block.vector
            def _(v):
                v.sem_inc(s.same_ready, 2)
                v.sem_inc(s.gath_used, 2)

                def early(g, u, i):
                    s.stage_idx(v, g, u, i)
                    s.compare(v, g, u, i)
                    r = s.rows[u]
                    v.wait_ge(s.gathered[u], i * (16 * G) + 16 * G)
                    v.wait_ge(expanded, done(g))
                    wait_prior(v, turned, g)
                    for c in range(2):
                        ins = v.tensor_tensor(zb[:, 4 * c:4 * c + 4, :], ex(0)[c], r[:, 4 * c:4 * c + 4, 0:D], ALU.add)
                    ins.then_inc(z_ready, 1)
                    v.wait_ge(v_ready, g - 1 + 2)
                    for c in range(2):
                        ins = v.tensor_tensor(db[u][:, 4 * c:4 * c + 4, :], r[:, 4 * c:4 * c + 4, D:2 * D], ex(D)[c], ALU.subtract)
                    ins.then_inc(d_ready, 1)
                    wait_prior(v, f_ready, g)
                    v.tensor_tensor(ft, r[:, :, 2 * D:4 * D].rearrange("p g (c d) -> p g c d", d=2),
                                    nvec[:, bass.ds(g * G, G), :].unsqueeze(2).to_broadcast([P, G, D, 2]),
                                    ALU.mult).then_inc(s.gath_used, 1)
                    v.wait_ge(s.gath_used, done(g))
                    v.tensor_reduce(fl[u], ft, X, ALU.add).then_inc(f_ready, 1)

                def late(g, u, i):
                    v.wait_ge(squared, g + 1)
                    v.tensor_reduce(var, sq.rearrange("p (g d) -> p g d", g=G), X, ALU.add).then_inc(chain, 1)
                    v.wait_ge(chain, g * CH_ + 1)
                    wait_prior(v, root, g)
                    v.tensor_scalar(var, var, 1.0 / D, EPS, ALU.mult, ALU.add).then_inc(var_ready, 1)
                    v.wait_ge(root, g + 1)
                    v.reciprocal(rstd, sd).then_inc(chain, 1)
                    v.wait_ge(chain, g * CH_ + 2)
                    v.tensor_tensor(ub, bank[7][:, :].rearrange("p (g d) -> p g d", g=G),
                                    rstd.unsqueeze(2).to_broadcast(wd), ALU.mult).then_inc(u_ready, 1)
                    v.wait_ge(u_ready, g + 1)
                    v.tensor_tensor(ub, ub, alwb[:, :].unsqueeze(1).to_broadcast(wd), ALU.mult).then_inc(chain, 1)
                    v.wait_ge(chain, g * CH_ + 3)
                    v.tensor_tensor(ub, ub, albb[:, :].unsqueeze(1).to_broadcast(wd), ALU.add).then_inc(chain, 1)
                    v.wait_ge(chain, g * CH_ + 4)
                    v.wait_ge(d_ready, g + 1)
                    v.tensor_tensor(ub, ub, db[u], ALU.mult).then_inc(mixed, 1)
                    v.wait_ge(mixed, g + 1)
                    v.wait_ge(f_ready, g + 1)
                    v.wait_ge(s.summed, free(g))
                    v.tensor_scalar(vals[u][:, :, D:W2], nvec[:, bass.ds(g * G, G), :], 1.0, None, ALU.mult)
                    v.tensor_tensor(vals[u][:, :, 0:D], ub, fl[u], ALU.add).then_inc(v_ready, 1)
                mixed = s.sem("mixed")
                v.sem_inc(v_ready, 2)
                groups(v, early, late)

            @block.tensor
            def _(pe):
                pe.sem_inc(s.summed, 2)
                pe.sem_inc(expanded, 2)

                def early(g, u, i):
                    pe.wait_ge(s.same_ready, done(g))
                    pe.wait_ge(s.put_in[u], i * 16 + 16)
                    wait_prior(pe, d_ready, g)
                    for j in range(G):
                        mm = pe.matmul(bank[j // 4][:, (j % 4) * P:(j % 4 + 1) * P], same[u][:, j, :], putr[u][:, j, :],
                                       start=True, stop=True)
                    mm.then_inc(expanded, 1)
                    pe.wait_ge(z_ready, g + 1)
                    wait_prior(pe, h1, g)
                    for j in range(4):
                        mm = pe.transpose(bank[2][:, j * P:(j + 1) * P],
                                          zb[:, 2 * j:2 * j + 2, :].rearrange("p a d -> p (a d)"), ident[:, :])
                    mm.then_inc(turned, 1)
                    pe.wait_ge(h1, g + 1)
                    wait_prior(pe, h2, g)
                    pe.matmul(bank[3][:, :], abd[0][:, :], h1b, start=True, stop=True).then_inc(m1, 1)
                    pe.wait_ge(h2, g + 1)
                    wait_prior(pe, h3, g)
                    pe.matmul(bank[6][:, :], abd[1][:, :], h2b, start=True, stop=True).then_inc(m2, 1)
                    pe.wait_ge(h3, g + 1)
                    wait_prior(pe, u_ready, g)
                    for j in range(4):
                        to = bank[7][:, j * P:(j + 1) * P]
                        pe.matmul(to, ones1[:, :], abo2[:, :], start=True, stop=False)
                        mm = pe.matmul(to, h3b[:, j * P:(j + 1) * P], abd[2][:, :], start=False, stop=True)
                    mm.then_inc(y, 1)

                def late(g, u, i):
                    pe.wait_ge(v_ready, g + 3)
                    wait_prior(pe, s.out_ready, g)
                    for j in range(G):
                        mm = pe.matmul(bank[4 + j // 4][:, (j % 4) * P:(j % 4) * P + W2], same[u][:, j, :],
                                       vals[u][:, j, 0:W2], start=True, stop=True)
                    mm.then_inc(s.summed, 1)
                groups(pe, early, late)

            @block.scalar
            def _(act):
                def early(g, u, i):
                    act.wait_ge(turned, g + 1)
                    wait_prior(act, m1, g)
                    act.activation(h1b, bank[2][:, :], ACT.Relu, bias=ab[:, 0:1]).then_inc(h1, 1)
                    act.wait_ge(m1, g + 1)
                    wait_prior(act, m2, g)
                    act.activation(h2b, bank[3][:, :], ACT.Relu, bias=ab[:, 1:2]).then_inc(h2, 1)
                    act.wait_ge(m2, g + 1)
                    wait_prior(act, y, g)
                    act.activation(h3b, bank[6][:, :], ACT.Relu, bias=ab[:, 2:3]).then_inc(h3, 1)

                def late(g, u, i):
                    act.wait_ge(y, g + 1)
                    wait_prior(act, var_ready, g)
                    act.activation(sq, bank[7][:, :], ACT.Square).then_inc(squared, 1)
                    act.wait_ge(var_ready, g + 1)
                    wait_prior(act, u_ready, g)
                    act.activation(sd, var, ACT.Sqrt).then_inc(root, 1)
                    act.wait_ge(s.summed, done(g))
                    wait_prior(act, s.stored[u], i * 16)
                    to = s.out[u].rearrange("p (g w) -> p g w", w=W2)
                    for c in range(2):
                        ins = act.copy(to[:, 4 * c:4 * c + 4, :],
                                       bank[4 + c][:, :].rearrange("p (g w) -> p g w", g=4)[:, :, 0:W2])
                    ins.then_inc(s.out_ready, 1)
                groups(act, early, late)

    flux_pass()
    collect(W2)
    with nc.Block() as block:
        @block.vector
        def _(v):
            nv = r_last[:, :, D:W2].unsqueeze(2).to_broadcast([NP, NB, D, 2])
            f4 = fx[:, :, :].rearrange("p b (c d) -> p b c d", d=2)
            dve(v, v.tensor_tensor(f4, f4, nv, ALU.mult))
            dve(v, v.tensor_reduce(hid[:, :, :], f4, X, ALU.add))
            dve(v, v.tensor_tensor(agg[:, :, :], agg[:, :, :], hid[:, :, :], ALU.add))
            dve(v, v.tensor_tensor(agg[:, :, :], agg[:, :, :], xs[:, :, :], ALU.add))
    residual(agg[:, :, :])

    turn_nodes(xs, featT)
    qz = fx
    for n, to in (("k", tab[:, :, 0:D]), ("v", tab[:, :, D:2 * D]), ("q", qz[:, :, 0:D])):
        project(featT, D + 1, wts[n][:, :], D)
        with nc.Block() as block:
            @block.vector
            def _(v):
                for view, b, m in by_bank(D):
                    v.tensor_copy(to[:, b:b + m, :], view)
                if n == "q":
                    v.memset(qz[:, :, D:2 * D], 0.0)
    kv = dram("kv", [N, 2 * D])
    qtab = dram("qtab", [N, 2 * D])
    publish([(nodes(kv), tab[:, :, :]), (nodes(qtab), qz[:, :, :])], qz, qtab)

    def reverse(ap_tensor, rows, n):
        a = ap_tensor
        return bass.AP(tensor=a.tensor, offset=a.offset + n - 1, ap=[list(a.ap[0]), [-1, n]])

    def attention_pass():
        s = Pass("p3", kv, 2 * D, W3)
        expanded, qk, scored, turned, fl_ready, fw_ready, mx, back, dif_ready, e_ready, v_ready, chain = (
            s.sem(n) for n in ("expanded", "qk", "scored", "turned", "fl_ready", "fw_ready", "mx", "back", "dif_ready",
                               "e_ready", "v_ready", "chain"))
        heads_in = [s.sem(f"heads_in{u}") for u in range(2)]
        GH = G * H
        prod = carve(0, (G, D))
        sc = [carve(512 + 32 * u, (GH,)) for u in range(2)]
        dif = carve(600, (GH,))
        exps = carve(640, (GH,))
        flags = carve(1024, (2 * P,), parts=GH)
        run_f = carve(1280, (P,), parts=GH)
        run_b = carve(1408, (P,), parts=GH)
        smax = carve(1536, (P,), parts=GH)

        with nc.Block() as block:
            @block.gpsimd
            def _(pool):
                s.gather(pool)

            @block.sync
            def _(sp):
                def early(g, u, i):
                    s.load_rows(sp, g, u)
                    s.load_put(sp, g, u, expanded)
                    sp.wait_ge(fl_ready, free(g))
                    for j in range(G):
                        sp.dma_start(rows32[u][j * H:(j + 1) * H, :],
                                     dst_tiles[bass.ds(g, 1), j, :].to_broadcast([H, P])
                                     ).then_inc(heads_in[u], 16)
                groups(sp, early, lambda g, u, i: s.store(sp, g, u))
                s.all_stored(sp)

            @block.vector
            def _(v):
                v.sem_inc(s.same_ready, 2)
                v.sem_inc(s.gath_used, 2)
                v.sem_inc(fl_ready, 2)
                vec_done.by(v.memset(flags, 0.0))
                vec_done.all(v)

                def early(g, u, i):
                    s.stage_idx(v, g, u, i)
                    s.compare(v, g, u, i)
                    v.wait_ge(heads_in[u], i * (16 * G) + 16 * G)
                    wait_prior(v, mx, g)
                    v.tensor_tensor(flags[:, 1:P], rows32[u][:, 1:P], rows32[u][:, 0:P - 1], ALU.not_equal).then_inc(fl_ready, 1)
                    v.wait_ge(fl_ready, done(g))
                    v.tensor_scalar(flags[:, 1:P], flags[:, 1:P], NEG, None, ALU.mult).then_inc(chain, 1)
                    r = s.rows[u]
                    v.wait_ge(s.gathered[u], i * (16 * G) + 16 * G)
                    v.wait_ge(expanded, done(g))
                    v.wait_ge(chain, g * 2 + 1)
                    v.tensor_tensor(prod, bank[0][:, :].rearrange("p (g d) -> p g d", g=G), r[:, :, 0:D], ALU.mult).then_inc(qk, 1)
                    v.wait_ge(qk, g + 1)
                    v.tensor_reduce(sc[u], prod.rearrange("p g (h d) -> p (g h) d", h=H), X, ALU.add).then_inc(chain, 1)
                    v.wait_ge(chain, g * 2 + 2)
                    v.tensor_tensor(sc[u].rearrange("p (g h) -> p g h", h=H), sc[u].rearrange("p (g h) -> p g h", h=H),
                                    ebias[:, bass.ds(g * G, G), :], ALU.add).then_inc(scored, 1)
                    v.wait_ge(turned, g + 1)
                    t = bank[2][0:GH, 0:P]
                    v.tensor_tensor_scan(run_f, flags[:, 0:P], t, NEG, ALU.add, ALU.max).then_inc(fw_ready, 1)
                    v.tensor_tensor_scan(reverse(run_b, GH, P), reverse(flags[:, 1:P + 1], GH, P), reverse(t, GH, P),
                                         NEG, ALU.add, ALU.max).then_inc(fw_ready, 1)
                    v.wait_ge(fw_ready, g * 2 + 2)
                    wait_prior(v, back, g)
                    v.tensor_tensor(smax, run_f, run_b, ALU.max).then_inc(mx, 1)

                def late(g, u, i):
                    v.wait_ge(back, g + 1)
                    wait_prior(v, e_ready, g)
                    m = bank[3][:, 0:GH]
                    v.tensor_tensor(dif, sc[u], m, ALU.subtract)
                    wait_prior(v, s.stored[u], i * 16)
                    v.tensor_copy(s.out[u].rearrange("p (g w) -> p g w", w=W3)[:, :, D + H:W3],
                                  m.rearrange("p (g h) -> p g h", h=H)).then_inc(dif_ready, 1)
                    v.wait_ge(e_ready, g + 1)
                    v.wait_ge(s.summed, free(g))
                    v.tensor_copy(vals[u][:, :, D:D + H], exps.rearrange("p (g h) -> p g h", h=H))
                    for c in range(G):
                        ins = v.tensor_tensor(vals[u][:, c, 0:D].rearrange("p (h d) -> p h d", h=H),
                                              s.rows[u][:, c, D:2 * D].rearrange("p (h d) -> p h d", h=H),
                                              exps[:, c * H:(c + 1) * H].unsqueeze(2).to_broadcast([P, H, HD]), ALU.mult)
                    ins.then_inc(v_ready, 1)
                    v.wait_ge(v_ready, g + 1)
                    v.sem_inc(s.gath_used, 1)
                groups(v, early, late)

            @block.tensor
            def _(pe):
                pe.sem_inc(s.summed, 2)
                pe.sem_inc(expanded, 2)

                def early(g, u, i):
                    pe.wait_ge(s.same_ready, done(g))
                    pe.wait_ge(s.put_in[u], i * 16 + 16)
                    wait_prior(pe, qk, g)
                    for j in range(G):
                        mm = pe.matmul(bank[0][:, j * D:(j + 1) * D], same[u][:, j, :], putr[u][:, j, 0:D],
                                       start=True, stop=True)
                    mm.then_inc(expanded, 1)
                    pe.wait_ge(scored, g + 1)
                    wait_prior(pe, fw_ready, g * 2)
                    pe.transpose(bank[2][0:GH, 0:P], sc[u], ident[:, :]).then_inc(turned, 1)
                    pe.wait_ge(mx, g + 1)
                    wait_prior(pe, dif_ready, g)
                    pe.matmul(bank[3][:, 0:GH], smax, ident[0:GH, 0:GH], start=True, stop=True).then_inc(back, 1)

                def late(g, u, i):
                    pe.wait_ge(v_ready, g + 1)
                    wait_prior(pe, s.out_ready, g)
                    for j in range(G):
                        mm = pe.matmul(bank[4 + j // 4][:, (j % 4) * P:(j % 4) * P + D + H], same[u][:, j, :],
                                       vals[u][:, j, 0:D + H], start=True, stop=True)
                    mm.then_inc(s.summed, 1)
                groups(pe, early, late)

            @block.scalar
            def _(act):
                def late(g, u, i):
                    act.wait_ge(dif_ready, g + 1)
                    wait_prior(act, v_ready, g)
                    act.activation(exps, dif, ACT.Exp).then_inc(e_ready, 1)
                    act.wait_ge(s.summed, done(g))
                    to = s.out[u].rearrange("p (g w) -> p g w", w=W3)
                    for c in range(2):
                        ins = act.copy(to[:, 4 * c:4 * c + 4, 0:D + H],
                                       bank[4 + c][:, :].rearrange("p (g w) -> p g w", g=4)[:, :, 0:D + H])
                    ins.then_inc(s.out_ready, 1)
                groups(act, lambda g, u, i: None, late)

    attention_pass()
    tmid = pick(W3)

    mT, flT, runT, runB, gT = (gath[0][0:H, k * 896:k * 896 + T] for k in range(2)), None, None, None, None
    mT, flT = gath[0][0:H, 0:T], gath[0][0:H, 896:896 + T]
    runT, runB = gath[1][0:H, 0:T], gath[1][0:H, 896:896 + T]
    with nc.Block() as block:
        @block.tensor
        def _(pe):
            for k in range(TK):
                pe.transpose(bank[k // 4][0:H, (k % 4) * P:(k % 4 + 1) * P], tmid[:, k, D + H:W3], ident[:, :])

    with nc.Block() as block:
        @block.vector
        def _(v):
            for k in range(TK):
                w = min(P, T - k * P)
                v.tensor_copy(mT[:, k * P:k * P + w], bank[k // 4][0:H, (k % 4) * P:(k % 4) * P + w])
            dve(v, v.memset(gath[0][0:H, 896:896 + T + 1], 0.0))
            dve(v, v.tensor_tensor(flT[:, 1:T], midrow[:, 1:T], midrow[:, 0:T - 1], ALU.not_equal))
            dve(v, v.tensor_scalar(flT[:, 1:T], flT[:, 1:T], NEG, None, ALU.mult))
            flR = gath[0][0:H, 897:897 + T]
            dve(v, v.tensor_tensor_scan(runT, flT, mT, NEG, ALU.add, ALU.max))
            dve(v, v.tensor_tensor_scan(reverse(runB, H, T), reverse(flR, H, T), reverse(mT, H, T), NEG, ALU.add, ALU.max))
            dve(v, v.tensor_tensor(runT, runT, runB, ALU.max))

    gcol = carve(600, (TK, H))
    mw = carve(640, (TK, H))
    ismid = carve(680, (TK,))
    tm3 = carve(1024, (TK, W3 + 1))
    with nc.Block() as block:
        @block.tensor
        def _(pe):
            for k in range(TK):
                w = min(P, T - k * P)
                pe.transpose(bank[0][0:w, k * H:(k + 1) * H], runT[:, k * P:k * P + w], ident[0:H, 0:H])

        @block.vector
        def _(v):
            v.memset(gcol, 0.0)

    with nc.Block() as block:
        @block.vector
        def _(v):
            g0 = bank[0][:, 0:TK * H].rearrange("p (k h) -> p k h", h=H)
            v.tensor_copy(gcol[:, 0:TK - 1, :], g0[:, 0:TK - 1, :])
            dve(v, v.tensor_copy(gcol[0:TL, TK - 1, :], g0[0:TL, TK - 1, :]))
            dve(v, v.tensor_tensor(mw, tmid[:, :, D + H:W3], gcol, ALU.subtract))
            dve(v, v.tensor_scalar(ismid, midnode[:, :], 0.0, None, ALU.is_ge))

    with nc.Block() as block:
        @block.scalar
        def _(act):
            act.activation(mw, mw, ACT.Exp)

    W4 = W3 + 1
    with nc.Block() as block:
        @block.vector
        def _(v):
            dve(v, v.tensor_tensor(mw, mw, ismid.unsqueeze(2).to_broadcast([P, TK, H]), ALU.mult))
            for k in range(TK):
                v.tensor_tensor(tm3[:, k, 0:D].rearrange("p (h d) -> p h d", h=H),
                                tmid[:, k, 0:D].rearrange("p (h d) -> p h d", h=H),
                                mw[:, k, :].unsqueeze(2).to_broadcast([P, H, HD]), ALU.mult)
            v.tensor_tensor(tm3[:, :, D:D + H], tmid[:, :, D:D + H], mw, ALU.mult)
            v.tensor_tensor(tm3[:, :, D + H:W3], gcol, midlast[:, :].unsqueeze(2).to_broadcast([P, TK, H]), ALU.mult)
            dve(v, v.tensor_copy(tm3[:, :, W3:W4], midlast[:, :].unsqueeze(2)))
    mids(tm3, W4)

    r_mid = gath[0][0:NP, 0:NB * W4].rearrange("p (b w) -> p b w", w=W4)
    ms = [carve(128 * k, (NB, H), parts=NP) for k in range(5)]
    with nc.Block() as block:
        @block.vector
        def _(v):
            for view, b, m in by_bank(W4):
                ins = v.tensor_copy(r_mid[:, b:b + m, :], view)
            dve(v, ins)
            none = carve(700, (NB, 1), parts=NP)
            dve(v, v.tensor_scalar(none, r_mid[:, :, W3:W4], -1.0, -NEG, ALU.add, ALU.mult))
            dve(v, v.tensor_tensor(r_mid[:, :, D + H:W3], r_mid[:, :, D + H:W3], none.to_broadcast([NP, NB, H]), ALU.add))
            top = ms[3]
            dve(v, v.tensor_tensor(top, r_last[:, :, D + H:W3], r_first[:, :, D + H:W3], ALU.max))
            dve(v, v.tensor_tensor(top, top, r_mid[:, :, D + H:W3], ALU.max))
            dve(v, v.tensor_scalar(top, top, -1.0e9, None, ALU.max))
            for k, r in enumerate((r_last, r_first, r_mid)):
                ins = v.tensor_tensor(ms[k], r[:, :, D + H:W3], top, ALU.subtract)
            dve(v, ins)

    with nc.Block() as block:
        @block.scalar
        def _(act):
            for k in range(3):
                act.activation(ms[k], ms[k], ACT.Exp)

    with nc.Block() as block:
        @block.vector
        def _(v):
            for k, r in enumerate((r_last, r_first, r_mid)):
                for b in range(NB):
                    a = r[:, b, 0:D].rearrange("p (h d) -> p h d", h=H)
                    v.tensor_tensor(a, a, ms[k][:, b, :].unsqueeze(2).to_broadcast([NP, H, HD]), ALU.mult)
                dve(v, v.tensor_tensor(r[:, :, D:D + H], r[:, :, D:D + H], ms[k], ALU.mult))
            S = D + H
            dve(v, v.tensor_tensor(r_last[:, :, 0:S], r_last[:, :, 0:S], r_first[:, :, 0:S], ALU.add))
            dve(v, v.tensor_tensor(r_last[:, :, 0:S], r_last[:, :, 0:S], r_mid[:, :, 0:S], ALU.add))
            dve(v, v.tensor_scalar(ms[4], r_last[:, :, D:S], 1e-12, None, ALU.add))
            dve(v, v.reciprocal(ms[3], ms[4]))
            for b in range(NB):
                ins = v.tensor_tensor(agg[:, b, :].rearrange("p (h d) -> p h d", h=H),
                                      r_last[:, b, 0:D].rearrange("p (h d) -> p h d", h=H),
                                      ms[3][:, b, :].unsqueeze(2).to_broadcast([NP, H, HD]), ALU.mult)
            dve(v, ins)
    turn_nodes(agg, featT)
    project(featT, D + 1, wts["o"][:, :], D)
    with nc.Block() as block:
        @block.vector
        def _(v):
            for view, b, m in by_bank(D):
                v.tensor_copy(agg[:, b:b + m, :], view)
    residual(agg[:, :, :])
    with nc.Block() as block:
        @block.sync
        def _(sp):
            sp_io.by(sp.dma_start(nodes(out), xs[:, :, :]), 16)
            sp_io.all(sp)


_INS = ["x", "src", "dst", "edge_attr_2", "edge_type_4", "L0_gnn_W1", "L0_gnn_b1", "L0_gnn_W2", "L0_gnn_b2",
        "L2_gnn_flux_Wh", "L2_gnn_flux_bh", "L2_gnn_flux_Wo", "L2_gnn_flux_bo", "L2_gnn_flux_ln_w",
        "L2_gnn_flux_ln_b", "L2_gnn_a_Wh", "L2_gnn_a_bh", "L2_gnn_a_Wo", "L2_gnn_a_bo", "L2_gnn_a_ln_w",
        "L2_gnn_a_ln_b", "L3_gnn_Wq", "L3_gnn_bq", "L3_gnn_Wk", "L3_gnn_bk", "L3_gnn_Wv", "L3_gnn_bv",
        "L3_gnn_Wo", "L3_gnn_bo", "L3_gnn_edge_bias"]


def kernel(**inputs):
    import numpy as _np
    import concourse.bacc as _bacc
    from concourse import mybir as _mybir
    from concourse.bass_utils import run_bass_kernel_spmd as _run

    nc = _bacc.Bacc("TRN2", target_bir_lowering=False, num_devices=1)
    arrays, args = {}, []
    for name in _INS:
        a = _np.ascontiguousarray(inputs[name])
        arrays[f"in_{name}"] = a
        args.append(nc.dram_tensor(f"in_{name}", a.shape, _mybir.dt.from_np(a.dtype), kind="ExternalInput").ap())
    out = nc.dram_tensor("out_0", (N, D), F32, kind="ExternalOutput").ap()
    build(nc, *args, out)
    r = _run(nc, [arrays], core_ids=[0])
    return r.results[0]["out_0"]
```

```python
import concourse.bass as bass
from concourse import mybir

F32 = mybir.dt.float32
BF16 = mybir.dt.bfloat16
I32 = mybir.dt.int32
ALU = mybir.AluOpType
ACT = mybir.ActivationFunctionType
X = mybir.AxisListType.X

N = 3125
E = 100000
D = 64
H = 4
HD = D // H
P = 128
NP, NB = 125, 25
G = 8
NG = -(-E // (P * G))
T = NG * G
TK = -(-T // P)
TL = T - (TK - 1) * P
ROWS = T * P
NEG = -3.0e38
EPS = 1e-5
PA = 28
assert ROWS % (P * PA) == 0
WG = 5 * D
W2 = 2 * D + 2
W3 = D + 2 * H


def build(nc, x, src, dst, edge_attr_2, edge_type_4, W1, b1, W2_, b2, fWh, fbh, fWo, fbo, flw, flb,
          aWh, abh, aWo, abo, alw, alb, Wq, bq, Wk, bk, Wv, bv, Wo, bo, edge_bias, out):
    sems = {}

    def sem(name):
        if name not in sems:
            sems[name] = nc.alloc_semaphore(name)
        return sems[name]

    def sb(name, shape, dt=F32):
        return nc.alloc_sbuf_tensor(name, shape, dt)

    class Count:

        def __init__(self, name):
            self.sem, self.n = sem(name), 0

        def by(self, ins, k=1):
            self.n += k
            return ins.then_inc(self.sem, k)

        def all(self, eng):
            eng.wait_ge(self.sem, self.n)

    zeroed, put_zero = sem("zeroed"), sem("put_zero")
    vec_done, act_done, pool_done = Count("vec_done"), Count("act_done"), Count("pool_done")
    sp_io, pool_io = Count("sp_io"), Count("pool_io")

    vec_step = [vec_done]

    def dve(eng, ins):
        vec_step[0].by(ins)
        vec_step[0].all(eng)

    def bc(ap, shape):
        return ap.to_broadcast(shape)

    bank = [nc.alloc_psum_tensor(f"bank{i}", [P, 512], F32) for i in range(8)]
    ident = sb("ident", [P, P])
    src_i = sb("src_i", [P, T], I32)
    dst_f = sb("dst_f", [P, T])
    nvec = sb("nvec", [P, T, 2])
    ebias = sb("ebias", [P, T, H])
    xs = sb("xs", [NP, NB, D])
    agg = sb("agg", [NP, NB, D])
    hid = sb("hid", [NP, NB, D])
    idx_last = sb("idx_last", [NP, NB], I32)
    idx_first = sb("idx_first", [NP, NB], I32)
    idx_put = sb("idx_put", [NP, NB], I32)
    idx_head = sb("idx_head", [P, TK], I32)
    midnode = sb("midnode", [P, TK])
    midlast = sb("midlast", [P, TK])
    anymid = sb("anymid", [1, 1], I32)
    colnode = sb("colnode", [P, NP])
    deg = sb("deg", [NP, NB])
    zeros = sb("zeros", [P, 256])
    midrow = sb("midrow", [H, T])
    area = sb("area", [P, 6 * G * P + 2 * G * D + 4 * G * W2])
    featT = area[0:D + 1, 0:NB * NP]
    hidT = area[0:D + 1, NB * NP:2 * NB * NP]
    scratch = sb("scratch", [P, 9600])

    def carve(o, shape, dt=F32, parts=P):
        n = 1
        for s in shape:
            n *= s
        half = dt is BF16
        v = scratch[0:parts, o:o + (-(-n // 2) if half else n)]
        if dt is not F32:
            v = v.bitcast(dt)[:, 0:n]
        if len(shape) == 2:
            v = v.rearrange("p (a b) -> p a b", a=shape[0])
        if len(shape) == 3:
            v = v.rearrange("p (a b c) -> p a b c", a=shape[0], b=shape[1])
        return v

    def dram(name, shape, dt=F32):
        return nc.dram_tensor(name, shape, dt).ap()

    dst_pad = dram("dst_pad", [T, P], I32)
    ends = dram("ends", [N + 1, 1])
    lastrow = dram("lastrow", [1, T])
    headrow = dram("headrow", [1, T])
    midrow_d = dram("midrow_d", [1, T])
    midlast_d = dram("midlast_d", [1, T])
    table = dram("table", [N, D])
    table2 = dram("table2", [N, WG])
    dst_heads = dram("dst_heads", [T * H, P], I32)
    put = dram("put", [ROWS, D])
    sums = {w: dram(f"sums{w}", [ROWS + 1, w]) for w in (D, W2, W3)}
    nodes = lambda ap: ap.rearrange("(p b) d -> p b d", b=NB)

    def tile_rows(ap):
        return ap[0:ROWS, :].rearrange("(g p j) w -> g p j w", p=P, j=G)[:, 0, :, :]

    raw = {"dst": carve(0, (TK, P), I32), "src": carve(896, (TK, P), I32), "typ": carve(1792, (TK, P), I32)}
    rawf = {"dst": carve(2688, (TK, P)), "src": carve(3584, (TK, P)), "typ": carve(4480, (TK, P))}
    raw_nv = carve(5376, (TK, 2 * P))
    typ_f = carve(7168, (T,))
    eb_b = sb("eb_b", [P, 4 * H])

    full = E // P
    fk, fr = full // P, full % P
    rest = E - full * P

    with nc.Block() as block:
        @block.gpsimd
        def _(pool):
            pool_done.by(pool.memset(ident[:, :], 0.0))
            pool_done.all(pool)
            pool.affine_select(out=ident[:, :], in_=ident[:, :], compare_op=ALU.not_equal, fill=1.0,
                               base=0, pattern=[[-1, P]], channel_multiplier=1)

        @block.scalar
        def _(act):
            act.wait_ge(zeroed, 1)
            flat = put.rearrange("(c p a) w -> c p (a w)", p=P, a=PA).rearrange("c p (m z) -> c p m z", z=256)
            for k in range(flat.shape[0]):
                act.dma_start(flat[k], zeros[:, :].unsqueeze(1).to_broadcast([P, PA * D // 256, 256])).then_inc(put_zero, 16)

        @block.vector
        def _(v):
            v.memset(zeros[:, :], 0.0).then_inc(zeroed, 1)
            v.memset(raw["dst"][:, TK - 1, :], N)
            v.memset(raw["src"][:, TK - 1, :], 0)
            v.memset(raw["typ"][:, TK - 1, :], 0)
            v.memset(raw_nv[:, TK - 1, :], 0.0)

    with nc.Block() as block:
        @block.sync
        def _(sp):
            for name, a, w in (("dst", dst, 1), ("src", src, 1), ("typ", edge_type_4, 1), ("nv", edge_attr_2, 2)):
                to = raw_nv if name == "nv" else raw[name]
                flat = a.rearrange("e d -> (e d)") if w == 2 else a
                c = P * w
                sp_io.by(sp.dma_start(to[:, 0:fk, :], flat[0:fk * P * c].rearrange("(k r c) -> r k c", r=P, c=c)), 16)
                sp_io.by(sp.dma_start(to[0:fr, fk, :], flat[fk * P * c:full * c].rearrange("(r c) -> r c", c=c)), 16)
                sp_io.by(sp.dma_start(to[fr:fr + 1, fk, 0:rest * w], flat[full * c:E * w].rearrange("(r c) -> r c", r=1)), 16)
            sp_io.by(sp.dma_start(xs[:, :, :], nodes(x)), 16)
            sp_io.by(sp.dma_start(eb_b[:, :], edge_bias.rearrange("k h -> (k h)").partition_broadcast(P)), 16)
            sp_io.all(sp)

    with nc.Block() as block:
        @block.vector
        def _(v):
            for name in raw:
                v.tensor_copy(rawf[name], raw[name])

        @block.sync
        def _(sp):
            sp_io.by(sp.dma_start(dst_pad[0:(TK - 1) * P, :].rearrange("(k r) c -> r k c", r=P), raw["dst"][:, 0:TK - 1, :]), 16)
            sp_io.by(sp.dma_start(dst_pad[(TK - 1) * P:T, :], raw["dst"][0:TL, TK - 1, :]), 16)
            heads = dst_heads.rearrange("(t h) c -> t h c", h=H)
            for h in range(H):
                sp_io.by(sp.dma_start(heads[0:(TK - 1) * P, h, :].rearrange("(k r) c -> r k c", r=P), raw["dst"][:, 0:TK - 1, :]), 16)
                sp_io.by(sp.dma_start(heads[(TK - 1) * P:T, h, :], raw["dst"][0:TL, TK - 1, :]), 16)
            sp_io.all(sp)

    def turn(sources, place):
        with nc.Block() as block:
            @block.tensor
            def _(pe):
                for i, s in enumerate(sources):
                    pe.transpose(bank[i // 4][:, (i % 4) * P:(i % 4 + 1) * P], s, ident[:, :])

        with nc.Block() as block:
            @block.vector
            def _(v):
                for i in range(len(sources)):
                    to = place(i)
                    w = to.shape[1]
                    v.tensor_copy(to, bank[i // 4][:, (i % 4) * P:(i % 4) * P + w])

    def cols(t):
        return lambda k: t[:, k * P:min((k + 1) * P, T)]

    turn([rawf["dst"][:, k, :] for k in range(TK)], cols(dst_f))
    turn([rawf["src"][:, k, :] for k in range(TK)], cols(src_i))
    turn([rawf["typ"][:, k, :] for k in range(TK)], cols(typ_f))
    for d in range(2):
        turn([raw_nv[:, k, :].rearrange("r (c d) -> r d c", d=2)[:, d, :] for k in range(TK)],
             lambda k: nvec[:, k * P:min((k + 1) * P, T), d])

    with nc.Block() as block:
        @block.sync
        def _(sp):
            sp_io.by(sp.dma_start(lastrow, dst_f[P - 1:P, :]), 16)
            sp_io.by(sp.dma_start(headrow, dst_f[0:1, :]), 16)
            sp_io.all(sp)

        @block.vector
        def _(v):
            mask = carve(0, (T,))
            dve(v, v.memset(ebias[:, :, :], 0.0))
            for k in range(4):
                dve(v, v.tensor_scalar(mask, typ_f, float(k), None, ALU.is_equal))
                for h in range(H):
                    c = k * H + h
                    ins = v.scalar_tensor_tensor(out=ebias[:, :, h], in0=mask, scalar=eb_b[:, c:c + 1],
                                                 in1=ebias[:, :, h], op0=ALU.mult, op1=ALU.add)
                dve(v, ins)

    nodeval = carve(0, (NB,), parts=NP)
    lastb = carve(32, (T,), parts=NP)
    lastH, headH = carve(832, (T,), parts=H), carve(1632, (T,), parts=H)
    five = 5
    cmp5 = carve(2432, (five, T), parts=NP)
    full_tiles = carve(6400, (NB,), parts=NP)
    q_i = carve(6432, (NB,), I32, NP)
    with nc.Block() as block:
        @block.sync
        def _(sp):
            sp_io.by(sp.dma_start(lastb, lastrow.rearrange("a t -> (a t)").partition_broadcast(NP)), 16)
            sp_io.by(sp.dma_start(lastH, lastrow.rearrange("a t -> (a t)").partition_broadcast(H)), 16)
            sp_io.by(sp.dma_start(headH, headrow.rearrange("a t -> (a t)").partition_broadcast(H)), 16)
            sp_io.all(sp)

        @block.gpsimd
        def _(pool):
            pool.iota(nodeval, [[1, NB]], base=0, channel_multiplier=NB, allow_small_or_imprecise_dtypes=True)

    zero1 = carve(9000, (1,), parts=1)
    mlH = carve(7300, (T,), parts=H)
    mid_eq = carve(6464, (T - 2,), parts=H)
    with nc.Block() as block:
        @block.vector
        def _(v):
            for q in range(NB // five):
                a = nodeval[:, q * five:(q + 1) * five]
                dve(v, v.tensor_tensor(cmp5, lastb.unsqueeze(1).to_broadcast([NP, five, T]),
                                       a.unsqueeze(2).to_broadcast([NP, five, T]), ALU.is_le))
                dve(v, v.tensor_reduce(full_tiles[:, q * five:(q + 1) * five], cmp5, X, ALU.add))
            dve(v, v.tensor_copy(q_i, full_tiles))
            dve(v, v.tensor_tensor(mid_eq, lastH[:, 0:T - 2], headH[:, 2:T], ALU.is_equal))
            dve(v, v.memset(midrow[:, :], -1.0))
            dve(v, v.tensor_scalar(midrow[:, 1:T - 1], lastH[:, 0:T - 2], 1.0, None, ALU.add))
            dve(v, v.tensor_tensor(midrow[:, 1:T - 1], midrow[:, 1:T - 1], mid_eq, ALU.mult))
            dve(v, v.tensor_scalar(midrow[:, 1:T - 1], midrow[:, 1:T - 1], -1.0, None, ALU.add))
            dve(v, v.tensor_scalar(mlH, midrow[:, :], float(N), None, ALU.is_lt))
            dve(v, v.tensor_scalar(midrow[:, :], midrow[:, :], 1.0, None, ALU.add))
            dve(v, v.tensor_tensor(midrow[:, :], midrow[:, :], mlH, ALU.mult))
            dve(v, v.tensor_scalar(midrow[:, :], midrow[:, :], -1.0, None, ALU.add))
            dve(v, v.memset(mlH, 0.0))
            dve(v, v.tensor_tensor(mlH[:, 0:T - 1], midrow[:, 0:T - 1], midrow[:, 1:T], ALU.not_equal))
            dve(v, v.tensor_scalar(mid_eq, midrow[:, 1:T - 1], 0.0, None, ALU.is_ge))
            dve(v, v.tensor_tensor(mlH[:, 1:T - 1], mlH[:, 1:T - 1], mid_eq, ALU.mult))
            dve(v, v.memset(mlH[:, 0:1], 0.0))
            dve(v, v.tensor_reduce(zero1, mlH[0:1, :], X, ALU.max))
            dve(v, v.tensor_copy(anymid[:, :], zero1))

    rows_of = carve(2432, (NB, P), I32, NP)
    with nc.Block() as block:
        @block.gpsimd
        def _(pool):
            for b in range(NB):
                pool_io.by(pool.indirect_dma_start(rows_of[:, b, :], None, dst_pad,
                                                   bass.IndirectOffsetOnAxis(ap=q_i[:, b:b + 1], axis=0)), 16)
            pool_io.all(pool)

        @block.sync
        def _(sp):
            sp_io.by(sp.dma_start(midrow_d, midrow[0:1, :]), 16)
            sp_io.by(sp.dma_start(midlast_d, mlH[0:1, :]), 16)
            sp_io.all(sp)

    cmp_f = carve(6464, (NB,), parts=NP)
    end_f = carve(6510, (NB,), parts=NP)
    start_f = carve(6540, (NB,), parts=NP)
    with nc.Block() as block:
        @block.vector
        def _(v):
            dve(v, v.tensor_tensor(rows_of, rows_of, nodeval.unsqueeze(2).to_broadcast([NP, NB, P]), ALU.is_le))
            dve(v, v.tensor_reduce(cmp_f, rows_of, X, ALU.add))
            dve(v, v.scalar_tensor_tensor(out=end_f, in0=full_tiles, scalar=float(P), in1=cmp_f, op0=ALU.mult, op1=ALU.add))
            v.memset(zero1, 0.0)
            v.memset(midnode[:, :], -1.0)
            v.memset(midlast[:, :], 0.0)

    def tile_cols(row):
        return row.rearrange("a t -> (a t)")

    with nc.Block() as block:
        @block.sync
        def _(sp):
            sp_io.by(sp.dma_start(ends[1:N + 1, :].rearrange("(p b) a -> p (b a)", b=NB), end_f), 16)
            sp_io.by(sp.dma_start(ends[0:1, :], zero1), 16)
            for to, row in ((midnode, midrow_d), (midlast, midlast_d)):
                flat = tile_cols(row)
                for k in range(TK):
                    n = min(P, T - k * P)
                    sp_io.by(sp.dma_start(to[0:n, k:k + 1], flat[k * P:k * P + n].rearrange("(r a) -> r a", a=1)), 16)
            sp_io.all(sp)

    with nc.Block() as block:
        @block.sync
        def _(sp):
            sp_io.by(sp.dma_start(start_f, ends[0:N, :].rearrange("(p b) a -> p (b a)", b=NB)), 16)
            sp_io.all(sp)

        @block.gpsimd
        def _(pool):
            pool.iota(colnode[:, :], [[NB, NP]], base=0, channel_multiplier=0,
                      allow_small_or_imprecise_dtypes=True)

    e_i, t_i, r_i = (carve(6600 + 32 * i, (NB,), I32, NP) for i in range(3))
    tf, has, two, row_f, tl_f = (carve(6700 + 32 * i, (NB,), parts=NP) for i in range(5))

    with nc.Block() as block:
        @block.vector
        def _(v):
            v.tensor_tensor(deg[:, :], end_f, start_f, ALU.subtract)

            def row(edge, keep_tile):
                dve(v, v.tensor_copy(e_i, edge))
                dve(v, v.tensor_scalar(t_i, e_i, 7, None, ALU.arith_shift_right))
                dve(v, v.tensor_copy(keep_tile, t_i))
                dve(v, v.tensor_scalar(r_i, t_i, 7, None, ALU.bitwise_and))
                dve(v, v.tensor_copy(row_f, r_i))
                dve(v, v.tensor_scalar(t_i, e_i, 10, None, ALU.arith_shift_right))
                dve(v, v.tensor_copy(tf, t_i))
                dve(v, v.scalar_tensor_tensor(out=row_f, in0=tf, scalar=float(P * G), in1=row_f, op0=ALU.mult, op1=ALU.add))
                dve(v, v.tensor_scalar(t_i, e_i, 127, None, ALU.bitwise_and))
                dve(v, v.tensor_copy(tf, t_i))
                dve(v, v.scalar_tensor_tensor(out=row_f, in0=tf, scalar=float(G), in1=row_f, op0=ALU.mult, op1=ALU.add))

            def choose(to, mask, other):
                dve(v, v.tensor_scalar(row_f, row_f, float(-other), None, ALU.add))
                dve(v, v.tensor_tensor(row_f, row_f, mask, ALU.mult))
                dve(v, v.tensor_scalar(to, row_f, float(other), None, ALU.add))

            dve(v, v.tensor_tensor(has, end_f, start_f, ALU.is_gt))
            dve(v, v.tensor_scalar(end_f, end_f, -1.0, None, ALU.add))
            row(end_f, tl_f)
            choose(idx_last[:, :], has, ROWS)
            row(start_f, full_tiles)
            dve(v, v.tensor_tensor(two, full_tiles, tl_f, ALU.is_lt))
            dve(v, v.tensor_tensor(two, two, has, ALU.mult))
            choose(idx_first[:, :], two, ROWS)
            row(start_f, full_tiles)
            dve(v, v.tensor_scalar(two, tf, 0.0, None, ALU.is_gt))
            dve(v, v.tensor_tensor(two, two, has, ALU.mult))
            choose(idx_put[:, :], two, 2 * ROWS)

    with nc.Block() as block:
        @block.sync
        def _(sp):
            flat = tile_cols(headrow)
            for k in range(TK):
                n = min(P, T - k * P)
                sp_io.by(sp.dma_start(carve(0, (TK,))[0:n, k:k + 1], flat[k * P:k * P + n].rearrange("(r a) -> r a", a=1)), 16)
            sp_io.all(sp)

    nullrow = sb("nullrow", [1, W3])
    with nc.Block() as block:
        @block.vector
        def _(v):
            dve(v, v.tensor_scalar(idx_head[0:TL, TK - 1:TK], carve(0, (TK,))[0:TL, TK - 1:TK], float(N - 1), None, ALU.min))
            dve(v, v.tensor_scalar(idx_head[:, 0:TK - 1], carve(0, (TK,))[:, 0:TK - 1], float(N - 1), None, ALU.min))
            dve(v, v.memset(nullrow[:, 0:D + H], 0.0))
            dve(v, v.memset(nullrow[:, D + H:W3], NEG))

    with nc.Block() as block:
        @block.sync
        def _(sp):
            for w in sums:
                sp_io.by(sp.dma_start(sums[w][ROWS:ROWS + 1, :], nullrow[:, 0:w] if w == W3 else zeros[0:1, 0:w]), 16)
            sp_io.all(sp)

    idx_st = [sb(f"idx_st{u}", [P, G], I32) for u in range(4)]
    at = [0]

    def take(shape, dt=F32):
        n = shape[0] * shape[1]
        v = area[:, at[0]:at[0] + n]
        at[0] += n
        return (v.bitcast(dt) if dt is not F32 else v).rearrange("p (a b) -> p a b", a=shape[0])

    dstrow = [take([G, P], I32) for u in range(2)]
    same = [take([G, P]) for u in range(4)]
    putr = [take([G, D]) for u in range(2)]
    vals = [take([G, W2]) for u in range(2)]
    outs = [take([G, W2]).rearrange("p a b -> p (a b)") for u in range(2)]
    gath = sb("gath", [P, 2 * G * WG])
    rows32 = [sb(f"rows32_{u}", [G * H, P], I32) for u in range(2)]

    dst_groups = dst_pad.rearrange("(g j) c -> g (j c)", j=G)
    head_groups = dst_heads.rearrange("(g j) c -> g j c", j=G * H)
    put_groups = put.rearrange("(g p j) w -> g p (j w)", p=P, j=G)

    def sums_groups(w):
        return sums[w][0:ROWS, :].rearrange("(g p j) w -> g p (j w)", p=P, j=G)

    TURN = 4

    class Group:

        def __init__(self, i, o):
            self.i, self.o = i, o
            self.n = i * TURN + o

        def slot(self, k):
            return self.o % k

        def turn(self, k):
            return self.i * (TURN // k) + self.o // k

    def done(g):
        return g.n + 1

    def prior(eng, s, n, k):
        n = n.n + 1 - k
        if not (isinstance(n, int) and n <= 0):
            eng.wait_ge(s, n)

    def prior_dma(eng, s, g, k, each=16):
        n = g.turn(k) * each
        if not (isinstance(n, int) and n <= 0):
            eng.wait_ge(s, n)

    LEAD, LAG = 2, 4

    def ticks(eng, step):
        def edge(t):
            def at(lag):
                g = t - lag
                return Group(0, g) if 0 <= g < NG else None
            step(at)
        last = (NG - LEAD) // TURN
        for t in range(-LEAD, 2 * TURN):
            edge(t)
        with eng.Fori(2, last) as i:
            for r in range(TURN):
                step(lambda lag: Group(i, r - lag))
        for t in range(last * TURN, NG + LAG):
            edge(t)

    class Pass:

        def __init__(self, tag, tab, width, w, slots):
            self.tag, self.tab, self.w, self.slots = tag, tab, w, slots
            self.idx_ready, self.begun = self.sem("idx_ready"), self.sem("begun")
            self.gathered = [self.sem(f"gathered{u}") for u in range(slots)]
            self.rows_in = [self.sem(f"rows_in{u}") for u in range(2)]
            self.put_in = [self.sem(f"put_in{u}") for u in range(2)]
            self.same_ready, self.summed = self.sem("same_ready"), self.sem("summed")
            self.out_ready = self.sem("out_ready")
            self.stored = [self.sem(f"stored{u}") for u in range(2)]
            n = 2 * G * WG // slots
            self.rows = [gath[:, u * n:u * n + G * width].rearrange("p (g w) -> p g w", w=width) for u in range(slots)]
            self.out = [outs[u][:, 0:G * w] for u in range(2)]

        def sem(self, name):
            return sem(f"{self.tag}_{name}")

        def gather(self, pool, used):
            def step(at):
                g = at(0)
                if g is None:
                    return
                pool.wait_ge(self.idx_ready, done(g))
                prior(pool, used, g, self.slots)
                pool.sem_inc(self.begun, 1)
                u = g.slot(self.slots)
                for j in range(G):
                    pool.indirect_dma_start(self.rows[u][:, j, :], None, self.tab,
                                            bass.IndirectOffsetOnAxis(ap=idx_st[g.slot(4)][:, j:j + 1], axis=0)
                                            ).then_inc(self.gathered[u], 16)
            ticks(pool, step)

        def rows_here(self, eng, g):
            eng.wait_ge(self.gathered[g.slot(self.slots)], (g.turn(self.slots) + 1) * (16 * G))

        def load_rows(self, sp, g):
            u = g.slot(2)
            prior(sp, self.same_ready, g, 2)
            sp.dma_start(dstrow[u].rearrange("p g c -> p (g c)"),
                         dst_groups[bass.ds(g.n, 1), :].to_broadcast([P, G * P])).then_inc(self.rows_in[u], 16)

        def load_put(self, sp, g, expanded):
            u = g.slot(2)
            prior(sp, expanded, g, 2)
            sp.dma_start(putr[u].rearrange("p g w -> p (g w)"),
                         put_groups[bass.ds(g.n, 1), :, :].rearrange("a p w -> (a p) w")).then_inc(self.put_in[u], 16)

        def store(self, sp, g):
            u = g.slot(2)
            sp.wait_ge(self.out_ready, done(g))
            sp.dma_start(sums_groups(self.w)[bass.ds(g.n, 1), :, :].rearrange("a p w -> (a p) w"), self.out[u]
                         ).then_inc(self.stored[u], 16)

        def all_stored(self, sp):
            for u in range(2):
                sp.wait_ge(self.stored[u], 16 * (NG // 2))

        def stage_idx(self, v, g):
            if self.slots == 4:
                prior_dma(v, self.gathered[g.slot(4)], g, 4, 16 * G)
            else:
                n = (g.turn(2) - 1) * (16 * G)
                if not (isinstance(n, int) and n <= 0):
                    v.wait_ge(self.gathered[g.slot(2)], n)
            v.tensor_scalar(idx_st[g.slot(4)][:, :], src_i[:, bass.ds(g.n * G, G)], 0.0, None, ALU.add
                            ).then_inc(self.idx_ready, 1)

        def compare(self, v, g):
            v.wait_ge(self.rows_in[g.slot(2)], g.turn(2) * 16 + 16)
            prior(v, self.summed, g, 4)
            v.tensor_tensor(same[g.slot(4)], dstrow[g.slot(2)],
                            dst_f[:, bass.ds(g.n * G, G)].unsqueeze(2).to_broadcast([P, G, P]),
                            ALU.is_equal).then_inc(self.same_ready, 1)

    def plain_pass(tag, tab):
        s = Pass(tag, tab, D, D, 4)
        with nc.Block() as block:
            @block.gpsimd
            def _(pool):
                s.gather(pool, s.summed)

            @block.sync
            def _(sp):
                def step(at):
                    if g := at(-2):
                        s.load_rows(sp, g)
                    if g := at(1):
                        s.store(sp, g)
                ticks(sp, step)
                s.all_stored(sp)

            @block.vector
            def _(v):
                def step(at):
                    if g := at(-2):
                        s.stage_idx(v, g)
                    if g := at(-1):
                        s.compare(v, g)
                ticks(v, step)

            @block.tensor
            def _(pe):
                def step(at):
                    if g := at(0):
                        pe.wait_ge(s.same_ready, done(g))
                        s.rows_here(pe, g)
                        prior(pe, s.out_ready, g, 2)
                        for j in range(G):
                            mm = pe.matmul(bank[g.slot(2)][:, j * D:(j + 1) * D], same[g.slot(4)][:, j, :],
                                           s.rows[g.slot(4)][:, j, :], start=True, stop=True)
                        mm.then_inc(s.summed, 1)
                ticks(pe, step)

            @block.scalar
            def _(act):
                def step(at):
                    if g := at(0):
                        act.wait_ge(s.summed, done(g))
                        prior_dma(act, s.stored[g.slot(2)], g, 2)
                        act.copy(s.out[g.slot(2)], bank[g.slot(2)][:, :]).then_inc(s.out_ready, 1)
                ticks(act, step)

    r_last, r_first = (area[0:NP, i * NB * W2:(i + 1) * NB * W2].rearrange("p (b w) -> p b w", w=W2) for i in range(2))

    def pick(w):
        tmid = carve(0, (TK, w))
        with nc.Block() as block:
            @block.gpsimd
            def _(pool):
                for b in range(NB):
                    for to, idx in ((r_last, idx_last), (r_first, idx_first)):
                        pool_io.by(pool.indirect_dma_start(to[:, b, 0:w], None, sums[w],
                                                           bass.IndirectOffsetOnAxis(ap=idx[:, b:b + 1], axis=0)), 16)
                pool_io.all(pool)

            @block.vector
            def _(v):
                vec_done.by(v.memset(scratch[:, 0:TK * w], 0.0))

            @block.sync
            def _(sp):
                vec_done.all(sp)
                heads = tile_rows(sums[w])
                for k in range(TK):
                    n = min(P, T - k * P) // G
                    sp_io.by(sp.dma_start(tmid[0:n * G, k, :],
                                          heads[k * P // G:k * P // G + n, :, :]), 16)
                sp_io.all(sp)
        return tmid

    def per_bank(w):
        return 512 // w

    class when_mids:

        def __init__(self, tag):
            self.steps = Count(f"{tag}_vec_step")

        def __enter__(self):
            vec_step[0] = self.steps
            flag = nc.values_load(anymid[0:1, 0:1], min_val=0, max_val=1,
                                  skip_runtime_bounds_check_because="0 or 1 by its making")
            self.cond = nc.If(flag != 0)
            self.cond.__enter__()
            for eng in (nc.sync, nc.gpsimd, nc.tensor, nc.vector, nc.scalar):
                eng.nop()

        def __exit__(self, *a):
            vec_step[0] = vec_done
            return self.cond.__exit__(*a)

    def mids(tag, tm, w):
        to = gath[0:NP, 0:NB * w].rearrange("p (b w) -> p b w", w=w)
        sel_ready, added, kept = (sem(f"{tag}_{n}") for n in ("sel_ready", "added", "kept"))
        sel = carve(2048, (TK, NP))
        mine = carve(2048 + TK * NP, (TK,))
        with nc.Block() as block:
            @block.vector
            def _(v):
                dve(v, v.tensor_copy(mine, midnode[:, :]))
                with v.Fori(0, NB) as b:
                    for k in range(TK):
                        ins = v.tensor_scalar(sel[:, k, :], colnode[:, :], mine[:, k:k + 1], None, ALU.is_equal)
                    ins.then_inc(sel_ready, 1)
                    v.wait_ge(added, b + 1)
                    v.tensor_scalar(to[:, bass.ds(b, 1), :].rearrange("p a w -> p (a w)"), bank[0][0:NP, 0:w], 1.0, None, ALU.mult)
                    v.tensor_scalar(mine, mine, -1.0, None, ALU.add).then_inc(kept, 1)
                    v.wait_ge(kept, b + 1)

            @block.tensor
            def _(pe):
                with pe.Fori(0, NB) as b:
                    pe.wait_ge(sel_ready, b + 1)
                    for k in range(TK):
                        mm = pe.matmul(bank[0][0:NP, 0:w], sel[:, k, :], tm[:, k, :], start=(k == 0), stop=(k == TK - 1))
                    mm.then_inc(added, 1)
        return to

    def by_bank(w):
        n = per_bank(w)
        for c in range(-(-NB // n)):
            m = min(n, NB - c * n)
            yield bank[c][0:NP, 0:m * w].rearrange("p (b w) -> p b w", w=w), c * n, m

    def collect(tag, w):
        tmid = pick(w)
        with when_mids(tag):
            more = mids(tag, tmid, w)
            with nc.Block() as block:
                @block.vector
                def _(v):
                    v.tensor_tensor(r_first[:, :, 0:w], r_first[:, :, 0:w], more, ALU.add)
        with nc.Block() as block:
            @block.vector
            def _(v):
                dve(v, v.tensor_tensor(r_last[:, :, 0:w], r_last[:, :, 0:w], r_first[:, :, 0:w], ALU.add))
                v.tensor_copy(agg[:, :, :], r_last[:, :, 0:D])

    def turn_nodes(a, to):
        with nc.Block() as block:
            @block.vector
            def _(v):
                v.memset(to[D:D + 1, :], 1.0)

            @block.tensor
            def _(pe):
                for b in range(NB):
                    pe.transpose(bank[b // 4][0:D, (b % 4) * NP:(b % 4 + 1) * NP], a[:, b, :], ident[0:NP, 0:NP])

        with nc.Block() as block:
            @block.vector
            def _(v):
                for c in range(-(-NB // 4)):
                    m = min(4, NB - 4 * c) * NP
                    v.tensor_copy(to[0:D, c * 4 * NP:c * 4 * NP + m], bank[c][0:D, 0:m])

    def project(a, rows, wt, w):
        n = per_bank(w)
        with nc.Block() as block:
            @block.tensor
            def _(pe):
                for b in range(NB):
                    pe.matmul(bank[b // n][0:NP, (b % n) * w:(b % n + 1) * w], a[0:rows, b * NP:(b + 1) * NP], wt,
                              start=True, stop=True)

    st1 = sb("st1", [P, NB])
    st2 = sb("st2", [P, NB])

    def normalize(v, z, wd, tmp):
        shape = [NP, NB, wd]
        dve(v, v.tensor_reduce(st1[0:NP, :], z, X, ALU.add))
        dve(v, v.tensor_scalar(st1[0:NP, :], st1[0:NP, :], 1.0 / wd, None, ALU.mult))
        dve(v, v.tensor_tensor(z, z, st1[0:NP, :].unsqueeze(2).to_broadcast(shape), ALU.subtract))
        dve(v, v.tensor_tensor(tmp, z, z, ALU.mult))
        dve(v, v.tensor_reduce(st2[0:NP, :], tmp, X, ALU.add))
        dve(v, v.tensor_scalar(st2[0:NP, :], st2[0:NP, :], 1.0 / wd, EPS, ALU.mult, ALU.add))

    def layernorm(z, wd, tmp):
        with nc.Block() as block:
            @block.vector
            def _(v):
                normalize(v, z, wd, tmp)

        with nc.Block() as block:
            @block.scalar
            def _(act):
                act.activation(st1[0:NP, :], st2[0:NP, :], ACT.Sqrt)

        with nc.Block() as block:
            @block.vector
            def _(v):
                dve(v, v.reciprocal(st2[0:NP, :], st1[0:NP, :]))
                dve(v, v.tensor_tensor(z, z, st2[0:NP, :].unsqueeze(2).to_broadcast([NP, NB, wd]), ALU.mult))

    tmp64 = carve(0, (NB, D), parts=NP)

    def to_table(tab, a):
        with nc.Block() as block:
            @block.sync
            def _(sp):
                sp_io.by(sp.dma_start(nodes(tab), a), 16)
                sp_io.all(sp)

    w1s, w2s = sb("w1s", [D + 1, D]), sb("w2s", [D + 1, D])
    wts = {n: sb(f"w_{n}", [D + 1, D]) for n in "qkvo"}
    wraw = {n: sb(f"wraw_{n}", [D, D]) for n in "qkvo"}
    fw = [sb(f"fw{i}", [D, D]) for i in range(3)]
    fb = sb("fb", [D, 3])
    fwo = sb("fwo", [D + 1, 2 * D])
    flwb = sb("flwb", [NP, 2 * D])
    flbb = sb("flbb", [NP, 2 * D])
    aw0 = sb("aw0", [D, D])
    abd = [sb(f"abd{i}", [P, P]) for i in range(3)]
    ab = sb("ab", [P, 3])
    alwb = sb("alwb", [P, D])
    albb = sb("albb", [P, D])
    abob = sb("abob", [P, D])
    tst = sb("tst", [P, 4])

    with nc.Block() as block:
        @block.vector
        def _(v):
            for a in abd:
                vec_done.by(v.memset(a[:, :], 0.0))

        @block.sync
        def _(sp):
            def load(to, a):
                sp_io.by(sp.dma_start(to, a), 16)

            def row(a):
                return a.rearrange("(a n) -> a n", a=1)

            def col(a):
                return a.rearrange("(n a) -> n a", a=1)

            for to, w, b in ((w1s, W1, b1), (w2s, W2_, b2), (fwo, fWo, fbo)):
                load(to[0:D, :], w)
                load(to[D:D + 1, :], row(b))
            for n, w, b in (("q", Wq, bq), ("k", Wk, bk), ("v", Wv, bv), ("o", Wo, bo)):
                load(wraw[n][:, :], w)
                load(wts[n][D:D + 1, :], row(b))
            for i in range(3):
                load(fw[i][:, :], fWh[i])
                load(fb[:, i:i + 1], col(fbh[i]))
                for c in range(2):
                    load(ab[c * D:(c + 1) * D, i:i + 1], col(abh[i]))
            load(flwb[:, :], flw.partition_broadcast(NP))
            load(flbb[:, :], flb.partition_broadcast(NP))
            load(alwb[:, :], alw.partition_broadcast(P))
            load(albb[:, :], alb.partition_broadcast(P))
            load(aw0[:, :], aWh[0])
            load(abob[:, :], abo.partition_broadcast(P))
            vec_done.all(sp)
            for i, w in ((0, aWh[1]), (1, aWh[2]), (2, aWo)):
                for c in range(2):
                    load(abd[i][c * D:(c + 1) * D, c * D:(c + 1) * D], w)
            sp_io.all(sp)

    with nc.Block() as block:
        @block.vector
        def _(v):
            dve(v, v.tensor_scalar(aw0[:, :], aw0[:, :], 0.5, None, ALU.mult))
            for c in range(2):
                a = abd[2][c * D:(c + 1) * D, c * D:(c + 1) * D]
                t = tst[c * D:(c + 1) * D, 0:1]
                dve(v, v.tensor_reduce(t, a, X, ALU.add))
                dve(v, v.tensor_scalar(t, t, 1.0 / D, None, ALU.mult))
                dve(v, v.tensor_scalar(a, a, t, None, ALU.subtract))
            t = tst[:, 1:2]
            dve(v, v.tensor_reduce(t, abob[:, :], X, ALU.add))
            dve(v, v.tensor_scalar(t, t, 1.0 / D, None, ALU.mult))
            dve(v, v.tensor_scalar(abob[:, :], abob[:, :], t, None, ALU.subtract))
            dve(v, v.tensor_scalar(alwb[:, :], alwb[:, :], -0.5, None, ALU.mult))
            dve(v, v.tensor_scalar(albb[:, :], albb[:, :], -0.5, None, ALU.mult))
            dve(v, v.tensor_scalar(flwb[:, :], flwb[:, :], 0.5, None, ALU.mult))
            dve(v, v.tensor_scalar(flbb[:, :], flbb[:, :], 0.5, None, ALU.mult))

        @block.tensor
        def _(pe):
            for c, n in enumerate("qkvo"):
                pe.transpose(bank[0][0:D, c * D:(c + 1) * D], wraw[n][:, :], ident[0:D, 0:D])

    with nc.Block() as block:
        @block.vector
        def _(v):
            for c, n in enumerate("qkvo"):
                dve(v, v.tensor_copy(wts[n][0:D, :], bank[0][0:D, c * D:(c + 1) * D]))
            dve(v, v.tensor_scalar(wts["q"][:, :], wts["q"][:, :], HD ** -0.5, None, ALU.mult))

    def gin(source, h, weights):
        plain_pass(source[0], source[1])
        collect(source[0], D)
        with nc.Block() as block:
            @block.vector
            def _(v):
                v.tensor_tensor(agg[:, :, :], agg[:, :, :], h, ALU.add)
        turn_nodes(agg, featT)
        project(featT, D + 1, weights[:, :], D)
        with nc.Block() as block:
            @block.scalar
            def _(act):
                for view, b, m in by_bank(D):
                    act.activation(hid[:, b:b + m, :], view, ACT.Relu)

    def residual(a):
        with nc.Block() as block:
            @block.vector
            def _(v):
                v.tensor_tensor(xs[:, :, :], xs[:, :, :], a, ALU.add)
        layernorm(xs[:, :, :], D, tmp64)

    gin(("p0a", x), xs[:, :, :], w1s)
    to_table(table, hid[:, :, :])
    gin(("p0b", table), hid[:, :, :], w2s)
    residual(hid[:, :, :])

    to_table(table, xs[:, :, :])
    plain_pass("p1a", table)
    collect("p1a", D)
    with nc.Block() as block:
        @block.vector
        def _(v):
            v.tensor_scalar(hid[:, :, :], agg[:, :, :], 0.0, None, ALU.max)
    to_table(table, hid[:, :, :])
    plain_pass("p1b", table)
    collect("p1b", D)
    residual(agg[:, :, :])

    tab = sb("tab", [NP, NB, 2 * D])
    flux = scratch[0:NP, 0:NB * 2 * D].rearrange("p (b w) -> p b w", w=2 * D)
    fsq = scratch[0:NP, NB * 2 * D:2 * NB * 2 * D].rearrange("p (b w) -> p b w", w=2 * D)
    turn_nodes(xs, featT)
    project(featT, D, aw0[:, :], D)
    with nc.Block() as block:
        @block.vector
        def _(v):
            for view, b, m in by_bank(D):
                v.tensor_copy(hid[:, b:b + m, :], view)
            v.tensor_tensor(tab[:, :, 0:D], xs[:, :, :], alwb[0:NP, :].unsqueeze(1).to_broadcast([NP, NB, D]), ALU.mult)
            v.tensor_tensor(tab[:, :, D:2 * D], xs[:, :, :], albb[0:NP, :].unsqueeze(1).to_broadcast([NP, NB, D]), ALU.mult)
            v.memset(hidT[D:D + 1, :], 1.0)
    CH = 4 * NP
    for layer in range(3):
        ins_, to = (featT, hidT) if layer % 2 == 0 else (hidT, featT)
        with nc.Block() as block:
            @block.tensor
            def _(pe):
                for c in range(-(-NB // 4)):
                    m = min(CH, NB * NP - c * CH)
                    pe.matmul(bank[c][0:D, 0:m], fw[layer][:, :], ins_[0:D, c * CH:c * CH + m], start=True, stop=True)

        with nc.Block() as block:
            @block.scalar
            def _(act):
                for c in range(-(-NB // 4)):
                    m = min(CH, NB * NP - c * CH)
                    act.activation(to[0:D, c * CH:c * CH + m], bank[c][0:D, 0:m], ACT.Relu, bias=fb[:, layer:layer + 1])
    project(hidT, D + 1, fwo[:, :], 2 * D)
    with nc.Block() as block:
        @block.vector
        def _(v):
            for view, b, m in by_bank(2 * D):
                v.tensor_copy(flux[:, b:b + m, :], view)
    layernorm(flux, 2 * D, fsq)
    with nc.Block() as block:
        @block.vector
        def _(v):
            shape = [NP, NB, 2 * D]
            dve(v, v.tensor_tensor(flux, flux, flwb[:, :].unsqueeze(1).to_broadcast(shape), ALU.mult))
            dve(v, v.tensor_tensor(flux, flux, flbb[:, :].unsqueeze(1).to_broadcast(shape), ALU.add))
    fx = sb("fx", [NP, NB, 2 * D])

    def publish(srcs, a, headtab):
        heads = gath[:, 0:TK * D].rearrange("p (k w) -> p k w", w=D)
        with nc.Block() as block:
            @block.sync
            def _(sp):
                for to, s_ in srcs:
                    sp_io.by(sp.dma_start(to, s_), 16)
                sp_io.all(sp)

            @block.gpsimd
            def _(pool):
                pool.wait_ge(put_zero, 16 * (ROWS // (P * PA)))
                for b in range(NB):
                    pool_io.by(pool.indirect_dma_start(put, bass.IndirectOffsetOnAxis(ap=idx_put[:, b:b + 1], axis=0),
                                                       a[:, b, :], None, bounds_check=ROWS - 1, oob_is_err=False), 16)
                pool_io.all(pool)

        with nc.Block() as block:
            @block.gpsimd
            def _(pool):
                for k in range(TK):
                    n = min(P, T - k * P)
                    pool_io.by(pool.indirect_dma_start(heads[0:n, k, :], None, headtab,
                                                       bass.IndirectOffsetOnAxis(ap=idx_head[0:n, k:k + 1], axis=0)), 16)
                pool_io.all(pool)

        with nc.Block() as block:
            @block.sync
            def _(sp):
                rows = tile_rows(put)
                for k in range(TK):
                    n = min(P, T - k * P) // G
                    sp_io.by(sp.dma_start(rows[k * P // G:k * P // G + n, :, :], heads[0:n * G, k, :]), 16)
                sp_io.all(sp)

    t2 = nodes(table2)
    publish([(t2[:, :, 0:D], hid[:, :, :]), (t2[:, :, D:2 * D], tab[:, :, 0:D]), (t2[:, :, 2 * D:4 * D], flux),
             (t2[:, :, 4 * D:WG], tab[:, :, D:2 * D]), (nodes(table), hid[:, :, :])], hid, table)
    with nc.Block() as block:
        @block.vector
        def _(v):
            v.tensor_copy(fx[:, :, :], flux)

    def flux_pass():
        s = Pass("p2", table2, WG, W2, 2)
        names = ("expanded z_ready turned h1 m1 h2 m2 h3 y yb_ready squared var1 var_ready root rstd_ready t_ready "
                 "u_ready v_ready f1 f_ready wx_ready")
        (expanded, z_ready, turned, h1, m1, h2, m2, h3, y, yb_ready, squared, var1, var_ready, root, rstd_ready, t_ready,
         u_ready, v_ready, f1, f_ready, wx_ready) = (s.sem(n) for n in names.split())
        zb, ft = carve(0, (G, D)), carve(512, (G, D, 2))
        fl = [carve(1536 + 512 * u, (G, D)) for u in range(4)]
        wxb = [carve(3584 + 512 * u, (G, D)) for u in range(4)]
        h1b, h2b, h3b, sq, ub = (carve(5632 + 512 * k, (512,)) for k in range(5))
        ysb = [carve(8192 + 512 * u, (G, D)) for u in range(2)]
        var, sd, rstd = (carve(9300 + 8 * k, (G,)) for k in range(3))
        wd = [P, G, D]
        lanes = ((5, 0, 3), (6, 3, 6), (7, 6, 8))

        def per_tile(a):
            return a.rearrange("p (g d) -> p g d", g=G)

        with nc.Block() as block:
            @block.gpsimd
            def _(pool):
                s.gather(pool, f_ready)

            @block.sync
            def _(sp):
                def step(at):
                    if g := at(-2):
                        s.load_rows(sp, g)
                    if g := at(-1):
                        s.load_put(sp, g, expanded)
                    if g := at(4):
                        s.store(sp, g)
                ticks(sp, step)
                s.all_stored(sp)

            @block.vector
            def _(v):
                def rstd_of(g):
                    v.wait_ge(root, done(g))
                    prior(v, t_ready, g, 1)
                    v.reciprocal(rstd, sd).then_inc(rstd_ready, 1)

                def weigh(g):
                    out = vals[g.slot(2)]
                    v.wait_ge(rstd_ready, done(g))
                    prior(v, s.summed, g, 2)
                    v.tensor_scalar(out[:, :, 2 * D:W2], nvec[:, bass.ds(g.n * G, G), :], 1.0, None, ALU.mult)
                    v.tensor_tensor(out[:, :, D:2 * D], ysb[g.slot(2)], rstd.unsqueeze(2).to_broadcast(wd), ALU.mult
                                    ).then_inc(t_ready, 1)
                    v.wait_ge(t_ready, done(g))
                    v.wait_ge(wx_ready, done(g))
                    v.tensor_tensor(per_tile(ub), out[:, :, D:2 * D], wxb[g.slot(4)], ALU.mult).then_inc(u_ready, 1)
                    v.wait_ge(u_ready, done(g))
                    v.wait_ge(f_ready, done(g))
                    v.tensor_tensor(out[:, :, 0:D], per_tile(ub), fl[g.slot(4)], ALU.add).then_inc(v_ready, 1)

                def sum_first(g):
                    s.rows_here(v, g)
                    v.wait_ge(expanded, done(g))
                    prior(v, turned, g, 1)
                    v.tensor_tensor(zb, per_tile(bank[0][:, :]), s.rows[g.slot(2)][:, :, 0:D], ALU.add).then_inc(z_ready, 1)

                def biased(g):
                    v.wait_ge(y, done(g))
                    prior(v, t_ready, g, 2)
                    prior(v, squared, g, 2)
                    v.tensor_tensor(ysb[g.slot(2)], per_tile(bank[4][:, :]), abob[:, :].unsqueeze(1).to_broadcast(wd), ALU.add
                                    ).then_inc(yb_ready, 1)

                def flux_part(g):
                    r = s.rows[g.slot(2)]
                    prior(v, f_ready, g, 1)
                    v.tensor_tensor(ft, r[:, :, 2 * D:4 * D].rearrange("p g (c d) -> p g c d", d=2),
                                    nvec[:, bass.ds(g.n * G, G), :].unsqueeze(2).to_broadcast([P, G, D, 2]),
                                    ALU.mult).then_inc(f1, 1)
                    v.wait_ge(f1, done(g))
                    prior(v, v_ready, g, 4)
                    v.tensor_reduce(fl[g.slot(4)], ft, X, ALU.add).then_inc(f_red, 1)
                    v.wait_ge(f_red, done(g))
                    v.wait_ge(wx_ready, done(g))
                    v.tensor_tensor(fl[g.slot(4)], fl[g.slot(4)], r[:, :, 4 * D:WG], ALU.add).then_inc(f_ready, 1)

                def variance(g):
                    v.wait_ge(squared, done(g))
                    prior(v, root, g, 1)
                    v.tensor_reduce(var, per_tile(sq), X, ALU.add).then_inc(var1, 1)
                    v.wait_ge(var1, done(g))
                    v.tensor_scalar(var, var, 1.0 / D, EPS, ALU.mult, ALU.add).then_inc(var_ready, 1)

                f_red = s.sem("f_red")

                def step(at):
                    if g := at(3):
                        rstd_of(g)
                        weigh(g)
                    if g := at(-2):
                        s.stage_idx(v, g)
                    if g := at(2):
                        biased(g)
                    if g := at(0):
                        sum_first(g)
                        flux_part(g)
                    if g := at(2):
                        variance(g)
                    if g := at(-1):
                        s.compare(v, g)
                ticks(v, step)

            @block.tensor
            def _(pe):
                def expand(g):
                    pe.wait_ge(s.same_ready, done(g))
                    pe.wait_ge(s.put_in[g.slot(2)], g.turn(2) * 16 + 16)
                    prior(pe, z_ready, g, 1)
                    for j in range(G):
                        mm = pe.matmul(bank[0][:, j * D:(j + 1) * D], same[g.slot(4)][:, j, :], putr[g.slot(2)][:, j, :],
                                       start=True, stop=True)
                    mm.then_inc(expanded, 1)

                def turn_z(g):
                    pe.wait_ge(z_ready, done(g))
                    prior(pe, h1, g, 1)
                    for j in range(4):
                        mm = pe.transpose(bank[1][:, j * P:(j + 1) * P],
                                          zb[:, 2 * j:2 * j + 2, :].rearrange("p a d -> p (a d)"), ident[:, :])
                    mm.then_inc(turned, 1)

                def hidden(g, i, ready, used, out):
                    pe.wait_ge(ready, done(g))
                    prior(pe, used, g, 1)
                    pe.matmul(bank[2 + i][:, :], abd[i][:, :], (h1b, h2b)[i], start=True, stop=True).then_inc(out, 1)

                def last(g):
                    pe.wait_ge(h3, done(g))
                    prior(pe, yb_ready, g, 1)
                    for j in range(4):
                        mm = pe.matmul(bank[4][:, j * P:(j + 1) * P], h3b[:, j * P:(j + 1) * P], abd[2][:, :],
                                       start=True, stop=True)
                    mm.then_inc(y, 1)

                def sums_of(g):
                    pe.wait_ge(v_ready, done(g))
                    prior(pe, s.out_ready, g, 1)
                    for c, a, b in lanes:
                        for j in range(a, b):
                            mm = pe.matmul(bank[c][:, (j - a) * W2:(j - a + 1) * W2], same[g.slot(4)][:, j, :],
                                           vals[g.slot(2)][:, j, :], start=True, stop=True)
                    mm.then_inc(s.summed, 1)

                def step(at):
                    if g := at(1):
                        hidden(g, 0, h1, h2, m1)
                    if g := at(0):
                        expand(g)
                    if g := at(1):
                        hidden(g, 1, h2, h3, m2)
                    if g := at(0):
                        turn_z(g)
                    if g := at(3):
                        sums_of(g)
                    if g := at(1):
                        last(g)
                ticks(pe, step)

            @block.scalar
            def _(act):
                def relu(g, i, src_bank, to, ready, used, out):
                    act.wait_ge(ready, done(g))
                    prior(act, used, g, 1)
                    act.activation(to, bank[src_bank][:, :], ACT.Relu, bias=ab[:, i:i + 1]).then_inc(out, 1)

                def square(g):
                    act.wait_ge(yb_ready, done(g))
                    prior(act, var1, g, 1)
                    act.activation(sq, ysb[g.slot(2)].rearrange("p g d -> p (g d)"), ACT.Square).then_inc(squared, 1)

                def keep_wx(g):
                    s.rows_here(act, g)
                    prior(act, u_ready, g, 4)
                    act.copy(wxb[g.slot(4)], s.rows[g.slot(2)][:, :, D:2 * D]).then_inc(wx_ready, 1)

                def sqrt(g):
                    act.wait_ge(var_ready, done(g))
                    prior(act, rstd_ready, g, 1)
                    act.activation(sd, var, ACT.Sqrt).then_inc(root, 1)

                def evict(g):
                    act.wait_ge(s.summed, done(g))
                    prior_dma(act, s.stored[g.slot(2)], g, 2)
                    for c, a, b in lanes:
                        ins = act.copy(s.out[g.slot(2)][:, a * W2:b * W2], bank[c][:, 0:(b - a) * W2])
                    ins.then_inc(s.out_ready, 1)

                def step(at):
                    if g := at(1):
                        relu(g, 1, 2, h2b, m1, m2, h2)
                    if g := at(2):
                        square(g)
                    if g := at(0):
                        keep_wx(g)
                    if g := at(1):
                        relu(g, 2, 3, h3b, m2, y, h3)
                    if g := at(0):
                        relu(g, 0, 1, h1b, turned, m1, h1)
                    if g := at(2):
                        sqrt(g)
                    if g := at(3):
                        evict(g)
                ticks(act, step)

    flux_pass()
    collect("p2", W2)
    with nc.Block() as block:
        @block.vector
        def _(v):
            wide = [NP, NB, D]
            nv = r_last[:, :, 2 * D:W2].unsqueeze(2).to_broadcast([NP, NB, D, 2])
            f4 = fx[:, :, :].rearrange("p b (c d) -> p b c d", d=2)
            dve(v, v.tensor_tensor(f4, f4, nv, ALU.mult))
            dve(v, v.tensor_reduce(hid[:, :, :], f4, X, ALU.add))
            dve(v, v.tensor_tensor(agg[:, :, :], agg[:, :, :], hid[:, :, :], ALU.add))
            t = r_last[:, :, D:2 * D]
            dve(v, v.tensor_tensor(t, t, tab[:, :, 0:D], ALU.mult))
            dve(v, v.tensor_tensor(hid[:, :, :], tab[:, :, D:2 * D], deg[:, :].unsqueeze(2).to_broadcast(wide), ALU.mult))
            dve(v, v.tensor_tensor(t, t, hid[:, :, :], ALU.add))
            dve(v, v.tensor_tensor(agg[:, :, :], agg[:, :, :], t, ALU.subtract))
            dve(v, v.tensor_tensor(agg[:, :, :], agg[:, :, :], xs[:, :, :], ALU.add))
    residual(agg[:, :, :])

    turn_nodes(xs, featT)
    qs = hid[:, :, :]
    for n, to in (("k", tab[:, :, 0:D]), ("v", tab[:, :, D:2 * D]), ("q", qs)):
        project(featT, D + 1, wts[n][:, :], D)
        with nc.Block() as block:
            @block.vector
            def _(v):
                for view, b, m in by_bank(D):
                    v.tensor_copy(to[:, b:b + m, :], view)
    kv = dram("kv", [N, 2 * D])
    publish([(nodes(kv), tab[:, :, :]), (nodes(table), qs)], qs, table)

    def reverse(ap_tensor, rows, n):
        a = ap_tensor
        return bass.AP(tensor=a.tensor, offset=a.offset + n - 1, ap=[list(a.ap[0]), [-1, n]])

    def attention_pass():
        s = Pass("p3", kv, 2 * D, W3, 4)
        names = "expanded qk reduced scored turned f1 flagged scanned mx back dif_ready e_ready v_ready"
        expanded, qk, reduced, scored, turned, f1, flagged, scanned, mx, back, dif_ready, e_ready, v_ready = (
            s.sem(n) for n in names.split())
        heads_in = [s.sem(f"heads_in{u}") for u in range(2)]
        GH = G * H
        prod = carve(0, (G, D))
        sc = [carve(512 + 32 * u, (GH,)) for u in range(4)]
        mb = [carve(640 + 32 * u, (GH,)) for u in range(4)]
        dif = carve(800, (GH,))
        flags = carve(1024, (2 * P,), parts=GH)
        run_f, run_b, smax = (carve(1280 + P * k, (P,), parts=GH) for k in range(3))
        vals3 = [vals[u].rearrange("p g w -> p (g w)")[:, 0:G * (D + H)].rearrange("p (g w) -> p g w", w=D + H)
                 for u in range(2)]
        lanes = ((4, 0, 4), (5, 4, 8))

        with nc.Block() as block:
            @block.gpsimd
            def _(pool):
                s.gather(pool, v_ready)

            @block.sync
            def _(sp):
                def step(at):
                    if g := at(-2):
                        s.load_rows(sp, g)
                    if g := at(-1):
                        s.load_put(sp, g, expanded)
                    if g := at(0):
                        prior(sp, f1, g, 2)
                        sp.dma_start(rows32[g.slot(2)][:, :],
                                     head_groups[bass.ds(g.n, 1), :, :].rearrange("a j c -> (a j) c")
                                     ).then_inc(heads_in[g.slot(2)], 16)
                    if g := at(4):
                        s.store(sp, g)
                ticks(sp, step)
                s.all_stored(sp)

            @block.vector
            def _(v):
                vec_done.by(v.memset(flags, 0.0))
                vec_done.all(v)

                def score(g):
                    s.rows_here(v, g)
                    v.wait_ge(expanded, done(g))
                    prior(v, reduced, g, 1)
                    v.tensor_tensor(prod, bank[0][:, :].rearrange("p (g d) -> p g d", g=G), s.rows[g.slot(4)][:, :, 0:D],
                                    ALU.mult).then_inc(qk, 1)
                    v.wait_ge(qk, done(g))
                    prior(v, dif_ready, g, 4)
                    a = sc[g.slot(4)]
                    v.tensor_reduce(a, prod.rearrange("p g (h d) -> p (g h) d", h=H), X, ALU.add).then_inc(reduced, 1)
                    v.wait_ge(reduced, done(g))
                    a = a.rearrange("p (g h) -> p g h", h=H)
                    v.tensor_tensor(a, a, ebias[:, bass.ds(g.n * G, G), :], ALU.add).then_inc(scored, 1)

                def flag(g):
                    r = rows32[g.slot(2)]
                    v.wait_ge(heads_in[g.slot(2)], g.turn(2) * 16 + 16)
                    prior(v, scanned, g, 1)
                    v.tensor_tensor(flags[:, 1:P], r[:, 1:P], r[:, 0:P - 1], ALU.not_equal).then_inc(f1, 1)
                    v.wait_ge(f1, done(g))
                    v.tensor_scalar(flags[:, 1:P], flags[:, 1:P], NEG, None, ALU.mult).then_inc(flagged, 1)

                def scan(g):
                    v.wait_ge(flagged, done(g))
                    v.wait_ge(turned, done(g))
                    prior(v, mx, g, 1)
                    t = bank[2][0:GH, 0:P]
                    v.tensor_tensor_scan(run_f, flags[:, 0:P], t, NEG, ALU.add, ALU.max)
                    v.tensor_tensor_scan(reverse(run_b, GH, P), reverse(flags[:, 1:P + 1], GH, P), reverse(t, GH, P),
                                         NEG, ALU.add, ALU.max).then_inc(scanned, 1)
                    v.wait_ge(scanned, done(g))
                    prior(v, back, g, 1)
                    v.tensor_tensor(smax, run_f, run_b, ALU.max).then_inc(mx, 1)

                def differ(g):
                    v.wait_ge(back, done(g))
                    prior(v, e_ready, g, 1)
                    prior(v, s.out_ready, g, 4)
                    v.tensor_copy(mb[g.slot(4)], bank[3][:, 0:GH])
                    v.tensor_tensor(dif, sc[g.slot(4)], bank[3][:, 0:GH], ALU.subtract).then_inc(dif_ready, 1)

                def weigh(g):
                    v.wait_ge(e_ready, done(g))
                    out = vals3[g.slot(2)]
                    v.tensor_tensor(out[:, :, 0:D].rearrange("p g (h d) -> p g h d", h=H),
                                    s.rows[g.slot(4)][:, :, D:2 * D].rearrange("p g (h d) -> p g h d", h=H),
                                    out[:, :, D:D + H].unsqueeze(3).to_broadcast([P, G, H, HD]), ALU.mult
                                    ).then_inc(v_ready, 1)

                def step(at):
                    if g := at(-2):
                        s.stage_idx(v, g)
                    if g := at(2):
                        differ(g)
                    if g := at(1):
                        flag(g)
                        scan(g)
                    if g := at(0):
                        score(g)
                    if g := at(2):
                        weigh(g)
                    if g := at(-1):
                        s.compare(v, g)
                ticks(v, step)

            @block.tensor
            def _(pe):
                def expand(g):
                    pe.wait_ge(s.same_ready, done(g))
                    pe.wait_ge(s.put_in[g.slot(2)], g.turn(2) * 16 + 16)
                    prior(pe, qk, g, 1)
                    for j in range(G):
                        mm = pe.matmul(bank[0][:, j * D:(j + 1) * D], same[g.slot(4)][:, j, :], putr[g.slot(2)][:, j, :],
                                       start=True, stop=True)
                    mm.then_inc(expanded, 1)

                def step(at):
                    if g := at(1):
                        pe.wait_ge(scored, done(g))
                        prior(pe, scanned, g, 1)
                        pe.transpose(bank[2][0:GH, 0:P], sc[g.slot(4)], ident[:, :]).then_inc(turned, 1)
                    if g := at(0):
                        expand(g)
                    if g := at(1):
                        pe.wait_ge(mx, done(g))
                        prior(pe, dif_ready, g, 1)
                        pe.matmul(bank[3][:, 0:GH], smax, ident[0:GH, 0:GH], start=True, stop=True).then_inc(back, 1)
                    if g := at(3):
                        pe.wait_ge(v_ready, done(g))
                        prior(pe, s.out_ready, g, 1)
                        for c, a, b in lanes:
                            for j in range(a, b):
                                mm = pe.matmul(bank[c][:, (j - a) * P:(j - a) * P + D + H], same[g.slot(4)][:, j, :],
                                               vals3[g.slot(2)][:, j, :], start=True, stop=True)
                        mm.then_inc(s.summed, 1)
                ticks(pe, step)

            @block.scalar
            def _(act):
                def step(at):
                    if g := at(3):
                        act.wait_ge(s.summed, done(g))
                        prior_dma(act, s.stored[g.slot(2)], g, 2)
                        to = s.out[g.slot(2)].rearrange("p (g w) -> p g w", w=W3)
                        act.copy(to[:, :, D + H:W3], mb[g.slot(4)].rearrange("p (g h) -> p g h", h=H))
                        for c, a, b in lanes:
                            ins = act.copy(to[:, a:b, 0:D + H],
                                           bank[c][:, :].rearrange("p (g w) -> p g w", g=4)[:, :, 0:D + H])
                        ins.then_inc(s.out_ready, 1)
                    if g := at(2):
                        act.wait_ge(dif_ready, done(g))
                        prior(act, s.summed, g, 2)
                        act.activation(vals3[g.slot(2)][:, :, D:D + H], dif.rearrange("p (g h) -> p g h", h=H),
                                       ACT.Exp).then_inc(e_ready, 1)
                ticks(act, step)

    attention_pass()
    tmid = pick(W3)

    with when_mids("p3"):
        mT, flT, runT, runB = (gath[0:H, 896 * k:896 * k + T] for k in range(4))
        with nc.Block() as block:
            @block.tensor
            def _(pe):
                for k in range(TK):
                    pe.transpose(bank[k // 4][0:H, (k % 4) * P:(k % 4 + 1) * P], tmid[:, k, D + H:W3], ident[:, :])

        with nc.Block() as block:
            @block.vector
            def _(v):
                for k in range(TK):
                    w = min(P, T - k * P)
                    v.tensor_copy(mT[:, k * P:k * P + w], bank[k // 4][0:H, (k % 4) * P:(k % 4) * P + w])
                dve(v, v.memset(gath[0:H, 896:896 + T + 1], 0.0))
                dve(v, v.tensor_tensor(flT[:, 1:T], midrow[:, 1:T], midrow[:, 0:T - 1], ALU.not_equal))
                dve(v, v.tensor_scalar(flT[:, 1:T], flT[:, 1:T], NEG, None, ALU.mult))
                flR = gath[0:H, 897:897 + T]
                dve(v, v.tensor_tensor_scan(runT, flT, mT, NEG, ALU.add, ALU.max))
                dve(v, v.tensor_tensor_scan(reverse(runB, H, T), reverse(flR, H, T), reverse(mT, H, T), NEG, ALU.add, ALU.max))
                dve(v, v.tensor_tensor(runT, runT, runB, ALU.max))

        gcol = carve(600, (TK, H))
        mw = carve(640, (TK, H))
        ismid = carve(680, (TK,))
        tm3 = carve(1024, (TK, W3 + 1))
        with nc.Block() as block:
            @block.tensor
            def _(pe):
                for k in range(TK):
                    w = min(P, T - k * P)
                    pe.transpose(bank[0][0:w, k * H:(k + 1) * H], runT[:, k * P:k * P + w], ident[0:H, 0:H])

            @block.vector
            def _(v):
                v.memset(gcol, 0.0)

        with nc.Block() as block:
            @block.vector
            def _(v):
                g0 = bank[0][:, 0:TK * H].rearrange("p (k h) -> p k h", h=H)
                v.tensor_copy(gcol[:, 0:TK - 1, :], g0[:, 0:TK - 1, :])
                dve(v, v.tensor_copy(gcol[0:TL, TK - 1, :], g0[0:TL, TK - 1, :]))
                dve(v, v.tensor_tensor(mw, tmid[:, :, D + H:W3], gcol, ALU.subtract))
                dve(v, v.tensor_scalar(ismid, midnode[:, :], 0.0, None, ALU.is_ge))

        with nc.Block() as block:
            @block.scalar
            def _(act):
                act.activation(mw, mw, ACT.Exp)

        W4 = W3 + 1
        with nc.Block() as block:
            @block.vector
            def _(v):
                dve(v, v.tensor_tensor(mw, mw, ismid.unsqueeze(2).to_broadcast([P, TK, H]), ALU.mult))
                for k in range(TK):
                    v.tensor_tensor(tm3[:, k, 0:D].rearrange("p (h d) -> p h d", h=H),
                                    tmid[:, k, 0:D].rearrange("p (h d) -> p h d", h=H),
                                    mw[:, k, :].unsqueeze(2).to_broadcast([P, H, HD]), ALU.mult)
                v.tensor_tensor(tm3[:, :, D:D + H], tmid[:, :, D:D + H], mw, ALU.mult)
                v.tensor_tensor(tm3[:, :, D + H:W3], gcol, midlast[:, :].unsqueeze(2).to_broadcast([P, TK, H]), ALU.mult)
                dve(v, v.tensor_copy(tm3[:, :, W3:W4], midlast[:, :].unsqueeze(2)))
        r_mid = mids("p3", tm3, W4)
        top2 = carve(128, (NB, H), parts=NP)
        m_f, m_m = carve(256, (NB, H), parts=NP), carve(384, (NB, H), parts=NP)
        none = carve(700, (NB, 1), parts=NP)

        def scale_rows(v, r, by):
            for b in range(NB):
                a = r[:, b, 0:D].rearrange("p (h d) -> p h d", h=H)
                v.tensor_tensor(a, a, by[:, b, :].unsqueeze(2).to_broadcast([NP, H, HD]), ALU.mult)
            dve(v, v.tensor_tensor(r[:, :, D:D + H], r[:, :, D:D + H], by, ALU.mult))

        with nc.Block() as block:
            @block.vector
            def _(v):
                dve(v, v.tensor_scalar(none, r_mid[:, :, W3:W4], -1.0, -NEG, ALU.add, ALU.mult))
                mm = r_mid[:, :, D + H:W3]
                dve(v, v.tensor_tensor(mm, mm, none.to_broadcast([NP, NB, H]), ALU.add))
                dve(v, v.tensor_tensor(top2, r_first[:, :, D + H:W3], mm, ALU.max))
                v.tensor_tensor(m_f, r_first[:, :, D + H:W3], top2, ALU.subtract)
                dve(v, v.tensor_tensor(m_m, mm, top2, ALU.subtract))

        with nc.Block() as block:
            @block.scalar
            def _(act):
                act.activation(m_f, m_f, ACT.Exp)
                act.activation(m_m, m_m, ACT.Exp)

        with nc.Block() as block:
            @block.vector
            def _(v):
                scale_rows(v, r_first, m_f)
                scale_rows(v, r_mid, m_m)
                dve(v, v.tensor_tensor(r_first[:, :, 0:D + H], r_first[:, :, 0:D + H], r_mid[:, :, 0:D + H], ALU.add))
                dve(v, v.tensor_copy(r_first[:, :, D + H:W3], top2))
    ms = [carve(128 * k, (NB, H), parts=NP) for k in range(5)]
    with nc.Block() as block:
        @block.vector
        def _(v):
            top = ms[3]
            dve(v, v.tensor_tensor(top, r_last[:, :, D + H:W3], r_first[:, :, D + H:W3], ALU.max))
            dve(v, v.tensor_scalar(top, top, -1.0e9, None, ALU.max))
            for k, r in enumerate((r_last, r_first)):
                ins = v.tensor_tensor(ms[k], r[:, :, D + H:W3], top, ALU.subtract)
            dve(v, ins)

    with nc.Block() as block:
        @block.scalar
        def _(act):
            for k in range(2):
                act.activation(ms[k], ms[k], ACT.Exp)

    with nc.Block() as block:
        @block.vector
        def _(v):
            for k, r in enumerate((r_last, r_first)):
                v.tensor_tensor(r[:, :, 0:D].rearrange("p b (h d) -> p b h d", h=H),
                                r[:, :, 0:D].rearrange("p b (h d) -> p b h d", h=H),
                                ms[k].unsqueeze(3).to_broadcast([NP, NB, H, HD]), ALU.mult)
                dve(v, v.tensor_tensor(r[:, :, D:D + H], r[:, :, D:D + H], ms[k], ALU.mult))
            S = D + H
            dve(v, v.tensor_tensor(r_last[:, :, 0:S], r_last[:, :, 0:S], r_first[:, :, 0:S], ALU.add))
            dve(v, v.tensor_scalar(ms[4], r_last[:, :, D:S], 1e-12, None, ALU.add))
            dve(v, v.reciprocal(ms[3], ms[4]))
            dve(v, v.tensor_tensor(agg[:, :, :].rearrange("p b (h d) -> p b h d", h=H),
                                   r_last[:, :, 0:D].rearrange("p b (h d) -> p b h d", h=H),
                                   ms[3].unsqueeze(3).to_broadcast([NP, NB, H, HD]), ALU.mult))
    turn_nodes(agg, featT)
    project(featT, D + 1, wts["o"][:, :], D)
    with nc.Block() as block:
        @block.vector
        def _(v):
            for view, b, m in by_bank(D):
                v.tensor_copy(agg[:, b:b + m, :], view)
    residual(agg[:, :, :])
    with nc.Block() as block:
        @block.sync
        def _(sp):
            sp_io.by(sp.dma_start(nodes(out), xs[:, :, :]), 16)
            sp_io.all(sp)


_INS = ["x", "src", "dst", "edge_attr_2", "edge_type_4", "L0_gnn_W1", "L0_gnn_b1", "L0_gnn_W2", "L0_gnn_b2",
        "L2_gnn_flux_Wh", "L2_gnn_flux_bh", "L2_gnn_flux_Wo", "L2_gnn_flux_bo", "L2_gnn_flux_ln_w",
        "L2_gnn_flux_ln_b", "L2_gnn_a_Wh", "L2_gnn_a_bh", "L2_gnn_a_Wo", "L2_gnn_a_bo", "L2_gnn_a_ln_w",
        "L2_gnn_a_ln_b", "L3_gnn_Wq", "L3_gnn_bq", "L3_gnn_Wk", "L3_gnn_bk", "L3_gnn_Wv", "L3_gnn_bv",
        "L3_gnn_Wo", "L3_gnn_bo", "L3_gnn_edge_bias"]


def kernel(**inputs):
    import numpy as _np
    import concourse.bacc as _bacc
    from concourse import mybir as _mybir
    from concourse.bass_utils import run_bass_kernel_spmd as _run

    nc = _bacc.Bacc("TRN2", target_bir_lowering=False, num_devices=1)
    arrays, args = {}, []
    for name in _INS:
        a = _np.ascontiguousarray(inputs[name])
        arrays[f"in_{name}"] = a
        args.append(nc.dram_tensor(f"in_{name}", a.shape, _mybir.dt.from_np(a.dtype), kind="ExternalInput").ap())
    out = nc.dram_tensor("out_0", (N, D), F32, kind="ExternalOutput").ap()
    build(nc, *args, out)
    r = _run(nc, [arrays], core_ids=[0])
    return r.results[0]["out_0"]
```

```python
import concourse.bass as bass
from concourse import mybir

F32 = mybir.dt.float32
BF16 = mybir.dt.bfloat16
U8 = mybir.dt.uint8
I32 = mybir.dt.int32
I16 = mybir.dt.int16
ALU = mybir.AluOpType
ACT = mybir.ActivationFunctionType
X = mybir.AxisListType.X

N = 3125
E = 100000
D = 64
H = 4
HD = D // H
P = 128
NP, NB = 125, 25
G = 8
NG = -(-E // (P * G))
T = NG * G
TK = -(-T // P)
TL = T - (TK - 1) * P
ROWS = T * P
NEG = -3.0e38
EPS = 1e-5
PA = 28
assert ROWS % (P * PA) == 0
WG = 5 * D
W2 = 2 * D + 2
W3 = D + 2 * H
UT = 4
NU = T // UT
UL = 500 // NB
CW = -(-(N + UL) // 4) * 4
MAXC = 127.0
UA, UK = 5, NB // 5
assert NU % 4 == 0 and NU * UT == T


def build(nc, x, src, dst, edge_attr_2, edge_type_4, W1, b1, W2_, b2, fWh, fbh, fWo, fbo, flw, flb,
          aWh, abh, aWo, abo, alw, alb, Wq, bq, Wk, bk, Wv, bv, Wo, bo, edge_bias, out):
    sems = {}

    def sem(name):
        if name not in sems:
            sems[name] = nc.alloc_semaphore(name)
        return sems[name]

    def sb(name, shape, dt=F32):
        return nc.alloc_sbuf_tensor(name, shape, dt)

    class Count:

        def __init__(self, name):
            self.sem, self.n = sem(name), 0

        def by(self, ins, k=1):
            self.n += k
            return ins.then_inc(self.sem, k)

        def all(self, eng):
            eng.wait_ge(self.sem, self.n)

    put_zero = sem("put_zero")
    vec_done, act_done, pool_done = Count("vec_done"), Count("act_done"), Count("pool_done")
    sp_io, pool_io = Count("sp_io"), Count("pool_io")

    def dve(eng, ins):
        vec_done.by(ins)
        vec_done.all(eng)

    def bc(ap, shape):
        return ap.to_broadcast(shape)

    bank = [nc.alloc_psum_tensor(f"bank{i}", [P, 512], F32) for i in range(8)]
    ident = sb("ident", [P, P])
    src_i = sb("src_i", [P, T], I32)
    dst_f = sb("dst_f", [P, T])
    nvec = sb("nvec", [P, T, 2])
    ebias = sb("ebias", [P, T, H])
    xs = sb("xs", [NP, NB, D])
    agg = sb("agg", [NP, NB, D])
    hid = sb("hid", [NP, NB, D])
    idx_last = sb("idx_last", [NP, NB], I32)
    idx_first = sb("idx_first", [NP, NB], I32)
    idx_put = sb("idx_put", [NP, NB], I32)
    idx_head = sb("idx_head", [P, TK], I32)
    midnode = sb("midnode", [P, TK])
    midlast = sb("midlast", [P, TK])
    anymid = sb("anymid", [1, 1], I32)
    colnode = sb("colnode", [P, NP])
    deg = sb("deg", [NP, NB])
    zeros = sb("zeros", [P, 256])
    midrow = sb("midrow", [H, T])
    base = sb("base", [P, NU])
    base_i = sb("base_i", [1, NU], I32)
    usable = sb("usable", [1, 1], I32)
    AREA = 6 * G * P + 2 * G * D + 4 * G * W2
    SCRATCH, GATH, NODE2 = 9600, 2 * G * WG, NB * 2 * D
    mem = sb("mem", [P, AREA + SCRATCH + GATH + 2 * NODE2])
    area = mem[:, 0:AREA]
    featT = area[0:D + 1, 0:NB * NP]
    hidT = area[0:D + 1, NB * NP:2 * NB * NP]
    scratch = mem[:, AREA:AREA + SCRATCH]
    at_gath = AREA + SCRATCH
    gath = mem[:, at_gath:at_gath + GATH]
    tab, fx = (mem[0:NP, at_gath + GATH + i * NODE2:at_gath + GATH + (i + 1) * NODE2].rearrange("p (b w) -> p b w", b=NB)
               for i in range(2))
    WIDE = UA * P // 2
    KEEP = 3 * NB * D
    assert 2 * UK * WIDE <= KEEP
    SPLIT = 3 * NB * D // 2
    xb = mem[0:NP, KEEP:KEEP + SPLIT].bitcast(BF16).rearrange("p (b w) -> p b w", b=NB)
    at_counts = KEEP + SPLIT
    counts_flat = mem[0:NP, at_counts:at_counts + NB * CW // 4]
    counts = counts_flat.bitcast(U8).rearrange("p (a n) -> p a n", a=NB)
    at_free = at_counts + NB * CW // 4
    assert at_free + 4 * T <= AREA + SCRATCH + GATH + 2 * NODE2

    def carve(o, shape, dt=F32, parts=P):
        n = 1
        for s in shape:
            n *= s
        half = dt is BF16
        v = scratch[0:parts, o:o + (-(-n // 2) if half else n)]
        if dt is not F32:
            v = v.bitcast(dt)[:, 0:n]
        if len(shape) == 2:
            v = v.rearrange("p (a b) -> p a b", a=shape[0])
        if len(shape) == 3:
            v = v.rearrange("p (a b c) -> p a b c", a=shape[0], b=shape[1])
        return v

    def dram(name, shape, dt=F32):
        return nc.dram_tensor(name, shape, dt).ap()

    dst_pad = dram("dst_pad", [T, P], I32)
    ends = dram("ends", [N + 1, 1])
    lastrow = dram("lastrow", [1, T])
    headrow = dram("headrow", [1, T])
    midrow_d = dram("midrow_d", [1, T])
    midlast_d = dram("midlast_d", [1, T])
    table = dram("table", [N, D])
    table2 = dram("table2", [N, WG])
    dst_heads = dram("dst_heads", [T * H, P], I32)
    put = dram("put", [ROWS, D])
    sums = {w: dram(f"sums{w}", [ROWS + 1, w]) for w in (D, W2, W3)}
    nodes = lambda ap: ap.rearrange("(p b) d -> p b d", b=NB)

    def tile_rows(ap):
        return ap[0:ROWS, :].rearrange("(g p j) w -> g p j w", p=P, j=G)[:, 0, :, :]

    raw = {"dst": carve(0, (TK, P), I32), "src": carve(896, (TK, P), I32), "typ": carve(1792, (TK, P), I32)}
    rawf = {"dst": carve(2688, (TK, P)), "src": carve(3584, (TK, P)), "typ": carve(4480, (TK, P))}
    raw_nv = carve(5376, (TK, 2 * P))
    typ_f = carve(7168, (T,))
    eb_b = sb("eb_b", [P, 4 * H])

    full = E // P
    fk, fr = full // P, full % P
    rest = E - full * P

    with nc.Block() as block:
        @block.gpsimd
        def _(pool):
            pool_done.by(pool.memset(ident[:, :], 0.0))
            pool_done.all(pool)
            pool.affine_select(out=ident[:, :], in_=ident[:, :], compare_op=ALU.not_equal, fill=1.0,
                               base=0, pattern=[[-1, P]], channel_multiplier=1)

        @block.vector
        def _(v):
            v.memset(zeros[:, :], 0.0)
            v.memset(raw["dst"][:, TK - 1, :], N)
            v.memset(raw["src"][:, TK - 1, :], 0)
            v.memset(raw["typ"][:, TK - 1, :], 0)
            v.memset(raw_nv[:, TK - 1, :], 0.0)

    with nc.Block() as block:
        @block.sync
        def _(sp):
            for name, a, w in (("dst", dst, 1), ("src", src, 1), ("typ", edge_type_4, 1), ("nv", edge_attr_2, 2)):
                to = raw_nv if name == "nv" else raw[name]
                flat = a.rearrange("e d -> (e d)") if w == 2 else a
                c = P * w
                sp_io.by(sp.dma_start(to[:, 0:fk, :], flat[0:fk * P * c].rearrange("(k r c) -> r k c", r=P, c=c)), 16)
                sp_io.by(sp.dma_start(to[0:fr, fk, :], flat[fk * P * c:full * c].rearrange("(r c) -> r c", c=c)), 16)
                sp_io.by(sp.dma_start(to[fr:fr + 1, fk, 0:rest * w], flat[full * c:E * w].rearrange("(r c) -> r c", r=1)), 16)
            sp_io.by(sp.dma_start(xs[:, :, :], nodes(x)), 16)
            sp_io.by(sp.dma_start(eb_b[:, :], edge_bias.rearrange("k h -> (k h)").partition_broadcast(P)), 16)
            sp_io.all(sp)

    with nc.Block() as block:
        @block.vector
        def _(v):
            for name in raw:
                v.tensor_copy(rawf[name], raw[name])

        @block.scalar
        def _(act):
            flat = put.rearrange("(c p a) w -> c p (a w)", p=P, a=PA).rearrange("c p (m z) -> c p m z", z=256)
            for k in range(flat.shape[0]):
                act.dma_start(flat[k], zeros[:, :].unsqueeze(1).to_broadcast([P, PA * D // 256, 256])).then_inc(put_zero, 16)

        @block.sync
        def _(sp):
            sp_io.by(sp.dma_start(dst_pad[0:(TK - 1) * P, :].rearrange("(k r) c -> r k c", r=P), raw["dst"][:, 0:TK - 1, :]), 16)
            sp_io.by(sp.dma_start(dst_pad[(TK - 1) * P:T, :], raw["dst"][0:TL, TK - 1, :]), 16)
            heads = dst_heads.rearrange("(t h) c -> t h c", h=H)
            for h in range(H):
                sp_io.by(sp.dma_start(heads[0:(TK - 1) * P, h, :].rearrange("(k r) c -> r k c", r=P), raw["dst"][:, 0:TK - 1, :]), 16)
                sp_io.by(sp.dma_start(heads[(TK - 1) * P:T, h, :], raw["dst"][0:TL, TK - 1, :]), 16)
            sp_io.all(sp)

    def turn(sources, place):
        with nc.Block() as block:
            @block.tensor
            def _(pe):
                for i, s in enumerate(sources):
                    pe.transpose(bank[i // 4][:, (i % 4) * P:(i % 4 + 1) * P], s, ident[:, :])

        with nc.Block() as block:
            @block.vector
            def _(v):
                for i in range(len(sources)):
                    to = place(i)
                    w = to.shape[1]
                    v.tensor_copy(to, bank[i // 4][:, (i % 4) * P:(i % 4) * P + w])

    def cols(t):
        return lambda k: t[:, k * P:min((k + 1) * P, T)]

    turn([rawf["dst"][:, k, :] for k in range(TK)], cols(dst_f))
    turn([rawf["src"][:, k, :] for k in range(TK)], cols(src_i))
    turn([rawf["typ"][:, k, :] for k in range(TK)], cols(typ_f))
    for d in range(2):
        turn([raw_nv[:, k, :].rearrange("r (c d) -> r d c", d=2)[:, d, :] for k in range(TK)],
             lambda k: nvec[:, k * P:min((k + 1) * P, T), d])

    with nc.Block() as block:
        @block.sync
        def _(sp):
            sp_io.by(sp.dma_start(lastrow, dst_f[P - 1:P, :]), 16)
            sp_io.by(sp.dma_start(headrow, dst_f[0:1, :]), 16)
            sp_io.all(sp)

        @block.vector
        def _(v):
            mask = carve(0, (T,))
            dve(v, v.memset(ebias[:, :, :], 0.0))
            for k in range(4):
                dve(v, v.tensor_scalar(mask, typ_f, float(k), None, ALU.is_equal))
                for h in range(H):
                    c = k * H + h
                    ins = v.scalar_tensor_tensor(out=ebias[:, :, h], in0=mask, scalar=eb_b[:, c:c + 1],
                                                 in1=ebias[:, :, h], op0=ALU.mult, op1=ALU.add)
                dve(v, ins)

    nodeval = carve(0, (NB,), parts=NP)
    lastb = carve(32, (T,), parts=NP)
    lastH, headH = carve(832, (T,), parts=H), carve(1632, (T,), parts=H)
    five = 5
    cmp5 = carve(2432, (five, T), parts=NP)
    full_tiles = carve(6400, (NB,), parts=NP)
    q_i = carve(6432, (NB,), I32, NP)
    with nc.Block() as block:
        @block.sync
        def _(sp):
            sp_io.by(sp.dma_start(lastb, lastrow.rearrange("a t -> (a t)").partition_broadcast(NP)), 16)
            sp_io.by(sp.dma_start(lastH, lastrow.rearrange("a t -> (a t)").partition_broadcast(H)), 16)
            sp_io.by(sp.dma_start(headH, headrow.rearrange("a t -> (a t)").partition_broadcast(H)), 16)
            sp_io.all(sp)

        @block.gpsimd
        def _(pool):
            pool.iota(nodeval, [[1, NB]], base=0, channel_multiplier=NB, allow_small_or_imprecise_dtypes=True)

    zero1 = carve(9000, (1,), parts=1)
    mlH = carve(7300, (T,), parts=H)
    mid_eq = carve(6464, (T - 2,), parts=H)
    with nc.Block() as block:
        @block.vector
        def _(v):
            for q in range(NB // five):
                a = nodeval[:, q * five:(q + 1) * five]
                dve(v, v.tensor_tensor(cmp5, lastb.unsqueeze(1).to_broadcast([NP, five, T]),
                                       a.unsqueeze(2).to_broadcast([NP, five, T]), ALU.is_le))
                dve(v, v.tensor_reduce(full_tiles[:, q * five:(q + 1) * five], cmp5, X, ALU.add))
            dve(v, v.tensor_copy(q_i, full_tiles))
            dve(v, v.tensor_tensor(mid_eq, lastH[:, 0:T - 2], headH[:, 2:T], ALU.is_equal))
            dve(v, v.memset(midrow[:, :], -1.0))
            dve(v, v.tensor_scalar(midrow[:, 1:T - 1], lastH[:, 0:T - 2], 1.0, None, ALU.add))
            dve(v, v.tensor_tensor(midrow[:, 1:T - 1], midrow[:, 1:T - 1], mid_eq, ALU.mult))
            dve(v, v.tensor_scalar(midrow[:, 1:T - 1], midrow[:, 1:T - 1], -1.0, None, ALU.add))
            dve(v, v.tensor_scalar(mlH, midrow[:, :], float(N), None, ALU.is_lt))
            dve(v, v.tensor_scalar(midrow[:, :], midrow[:, :], 1.0, None, ALU.add))
            dve(v, v.tensor_tensor(midrow[:, :], midrow[:, :], mlH, ALU.mult))
            dve(v, v.tensor_scalar(midrow[:, :], midrow[:, :], -1.0, None, ALU.add))
            dve(v, v.memset(mlH, 0.0))
            dve(v, v.tensor_tensor(mlH[:, 0:T - 1], midrow[:, 0:T - 1], midrow[:, 1:T], ALU.not_equal))
            dve(v, v.tensor_scalar(mid_eq, midrow[:, 1:T - 1], 0.0, None, ALU.is_ge))
            dve(v, v.tensor_tensor(mlH[:, 1:T - 1], mlH[:, 1:T - 1], mid_eq, ALU.mult))
            dve(v, v.memset(mlH[:, 0:1], 0.0))
            dve(v, v.tensor_reduce(zero1, mlH[0:1, :], X, ALU.max))
            dve(v, v.tensor_copy(anymid[:, :], zero1))

    rows_of = carve(2432, (NB, P), I32, NP)
    with nc.Block() as block:
        @block.gpsimd
        def _(pool):
            for b in range(NB):
                pool_io.by(pool.indirect_dma_start(rows_of[:, b, :], None, dst_pad,
                                                   bass.IndirectOffsetOnAxis(ap=q_i[:, b:b + 1], axis=0)), 16)
            pool_io.all(pool)

        @block.sync
        def _(sp):
            sp_io.by(sp.dma_start(midrow_d, midrow[0:1, :]), 16)
            sp_io.by(sp.dma_start(midlast_d, mlH[0:1, :]), 16)
            sp_io.all(sp)

    cmp_f = carve(6464, (NB,), parts=NP)
    end_f = carve(6510, (NB,), parts=NP)
    start_f = carve(6540, (NB,), parts=NP)
    with nc.Block() as block:
        @block.vector
        def _(v):
            dve(v, v.tensor_tensor(rows_of, rows_of, nodeval.unsqueeze(2).to_broadcast([NP, NB, P]), ALU.is_le))
            dve(v, v.tensor_reduce(cmp_f, rows_of, X, ALU.add))
            dve(v, v.scalar_tensor_tensor(out=end_f, in0=full_tiles, scalar=float(P), in1=cmp_f, op0=ALU.mult, op1=ALU.add))
            v.memset(zero1, 0.0)
            v.memset(midnode[:, :], -1.0)
            v.memset(midlast[:, :], 0.0)

    def tile_cols(row):
        return row.rearrange("a t -> (a t)")

    with nc.Block() as block:
        @block.sync
        def _(sp):
            sp_io.by(sp.dma_start(ends[1:N + 1, :].rearrange("(p b) a -> p (b a)", b=NB), end_f), 16)
            sp_io.by(sp.dma_start(ends[0:1, :], zero1), 16)
            for to, row in ((midnode, midrow_d), (midlast, midlast_d)):
                flat = tile_cols(row)
                for k in range(TK):
                    n = min(P, T - k * P)
                    sp_io.by(sp.dma_start(to[0:n, k:k + 1], flat[k * P:k * P + n].rearrange("(r a) -> r a", a=1)), 16)
            sp_io.all(sp)

    with nc.Block() as block:
        @block.sync
        def _(sp):
            sp_io.by(sp.dma_start(start_f, ends[0:N, :].rearrange("(p b) a -> p (b a)", b=NB)), 16)
            sp_io.all(sp)

        @block.gpsimd
        def _(pool):
            pool.iota(colnode[:, :], [[NB, NP]], base=0, channel_multiplier=0,
                      allow_small_or_imprecise_dtypes=True)

    e_i, t_i, r_i = (carve(6600 + 32 * i, (NB,), I32, NP) for i in range(3))
    tf, has, two, row_f, tl_f = (carve(6700 + 32 * i, (NB,), parts=NP) for i in range(5))

    with nc.Block() as block:
        @block.vector
        def _(v):
            v.tensor_tensor(deg[:, :], end_f, start_f, ALU.subtract)

            def row(edge, keep_tile):
                dve(v, v.tensor_copy(e_i, edge))
                dve(v, v.tensor_scalar(t_i, e_i, 7, None, ALU.arith_shift_right))
                dve(v, v.tensor_copy(keep_tile, t_i))
                dve(v, v.tensor_scalar(r_i, t_i, 7, None, ALU.bitwise_and))
                dve(v, v.tensor_copy(row_f, r_i))
                dve(v, v.tensor_scalar(t_i, e_i, 10, None, ALU.arith_shift_right))
                dve(v, v.tensor_copy(tf, t_i))
                dve(v, v.scalar_tensor_tensor(out=row_f, in0=tf, scalar=float(P * G), in1=row_f, op0=ALU.mult, op1=ALU.add))
                dve(v, v.tensor_scalar(t_i, e_i, 127, None, ALU.bitwise_and))
                dve(v, v.tensor_copy(tf, t_i))
                dve(v, v.scalar_tensor_tensor(out=row_f, in0=tf, scalar=float(G), in1=row_f, op0=ALU.mult, op1=ALU.add))

            def choose(to, mask, other):
                dve(v, v.tensor_scalar(row_f, row_f, float(-other), None, ALU.add))
                dve(v, v.tensor_tensor(row_f, row_f, mask, ALU.mult))
                dve(v, v.tensor_scalar(to, row_f, float(other), None, ALU.add))

            dve(v, v.tensor_tensor(has, end_f, start_f, ALU.is_gt))
            dve(v, v.tensor_scalar(end_f, end_f, -1.0, None, ALU.add))
            row(end_f, tl_f)
            choose(idx_last[:, :], has, ROWS)
            row(start_f, full_tiles)
            dve(v, v.tensor_tensor(two, full_tiles, tl_f, ALU.is_lt))
            dve(v, v.tensor_tensor(two, two, has, ALU.mult))
            choose(idx_first[:, :], two, ROWS)
            row(start_f, full_tiles)
            dve(v, v.tensor_scalar(two, tf, 0.0, None, ALU.is_gt))
            dve(v, v.tensor_tensor(two, two, has, ALU.mult))
            choose(idx_put[:, :], two, 2 * ROWS)

    first_row = area[:, 5400:5528]
    bad_base, bad_edge, bad_count, ones1, top_count = (
        sb(n, [P, 1]) for n in ("bad_base", "bad_edge", "bad_count", "ones1", "top_count"))
    with nc.Block() as block:
        @block.vector
        def _(v):
            vec_done.by(v.memset(first_row, 0.0))
            vec_done.all(v)
            vec_done.by(v.memset(first_row[0:1, :], 1.0))
            v.memset(ones1[:, :], 1.0)
            v.memset(top_count[:, :], -MAXC)

        @block.tensor
        def _(pe):
            vec_done.all(pe)
            pe.matmul(bank[0][:, 0:NU], first_row, dst_f[:, :].rearrange("p (u j) -> p u j", j=UT)[:, :, 0], start=True, stop=True)

    with nc.Block() as block:
        @block.vector
        def _(v):
            dve(v, v.tensor_copy(base[:, :], bank[0][:, 0:NU]))
            dve(v, v.tensor_copy(base_i[:, :], base[0:1, :]))
            same_base = area[:, 0:NU - 1]
            dve(v, v.tensor_tensor(same_base, base[:, 1:NU], base[:, 0:NU - 1], ALU.is_le))
            dve(v, v.tensor_reduce(bad_base[:, :], same_base, X, ALU.max))

    with nc.Block() as block:
        @block.sync
        def _(sp):
            flat = tile_cols(headrow)
            for k in range(TK):
                n = min(P, T - k * P)
                sp_io.by(sp.dma_start(carve(0, (TK,))[0:n, k:k + 1], flat[k * P:k * P + n].rearrange("(r a) -> r a", a=1)), 16)
            sp_io.all(sp)

    nullrow = sb("nullrow", [1, W3])
    with nc.Block() as block:
        @block.vector
        def _(v):
            dve(v, v.tensor_scalar(idx_head[0:TL, TK - 1:TK], carve(0, (TK,))[0:TL, TK - 1:TK], float(N - 1), None, ALU.min))
            dve(v, v.tensor_scalar(idx_head[:, 0:TK - 1], carve(0, (TK,))[:, 0:TK - 1], float(N - 1), None, ALU.min))
            dve(v, v.memset(nullrow[:, 0:D + H], 0.0))
            dve(v, v.memset(nullrow[:, D + H:W3], NEG))

    with nc.Block() as block:
        @block.sync
        def _(sp):
            for w in sums:
                sp_io.by(sp.dma_start(sums[w][ROWS:ROWS + 1, :], nullrow[:, 0:w] if w == W3 else zeros[0:1, 0:w]), 16)
            sp_io.all(sp)

    idx_st = [sb(f"idx_st{u}", [P, G], I32) for u in range(4)]
    at = [0]

    def take(shape, dt=F32):
        n = shape[0] * shape[1]
        v = area[:, at[0]:at[0] + n]
        at[0] += n
        return (v.bitcast(dt) if dt is not F32 else v).rearrange("p (a b) -> p a b", a=shape[0])

    dstrow = [take([G, P], I32) for u in range(2)]
    same = [take([G, P]) for u in range(4)]
    putr = [take([G, D]) for u in range(2)]
    vals = [take([G, W2]) for u in range(2)]
    outs = [take([G, W2]).rearrange("p a b -> p (a b)") for u in range(2)]
    rows32 = [sb(f"rows32_{u}", [G * H, P], I32) for u in range(2)]

    dst_groups = dst_pad.rearrange("(g j) c -> g (j c)", j=G)
    head_groups = dst_heads.rearrange("(g j) c -> g j c", j=G * H)
    put_groups = put.rearrange("(g p j) w -> g p (j w)", p=P, j=G)

    def sums_groups(w):
        return sums[w][0:ROWS, :].rearrange("(g p j) w -> g p (j w)", p=P, j=G)

    TURN = 4

    class Group:

        def __init__(self, i, o):
            self.i, self.o = i, o
            self.n = i * TURN + o

        def slot(self, k):
            return self.o % k

        def turn(self, k):
            return self.i * (TURN // k) + self.o // k

    def done(g):
        return g.n + 1

    def prior(eng, s, n, k):
        n = n.n + 1 - k
        if not (isinstance(n, int) and n <= 0):
            eng.wait_ge(s, n)

    def prior_dma(eng, s, g, k, each=16):
        n = g.turn(k) * each
        if not (isinstance(n, int) and n <= 0):
            eng.wait_ge(s, n)

    LEAD, LAG = 2, 4

    def ticks(eng, step):
        def edge(t):
            def at(lag):
                g = t - lag
                return Group(0, g) if 0 <= g < NG else None
            step(at)
        last = (NG - LEAD) // TURN
        for t in range(-LEAD, 2 * TURN):
            edge(t)
        with eng.Fori(2, last) as i:
            for r in range(TURN):
                step(lambda lag: Group(i, r - lag))
        for t in range(last * TURN, NG + LAG):
            edge(t)

    class Pass:

        def __init__(self, tag, tab, width, w, slots):
            self.tag, self.tab, self.w, self.slots = tag, tab, w, slots
            self.idx_ready, self.begun = self.sem("idx_ready"), sem("begun")
            self.gathered = [self.sem(f"gathered{u}") for u in range(slots)]
            self.rows_in = [self.sem(f"rows_in{u}") for u in range(2)]
            self.put_in = [self.sem(f"put_in{u}") for u in range(2)] if slots == 2 or w == W3 else None
            self.same_ready, self.summed = self.sem("same_ready"), self.sem("summed")
            self.out_ready = self.sem("out_ready")
            self.stored = [self.sem(f"stored{u}") for u in range(2)]
            n = 2 * G * WG // slots
            self.rows = [gath[:, u * n:u * n + G * width].rearrange("p (g w) -> p g w", w=width) for u in range(slots)]
            self.out = [outs[u][:, 0:G * w] for u in range(2)]

        def sem(self, name):
            return sem(f"{self.tag}_{name}")

        def gather(self, pool, used):
            def step(at):
                g = at(0)
                if g is None:
                    return
                pool.wait_ge(self.idx_ready, done(g))
                prior(pool, used, g, self.slots)
                pool.sem_inc(self.begun, 1)
                u = g.slot(self.slots)
                for j in range(G):
                    pool.indirect_dma_start(self.rows[u][:, j, :], None, self.tab,
                                            bass.IndirectOffsetOnAxis(ap=idx_st[g.slot(4)][:, j:j + 1], axis=0)
                                            ).then_inc(self.gathered[u], 16)
            ticks(pool, step)

        def rows_here(self, eng, g):
            eng.wait_ge(self.gathered[g.slot(self.slots)], (g.turn(self.slots) + 1) * (16 * G))

        def load_rows(self, sp, g):
            u = g.slot(2)
            prior(sp, self.same_ready, g, 2)
            sp.dma_start(dstrow[u].rearrange("p g c -> p (g c)"),
                         dst_groups[bass.ds(g.n, 1), :].to_broadcast([P, G * P])).then_inc(self.rows_in[u], 16)

        def load_put(self, sp, g, expanded):
            u = g.slot(2)
            prior(sp, expanded, g, 2)
            sp.dma_start(putr[u].rearrange("p g w -> p (g w)"),
                         put_groups[bass.ds(g.n, 1), :, :].rearrange("a p w -> (a p) w")).then_inc(self.put_in[u], 16)

        def store(self, sp, g):
            u = g.slot(2)
            sp.wait_ge(self.out_ready, done(g))
            sp.dma_start(sums_groups(self.w)[bass.ds(g.n, 1), :, :].rearrange("a p w -> (a p) w"), self.out[u]
                         ).then_inc(self.stored[u], 16)

        def all_stored(self, sp):
            for u in range(2):
                sp.wait_ge(self.stored[u], 16 * (NG // 2))

        def stage_idx(self, v, g):
            if self.slots == 4:
                prior_dma(v, self.gathered[g.slot(4)], g, 4, 16 * G)
            else:
                n = (g.turn(2) - 1) * (16 * G)
                if not (isinstance(n, int) and n <= 0):
                    v.wait_ge(self.gathered[g.slot(2)], n)
            v.tensor_scalar(idx_st[g.slot(4)][:, :], src_i[:, bass.ds(g.n * G, G)], 0.0, None, ALU.add
                            ).then_inc(self.idx_ready, 1)

        def compare(self, v, g):
            v.wait_ge(self.rows_in[g.slot(2)], g.turn(2) * 16 + 16)
            prior(v, self.summed, g, 4)
            v.tensor_tensor(same[g.slot(4)], dstrow[g.slot(2)],
                            dst_f[:, bass.ds(g.n * G, G)].unsqueeze(2).to_broadcast([P, G, P]),
                            ALU.is_equal).then_inc(self.same_ready, 1)

    def plain_pass(tag, tab):
        s = Pass(tag, tab, D, D, 4)
        with nc.Block() as block:
            @block.gpsimd
            def _(pool):
                s.gather(pool, s.summed)

            @block.sync
            def _(sp):
                def step(at):
                    if g := at(-2):
                        s.load_rows(sp, g)
                    if g := at(1):
                        s.store(sp, g)
                ticks(sp, step)
                s.all_stored(sp)

            @block.vector
            def _(v):
                def step(at):
                    if g := at(-2):
                        s.stage_idx(v, g)
                    if g := at(-1):
                        s.compare(v, g)
                ticks(v, step)

            @block.tensor
            def _(pe):
                def step(at):
                    if g := at(0):
                        pe.wait_ge(s.same_ready, done(g))
                        s.rows_here(pe, g)
                        prior(pe, s.out_ready, g, 2)
                        for j in range(G):
                            mm = pe.matmul(bank[g.slot(2)][:, j * D:(j + 1) * D], same[g.slot(4)][:, j, :],
                                           s.rows[g.slot(4)][:, j, :], start=True, stop=True)
                        mm.then_inc(s.summed, 1)
                ticks(pe, step)

            @block.scalar
            def _(act):
                def step(at):
                    if g := at(0):
                        act.wait_ge(s.summed, done(g))
                        prior_dma(act, s.stored[g.slot(2)], g, 2)
                        act.copy(s.out[g.slot(2)], bank[g.slot(2)][:, :]).then_inc(s.out_ready, 1)
                ticks(act, step)

    r_last, r_first = (area[0:NP, i * NB * W2:(i + 1) * NB * W2].rearrange("p (b w) -> p b w", w=W2) for i in range(2))

    def pick(w):
        tmid = carve(0, (TK, w))
        with nc.Block() as block:
            @block.gpsimd
            def _(pool):
                for b in range(NB):
                    for to, idx in ((r_last, idx_last), (r_first, idx_first)):
                        pool_io.by(pool.indirect_dma_start(to[:, b, 0:w], None, sums[w],
                                                           bass.IndirectOffsetOnAxis(ap=idx[:, b:b + 1], axis=0)), 16)
                pool_io.all(pool)

            @block.vector
            def _(v):
                vec_done.by(v.memset(scratch[:, 0:TK * w], 0.0))

            @block.sync
            def _(sp):
                vec_done.all(sp)
                heads = tile_rows(sums[w])
                for k in range(TK):
                    n = min(P, T - k * P) // G
                    sp_io.by(sp.dma_start(tmid[0:n * G, k, :],
                                          heads[k * P // G:k * P // G + n, :, :]), 16)
                sp_io.all(sp)
        return tmid

    def per_bank(w):
        return 512 // w

    straight = (vec_done, sp_io, pool_io)
    branch_counts = {}

    class when:

        def __init__(self, name, flag, value):
            self.name, self.flag, self.value = name, flag, value

        def __enter__(self):
            flag = nc.values_load(self.flag[0:1, 0:1], min_val=0, max_val=1,
                                  skip_runtime_bounds_check_because="0 or 1 by its making")
            self.cond = nc.If(flag == self.value)
            self.cond.__enter__()
            for eng in (nc.sync, nc.gpsimd, nc.tensor, nc.vector, nc.scalar):
                eng.nop()
            self.outer = [(c.sem, c.n) for c in straight]
            if self.name not in branch_counts:
                branch_counts[self.name] = [(sem(f"{self.name}_{what}"), 0) for what in ("vec", "sp", "pool")]
            self.set_counts(branch_counts[self.name])

        def set_counts(self, values):
            for c, (s, n) in zip(straight, values):
                c.sem, c.n = s, n

        def __exit__(self, *a):
            branch_counts[self.name] = [(c.sem, c.n) for c in straight]
            self.set_counts(self.outer)
            return self.cond.__exit__(*a)

    def when_mids(name):
        return when(name, anymid, 1)

    def mids(tag, tm, w):
        to = gath[0:NP, 0:NB * w].rearrange("p (b w) -> p b w", w=w)
        sel_ready, added, kept = (sem(f"{tag}_{n}") for n in ("sel_ready", "added", "kept"))
        sel = carve(2048, (TK, NP))
        mine = carve(2048 + TK * NP, (TK,))
        with nc.Block() as block:
            @block.vector
            def _(v):
                dve(v, v.tensor_copy(mine, midnode[:, :]))
                with v.Fori(0, NB) as b:
                    for k in range(TK):
                        ins = v.tensor_scalar(sel[:, k, :], colnode[:, :], mine[:, k:k + 1], None, ALU.is_equal)
                    ins.then_inc(sel_ready, 1)
                    v.wait_ge(added, b + 1)
                    v.tensor_scalar(to[:, bass.ds(b, 1), :].rearrange("p a w -> p (a w)"), bank[0][0:NP, 0:w], 1.0, None, ALU.mult)
                    v.tensor_scalar(mine, mine, -1.0, None, ALU.add).then_inc(kept, 1)
                    v.wait_ge(kept, b + 1)

            @block.tensor
            def _(pe):
                with pe.Fori(0, NB) as b:
                    pe.wait_ge(sel_ready, b + 1)
                    for k in range(TK):
                        mm = pe.matmul(bank[0][0:NP, 0:w], sel[:, k, :], tm[:, k, :], start=(k == 0), stop=(k == TK - 1))
                    mm.then_inc(added, 1)
        return to

    def by_bank(w):
        n = per_bank(w)
        for c in range(-(-NB // n)):
            m = min(n, NB - c * n)
            yield bank[c][0:NP, 0:m * w].rearrange("p (b w) -> p b w", w=w), c * n, m

    def collect(tag, w):
        tmid = pick(w)
        with when_mids("plain_mids" if w == D else "mids"):
            more = mids(tag, tmid, w)
            with nc.Block() as block:
                @block.vector
                def _(v):
                    v.tensor_tensor(r_first[:, :, 0:w], r_first[:, :, 0:w], more, ALU.add)
        with nc.Block() as block:
            @block.vector
            def _(v):
                dve(v, v.tensor_tensor(r_last[:, :, 0:w], r_last[:, :, 0:w], r_first[:, :, 0:w], ALU.add))
                v.tensor_copy(agg[:, :, :], r_last[:, :, 0:D])

    def turn_nodes(a, to):
        with nc.Block() as block:
            @block.vector
            def _(v):
                v.memset(to[D:D + 1, :], 1.0)

            @block.tensor
            def _(pe):
                for b in range(NB):
                    pe.transpose(bank[b // 4][0:D, (b % 4) * NP:(b % 4 + 1) * NP], a[:, b, :], ident[0:NP, 0:NP])

        with nc.Block() as block:
            @block.vector
            def _(v):
                for c in range(-(-NB // 4)):
                    m = min(4, NB - 4 * c) * NP
                    v.tensor_copy(to[0:D, c * 4 * NP:c * 4 * NP + m], bank[c][0:D, 0:m])

    def project(a, rows, wt, w):
        n = per_bank(w)
        with nc.Block() as block:
            @block.tensor
            def _(pe):
                for b in range(NB):
                    pe.matmul(bank[b // n][0:NP, (b % n) * w:(b % n + 1) * w], a[0:rows, b * NP:(b + 1) * NP], wt,
                              start=True, stop=True)

    st1 = sb("st1", [P, NB])
    st2 = sb("st2", [P, NB])

    def normalize(v, z, wd, tmp):
        shape = [NP, NB, wd]
        dve(v, v.tensor_reduce(st1[0:NP, :], z, X, ALU.add))
        dve(v, v.tensor_scalar(st1[0:NP, :], st1[0:NP, :], 1.0 / wd, None, ALU.mult))
        dve(v, v.tensor_tensor(z, z, st1[0:NP, :].unsqueeze(2).to_broadcast(shape), ALU.subtract))
        dve(v, v.tensor_tensor(tmp, z, z, ALU.mult))
        dve(v, v.tensor_reduce(st2[0:NP, :], tmp, X, ALU.add))
        dve(v, v.tensor_scalar(st2[0:NP, :], st2[0:NP, :], 1.0 / wd, EPS, ALU.mult, ALU.add))

    def layernorm(z, wd, tmp):
        with nc.Block() as block:
            @block.vector
            def _(v):
                normalize(v, z, wd, tmp)

        with nc.Block() as block:
            @block.scalar
            def _(act):
                act.activation(st1[0:NP, :], st2[0:NP, :], ACT.Sqrt)

        with nc.Block() as block:
            @block.vector
            def _(v):
                dve(v, v.reciprocal(st2[0:NP, :], st1[0:NP, :]))
                dve(v, v.tensor_tensor(z, z, st2[0:NP, :].unsqueeze(2).to_broadcast([NP, NB, wd]), ALU.mult))

    tmp64 = area[0:NP, 2 * NB * D:3 * NB * D].rearrange("p (b d) -> p b d", b=NB)

    def to_table(tab, a):
        with nc.Block() as block:
            @block.sync
            def _(sp):
                sp_io.by(sp.dma_start(nodes(tab), a), 16)
                sp_io.all(sp)

    w1s, w2s = sb("w1s", [D + 1, D]), sb("w2s", [D + 1, D])
    wts = {n: sb(f"w_{n}", [D + 1, D]) for n in "qkvo"}
    wraw = {n: sb(f"wraw_{n}", [D, D]) for n in "qkvo"}
    fw = [sb(f"fw{i}", [D, D]) for i in range(3)]
    fb = sb("fb", [D, 3])
    fwo = sb("fwo", [D + 1, 2 * D])
    flwb = sb("flwb", [NP, 2 * D])
    flbb = sb("flbb", [NP, 2 * D])
    aw0 = sb("aw0", [D, D])
    abd = [sb(f"abd{i}", [P, P]) for i in range(3)]
    ab = sb("ab", [P, 3])
    alwb = sb("alwb", [P, D])
    albb = sb("albb", [P, D])
    abob = sb("abob", [P, D])
    tst = sb("tst", [P, 4])

    with nc.Block() as block:
        @block.vector
        def _(v):
            for a in abd:
                v.memset(a[:, :], 0.0)

    def load_weights(sp):
        def load(to, a):
            sp_io.by(sp.dma_start(to, a), 16)

        def row(a):
            return a.rearrange("(a n) -> a n", a=1)

        def col(a):
            return a.rearrange("(n a) -> n a", a=1)

        for to, w, b in ((w1s, W1, b1), (w2s, W2_, b2), (fwo, fWo, fbo)):
            load(to[0:D, :], w)
            load(to[D:D + 1, :], row(b))
        for n, w, b in (("q", Wq, bq), ("k", Wk, bk), ("v", Wv, bv), ("o", Wo, bo)):
            load(wraw[n][:, :], w)
            load(wts[n][D:D + 1, :], row(b))
        for i in range(3):
            load(fw[i][:, :], fWh[i])
            load(fb[:, i:i + 1], col(fbh[i]))
            for c in range(2):
                load(ab[c * D:(c + 1) * D, i:i + 1], col(abh[i]))
        load(flwb[:, :], flw.partition_broadcast(NP))
        load(flbb[:, :], flb.partition_broadcast(NP))
        load(alwb[:, :], alw.partition_broadcast(P))
        load(albb[:, :], alb.partition_broadcast(P))
        load(aw0[:, :], aWh[0])
        load(abob[:, :], abo.partition_broadcast(P))
        for i, w in ((0, aWh[1]), (1, aWh[2]), (2, aWo)):
            for c in range(2):
                load(abd[i][c * D:(c + 1) * D, c * D:(c + 1) * D], w)
        sp_io.all(sp)

    cidx = area[:, 0:T]
    srcp = area[:, T:2 * T]
    o_b = 2 * T
    icols = area[:, o_b:o_b + NB * UL // 2].bitcast(I16)
    o_b += NB * UL // 2
    is_src = [area[:, o_b + i * UT * 64:o_b + (i + 1) * UT * 64].bitcast(BF16).rearrange("p (j c) -> p j c", j=UT)
              for i in range(2)]
    o_b += 2 * UT * 64
    is_col = [area[:, o_b + i * UT * NB * UL // 2:o_b + (i + 1) * UT * NB * UL // 2].bitcast(BF16)
              .rearrange("p (j c) -> p j c", j=UT) for i in range(2)]
    o_b += UT * NB * UL
    unused = [area[0:NP, o_b + i * NB * UL // 2:o_b + (i + 1) * NB * UL // 2].bitcast(BF16) for i in range(2)]
    o_b += NB * UL
    over = area[0:NP, o_b:o_b + NU]
    o_b += NU
    first_col = [area[0:NP, o_b + i * 32:o_b + i * 32 + NB] for i in range(4)]
    o_b += 128
    assert o_b <= at_counts
    t1, t2_, t3 = (mem[:, at_free + i * T:at_free + (i + 1) * T] for i in range(3))
    ti = mem[:, at_free + 3 * T:at_free + 4 * T].bitcast(I32)
    with nc.Block() as block:
        @block.gpsimd
        def _(pool):
            pool.iota(icols, [[1, NB * UL]], base=0, channel_multiplier=0)
            pool.memset(counts_flat, 0.0)

        @block.vector
        def _(v):
            dve(v, v.tensor_copy(t2_, src_i[:, :]))
            dve(v, v.tensor_scalar(t1, t2_, 1.0 / NB, None, ALU.mult))
            dve(v, v.tensor_copy(ti, t1))
            dve(v, v.tensor_copy(srcp, ti))
            dve(v, v.scalar_tensor_tensor(out=t1, in0=srcp, scalar=float(-NB), in1=t2_, op0=ALU.mult, op1=ALU.add))
            for op, bound, by in ((ALU.is_lt, 0.0, 1.0), (ALU.is_ge, float(NB), -1.0)):
                dve(v, v.tensor_scalar(t2_, t1, bound, None, op))
                dve(v, v.scalar_tensor_tensor(out=srcp, in0=t2_, scalar=-by, in1=srcp, op0=ALU.mult, op1=ALU.add))
                dve(v, v.scalar_tensor_tensor(out=t1, in0=t2_, scalar=NB * by, in1=t1, op0=ALU.mult, op1=ALU.add))
            dve(v, v.tensor_tensor(t2_.rearrange("p (u j) -> p u j", j=UT), dst_f[:, :].rearrange("p (u j) -> p u j", j=UT),
                                   base[:, :].unsqueeze(2).to_broadcast([P, NU, UT]), ALU.subtract))
            dve(v, v.scalar_tensor_tensor(out=cidx, in0=t1, scalar=float(UL), in1=t2_, op0=ALU.mult, op1=ALU.add))
            dve(v, v.tensor_scalar(t3, t2_, float(UL), None, ALU.is_ge))
            dve(v, v.tensor_scalar(t1, t2_, 0.0, None, ALU.is_lt))
            dve(v, v.tensor_tensor(t3, t3, t1, ALU.max))
            dve(v, v.tensor_scalar(t1, dst_f[:, :], float(N), None, ALU.is_lt))
            dve(v, v.tensor_tensor(t2_, t3, t1, ALU.mult))
            dve(v, v.tensor_reduce(bad_edge[:, :], t2_, X, ALU.max))
            dve(v, v.tensor_tensor(t1, t1, t2_, ALU.subtract))
            dve(v, v.tensor_scalar(cidx, cidx, 1.0, None, ALU.add))
            dve(v, v.tensor_tensor(cidx, cidx, t1, ALU.mult))
            dve(v, v.tensor_scalar(cidx, cidx, -1.0, None, ALU.add))

    def bases(engine, turn):
        return nc.values_load_multi_w_load_instructions(
            base_i[0:1, bass.ds(turn * TURN, TURN)], engines=(engine,), min_val=0, max_val=N - 1,
            skip_runtime_bounds_check_because="nodes of the graph by the edges' making")[1]

    def units(eng, step, begin=lambda turn: None):
        begin(0)
        for o in range(TURN):
            step(Group(0, o))
        with eng.Fori(1, NU // TURN) as i:
            begin(i)
            for o in range(TURN):
                step(Group(i, o))

    spread, counted, kept_u, added_u = sem("spread"), sem("counted"), sem("kept_u"), sem("added_u")
    with nc.Block() as block:
        @block.vector
        def _(v):
            firsts = []

            def begin(turn):
                if not (isinstance(turn, int) and turn == 0):
                    firsts[:] = bases(mybir.EngineType.DVE, turn - 1)

            def add_first(n, o):
                v.wait_ge(kept_u, n + 1)
                if not (isinstance(n, int) and n == 0):
                    v.wait_ge(added_u, n)
                col = counts[:, :, bass.ds(firsts[o], 1)].rearrange("p a n -> p (a n)")
                v.tensor_tensor(col, col, first_col[o], ALU.add).then_inc(added_u, 1)

            def step(u):
                if firsts:
                    add_first((u.i - 1) * TURN + u.o, u.o)
                prior(v, counted, u, 2)
                for j in range(UT):
                    c = bass.ds(u.n * UT + j, 1)
                    v.tensor_scalar(is_src[u.slot(2)][:, j, :], icols[:, 0:P], srcp[:, c], None, ALU.is_equal)
                    ins = v.tensor_scalar(is_col[u.slot(2)][:, j, :], icols, cidx[:, c], None, ALU.is_equal)
                ins.then_inc(spread, 1)
            units(v, step, begin)
            begin(NU // TURN)
            for o in range(TURN):
                add_first(NU - TURN + o, o)

        @block.tensor
        def _(pe):
            def step(u):
                pe.wait_ge(spread, done(u))
                prior(pe, kept_u, u, 4)
                for j in range(UT):
                    mm = pe.matmul(bank[u.slot(4)][0:NP, 0:NB * UL], is_src[u.slot(2)][:, j, 0:NP],
                                   is_col[u.slot(2)][:, j, :], start=(j == 0), stop=(j == UT - 1))
                mm.then_inc(counted, 1)
            units(pe, step)

        @block.sync
        def _(sp):
            load_weights(sp)

        @block.scalar
        def _(act):
            firsts = []

            def step(u):
                first = firsts[u.o]
                act.wait_ge(counted, done(u))
                prior(act, kept_u, u, 1)
                prior(act, added_u, u, 4)
                c = bank[u.slot(4)][0:NP, 0:NB * UL]
                per_dst = c.rearrange("p (a l) -> p a l", l=UL)
                act.activation(counts[:, :, bass.ds(first + 1, UL - 1)], per_dst[:, :, 1:UL], ACT.Relu)
                act.activation(first_col[u.slot(4)], per_dst[:, :, 0], ACT.Relu)
                act.activation(unused[u.slot(2)], c, ACT.Relu, bias=top_count[0:NP, :], accum_out=over[:, bass.ds(u.n, 1)]
                               ).then_inc(kept_u, 1)
            def begin(turn):
                firsts[:] = bases(mybir.EngineType.Activation, turn)

            units(act, step, begin)

    with nc.Block() as block:
        @block.vector
        def _(v):
            dve(v, v.tensor_reduce(bad_count[0:NP, :], over, X, ALU.max))
            dve(v, v.tensor_tensor(bad_edge[0:NP, :], bad_edge[0:NP, :], bad_count[0:NP, :], ALU.add))
            dve(v, v.tensor_tensor(bad_edge[:, :], bad_edge[:, :], bad_base[:, :], ALU.add))

    with nc.Block() as block:
        @block.tensor
        def _(pe):
            pe.matmul(bank[0][0:1, 0:1], bad_edge[:, :], ones1[:, :], start=True, stop=True)

    with nc.Block() as block:
        @block.vector
        def _(v):
            dve(v, v.tensor_scalar(bad_count[0:1, :], bank[0][0:1, 0:1], 0.0, None, ALU.is_le))
            dve(v, v.tensor_copy(usable[:, :], bad_count[0:1, :]))

    with nc.Block() as block:
        @block.vector
        def _(v):
            dve(v, v.tensor_scalar(aw0[:, :], aw0[:, :], 0.5, None, ALU.mult))
            for c in range(2):
                a = abd[2][c * D:(c + 1) * D, c * D:(c + 1) * D]
                t = tst[c * D:(c + 1) * D, 0:1]
                dve(v, v.tensor_reduce(t, a, X, ALU.add))
                dve(v, v.tensor_scalar(t, t, 1.0 / D, None, ALU.mult))
                dve(v, v.tensor_scalar(a, a, t, None, ALU.subtract))
            t = tst[:, 1:2]
            dve(v, v.tensor_reduce(t, abob[:, :], X, ALU.add))
            dve(v, v.tensor_scalar(t, t, 1.0 / D, None, ALU.mult))
            dve(v, v.tensor_scalar(abob[:, :], abob[:, :], t, None, ALU.subtract))
            dve(v, v.tensor_scalar(alwb[:, :], alwb[:, :], -0.5, None, ALU.mult))
            dve(v, v.tensor_scalar(albb[:, :], albb[:, :], -0.5, None, ALU.mult))
            dve(v, v.tensor_scalar(flwb[:, :], flwb[:, :], 0.5, None, ALU.mult))
            dve(v, v.tensor_scalar(flbb[:, :], flbb[:, :], 0.5, None, ALU.mult))

        @block.tensor
        def _(pe):
            for c, n in enumerate("qkvo"):
                pe.transpose(bank[0][0:D, c * D:(c + 1) * D], wraw[n][:, :], ident[0:D, 0:D])

    with nc.Block() as block:
        @block.vector
        def _(v):
            for c, n in enumerate("qkvo"):
                dve(v, v.tensor_copy(wts[n][0:D, :], bank[0][0:D, c * D:(c + 1) * D]))
            dve(v, v.tensor_scalar(wts["q"][:, :], wts["q"][:, :], HD ** -0.5, None, ALU.mult))

    wide = [mem[0:NP, i * WIDE:(i + 1) * WIDE].bitcast(BF16).rearrange("p (a c) -> p a c", a=UA)
            for i in range(2 * UK)]
    rest_x = mem[0:NP, 0:NB * D].rearrange("p (b d) -> p b d", b=NB)
    by_block = counts[:, :, 0:N].rearrange("p a (n b) -> p a n b", b=NB)
    dense_passes = [0]

    def dense_pass(h):
        with nc.Block() as block:
            @block.vector
            def _(v):
                dve(v, v.tensor_copy(xb[:, :, 0:D], h))
                dve(v, v.tensor_tensor(rest_x, h, xb[:, :, 0:D], ALU.subtract))
                dve(v, v.tensor_copy(xb[:, :, D:2 * D], rest_x))
                dve(v, v.tensor_tensor(rest_x, rest_x, xb[:, :, D:2 * D], ALU.subtract))
                dve(v, v.tensor_copy(xb[:, :, 2 * D:3 * D], rest_x))

        chunk_done, chunk_out, act_wide, vec_wide = (sem(n) for n in ("chunk_done", "chunk_out", "act_wide", "vec_wide"))
        for_act, for_vec = range(0, UK, 2), range(1, UK, 2)
        before = dense_passes[0] * NB
        dense_passes[0] += 1
        with nc.Block() as block:
            def chunks(eng, step):
                for c in range(2):
                    step(Chunk(0, c))
                with eng.Fori(1, NB // 2) as i:
                    for o in range(2):
                        step(Chunk(i, o))
                for c in range(NB // 2 * 2, NB):
                    step(Chunk(0, c))

            class Chunk:

                def __init__(self, i, o):
                    self.i, self.o, self.slot = i, o, o % 2

                def times(self, n, k):
                    return self.i * (2 * n) + ((before + self.o) * n + k)

                def old(self, eng, s):
                    if isinstance(self.i, int) and self.o < 2:
                        return
                    eng.wait_ge(s, self.times(1, -1))

            def widen(eng, chunk, parts_, op, s):
                chunk.old(eng, chunk_done)
                for k in parts_:
                    op(wide[chunk.slot * UK + k][:, :, 0:NP],
                       by_block[:, k * UA:(k + 1) * UA, :, bass.ds(chunk.i * 2 + chunk.o, 1)].rearrange("p a n b -> p a (n b)")
                       ).then_inc(s, 1)

            @block.tensor
            def _(pe):
                def chunk(c):
                    c.old(pe, chunk_out)
                    for k in range(UK):
                        mine, s = (for_act, act_wide) if k in for_act else (for_vec, vec_wide)
                        pe.wait_ge(s, c.times(len(mine), mine.index(k) + 1))
                        for a in range(UA):
                            mm = pe.matmul(bank[c.slot][0:NP, 0:3 * D], wide[c.slot * UK + k][:, a, 0:NP], xb[:, k * UA + a, :],
                                           start=(k == a == 0), stop=(k == UK - 1 and a == UA - 1))
                    mm.then_inc(chunk_done, 1)
                chunks(pe, chunk)

            @block.scalar
            def _(act):
                chunks(act, lambda c: widen(act, c, for_act, lambda to, a: act.activation(to, a, ACT.Relu), act_wide))

            @block.vector
            def _(v):
                def total(c):
                    v.wait_ge(chunk_done, c.times(1, 1))
                    v.tensor_reduce(agg[:, bass.ds(c.i * 2 + c.o, 1), :].rearrange("p c d -> p (c d)"),
                                    bank[c.slot][0:NP, 0:3 * D].rearrange("p (k d) -> p d k", k=3), X, ALU.add
                                    ).then_inc(chunk_out, 1)

                def widen_v(c):
                    widen(v, c, for_vec, lambda to, a: v.tensor_scalar(to, a, 0.0, None, ALU.add), vec_wide)

                widen_v(Chunk(0, 0))
                widen_v(Chunk(0, 1))
                total(Chunk(0, 0))
                with v.Fori(1, NB // 2) as i:
                    widen_v(Chunk(i, 0))
                    total(Chunk(i, -1))
                    widen_v(Chunk(i, 1))
                    total(Chunk(i, 0))
                last = NB // 2 * 2 - 1
                for c in range(last + 1, NB):
                    widen_v(Chunk(0, c))
                    total(Chunk(0, c - 1))
                total(Chunk(0, NB - 1))

    def aggregate(tag, tab, h):
        with when("counts", usable, 1):
            dense_pass(h)
        with when("plain", usable, 0):
            if tab is table:
                to_table(tab, h)
            plain_pass(tag, tab)
            collect(tag, D)

    def gin(source, h, weights):
        aggregate(source[0], source[1], h)
        with nc.Block() as block:
            @block.vector
            def _(v):
                v.tensor_tensor(agg[:, :, :], agg[:, :, :], h, ALU.add)
        turn_nodes(agg, featT)
        project(featT, D + 1, weights[:, :], D)
        with nc.Block() as block:
            @block.scalar
            def _(act):
                for view, b, m in by_bank(D):
                    act.activation(hid[:, b:b + m, :], view, ACT.Relu)

    def residual(a):
        with nc.Block() as block:
            @block.vector
            def _(v):
                v.tensor_tensor(xs[:, :, :], xs[:, :, :], a, ALU.add)
        layernorm(xs[:, :, :], D, tmp64)

    gin(("p0a", x), xs[:, :, :], w1s)
    gin(("p0b", table), hid[:, :, :], w2s)
    residual(hid[:, :, :])

    aggregate("p1a", table, xs[:, :, :])
    with nc.Block() as block:
        @block.vector
        def _(v):
            v.tensor_scalar(hid[:, :, :], agg[:, :, :], 0.0, None, ALU.max)
    aggregate("p1b", table, hid[:, :, :])
    residual(agg[:, :, :])

    flux = scratch[0:NP, 0:NB * 2 * D].rearrange("p (b w) -> p b w", w=2 * D)
    fsq = scratch[0:NP, NB * 2 * D:2 * NB * 2 * D].rearrange("p (b w) -> p b w", w=2 * D)
    turn_nodes(xs, featT)
    project(featT, D, aw0[:, :], D)
    with nc.Block() as block:
        @block.vector
        def _(v):
            for view, b, m in by_bank(D):
                v.tensor_copy(hid[:, b:b + m, :], view)
            v.tensor_tensor(tab[:, :, 0:D], xs[:, :, :], alwb[0:NP, :].unsqueeze(1).to_broadcast([NP, NB, D]), ALU.mult)
            v.tensor_tensor(tab[:, :, D:2 * D], xs[:, :, :], albb[0:NP, :].unsqueeze(1).to_broadcast([NP, NB, D]), ALU.mult)
            v.memset(hidT[D:D + 1, :], 1.0)
    CH = 4 * NP
    for layer in range(3):
        ins_, to = (featT, hidT) if layer % 2 == 0 else (hidT, featT)
        with nc.Block() as block:
            @block.tensor
            def _(pe):
                for c in range(-(-NB // 4)):
                    m = min(CH, NB * NP - c * CH)
                    pe.matmul(bank[c][0:D, 0:m], fw[layer][:, :], ins_[0:D, c * CH:c * CH + m], start=True, stop=True)

        with nc.Block() as block:
            @block.scalar
            def _(act):
                for c in range(-(-NB // 4)):
                    m = min(CH, NB * NP - c * CH)
                    act.activation(to[0:D, c * CH:c * CH + m], bank[c][0:D, 0:m], ACT.Relu, bias=fb[:, layer:layer + 1])
    project(hidT, D + 1, fwo[:, :], 2 * D)
    with nc.Block() as block:
        @block.vector
        def _(v):
            for view, b, m in by_bank(2 * D):
                v.tensor_copy(flux[:, b:b + m, :], view)
    layernorm(flux, 2 * D, fsq)
    with nc.Block() as block:
        @block.vector
        def _(v):
            shape = [NP, NB, 2 * D]
            dve(v, v.tensor_tensor(flux, flux, flwb[:, :].unsqueeze(1).to_broadcast(shape), ALU.mult))
            dve(v, v.tensor_tensor(flux, flux, flbb[:, :].unsqueeze(1).to_broadcast(shape), ALU.add))

    def publish(srcs, a, headtab):
        heads = gath[:, 0:TK * D].rearrange("p (k w) -> p k w", w=D)
        with nc.Block() as block:
            @block.sync
            def _(sp):
                for to, s_ in srcs:
                    sp_io.by(sp.dma_start(to, s_), 16)
                sp_io.all(sp)

            @block.gpsimd
            def _(pool):
                pool.wait_ge(put_zero, 16 * (ROWS // (P * PA)))
                for b in range(NB):
                    pool_io.by(pool.indirect_dma_start(put, bass.IndirectOffsetOnAxis(ap=idx_put[:, b:b + 1], axis=0),
                                                       a[:, b, :], None, bounds_check=ROWS - 1, oob_is_err=False), 16)
                pool_io.all(pool)

        with nc.Block() as block:
            @block.gpsimd
            def _(pool):
                for k in range(TK):
                    n = min(P, T - k * P)
                    pool_io.by(pool.indirect_dma_start(heads[0:n, k, :], None, headtab,
                                                       bass.IndirectOffsetOnAxis(ap=idx_head[0:n, k:k + 1], axis=0)), 16)
                pool_io.all(pool)

        with nc.Block() as block:
            @block.sync
            def _(sp):
                rows = tile_rows(put)
                for k in range(TK):
                    n = min(P, T - k * P) // G
                    sp_io.by(sp.dma_start(rows[k * P // G:k * P // G + n, :, :], heads[0:n * G, k, :]), 16)
                sp_io.all(sp)

    t2 = nodes(table2)
    publish([(t2[:, :, 0:D], hid[:, :, :]), (t2[:, :, D:2 * D], tab[:, :, 0:D]), (t2[:, :, 2 * D:4 * D], flux),
             (t2[:, :, 4 * D:WG], tab[:, :, D:2 * D]), (nodes(table), hid[:, :, :])], hid, table)
    with nc.Block() as block:
        @block.vector
        def _(v):
            v.tensor_copy(fx[:, :, :], flux)

    def flux_pass():
        s = Pass("p2", table2, WG, W2, 2)
        names = ("expanded z_ready turned h1 m1 h2 m2 h3 y yb_ready squared var1 var_ready root rstd_ready t_ready "
                 "u_ready v_ready f1 f_ready wx_ready")
        (expanded, z_ready, turned, h1, m1, h2, m2, h3, y, yb_ready, squared, var1, var_ready, root, rstd_ready, t_ready,
         u_ready, v_ready, f1, f_ready, wx_ready) = (s.sem(n) for n in names.split())
        zb, ft = carve(0, (G, D)), carve(512, (G, D, 2))
        fl = [carve(1536 + 512 * u, (G, D)) for u in range(4)]
        wxb = [carve(3584 + 512 * u, (G, D)) for u in range(4)]
        h1b, h2b, h3b, sq, ub = (carve(5632 + 512 * k, (512,)) for k in range(5))
        ysb = [carve(8192 + 512 * u, (G, D)) for u in range(2)]
        var, sd, rstd = (carve(9300 + 8 * k, (G,)) for k in range(3))
        wd = [P, G, D]
        lanes = ((5, 0, 3), (6, 3, 6), (7, 6, 8))

        def per_tile(a):
            return a.rearrange("p (g d) -> p g d", g=G)

        with nc.Block() as block:
            @block.gpsimd
            def _(pool):
                s.gather(pool, f_ready)

            @block.sync
            def _(sp):
                def step(at):
                    if g := at(-2):
                        s.load_rows(sp, g)
                    if g := at(-1):
                        s.load_put(sp, g, expanded)
                    if g := at(4):
                        s.store(sp, g)
                ticks(sp, step)
                s.all_stored(sp)

            @block.vector
            def _(v):
                def rstd_of(g):
                    v.wait_ge(root, done(g))
                    prior(v, t_ready, g, 1)
                    v.reciprocal(rstd, sd).then_inc(rstd_ready, 1)

                def weigh(g):
                    out = vals[g.slot(2)]
                    v.wait_ge(rstd_ready, done(g))
                    prior(v, s.summed, g, 2)
                    v.tensor_scalar(out[:, :, 2 * D:W2], nvec[:, bass.ds(g.n * G, G), :], 1.0, None, ALU.mult)
                    v.tensor_tensor(out[:, :, D:2 * D], ysb[g.slot(2)], rstd.unsqueeze(2).to_broadcast(wd), ALU.mult
                                    ).then_inc(t_ready, 1)
                    v.wait_ge(t_ready, done(g))
                    v.wait_ge(wx_ready, done(g))
                    v.tensor_tensor(per_tile(ub), out[:, :, D:2 * D], wxb[g.slot(4)], ALU.mult).then_inc(u_ready, 1)
                    v.wait_ge(u_ready, done(g))
                    v.wait_ge(f_ready, done(g))
                    v.tensor_tensor(out[:, :, 0:D], per_tile(ub), fl[g.slot(4)], ALU.add).then_inc(v_ready, 1)

                def sum_first(g):
                    s.rows_here(v, g)
                    v.wait_ge(expanded, done(g))
                    prior(v, turned, g, 1)
                    v.tensor_tensor(zb, per_tile(bank[0][:, :]), s.rows[g.slot(2)][:, :, 0:D], ALU.add).then_inc(z_ready, 1)

                def biased(g):
                    v.wait_ge(y, done(g))
                    prior(v, t_ready, g, 2)
                    prior(v, squared, g, 2)
                    v.tensor_tensor(ysb[g.slot(2)], per_tile(bank[4][:, :]), abob[:, :].unsqueeze(1).to_broadcast(wd), ALU.add
                                    ).then_inc(yb_ready, 1)

                def flux_part(g):
                    r = s.rows[g.slot(2)]
                    prior(v, f_ready, g, 1)
                    v.tensor_tensor(ft, r[:, :, 2 * D:4 * D].rearrange("p g (c d) -> p g c d", d=2),
                                    nvec[:, bass.ds(g.n * G, G), :].unsqueeze(2).to_broadcast([P, G, D, 2]),
                                    ALU.mult).then_inc(f1, 1)
                    v.wait_ge(f1, done(g))
                    prior(v, v_ready, g, 4)
                    v.tensor_tensor(fl[g.slot(4)], ft[:, :, :, 0], ft[:, :, :, 1], ALU.add).then_inc(f_red, 1)
                    v.wait_ge(f_red, done(g))
                    v.wait_ge(wx_ready, done(g))
                    v.tensor_tensor(fl[g.slot(4)], fl[g.slot(4)], r[:, :, 4 * D:WG], ALU.add).then_inc(f_ready, 1)

                def variance(g):
                    v.wait_ge(squared, done(g))
                    prior(v, root, g, 1)
                    v.tensor_reduce(var, per_tile(sq), X, ALU.add).then_inc(var1, 1)
                    v.wait_ge(var1, done(g))
                    v.tensor_scalar(var, var, 1.0 / D, EPS, ALU.mult, ALU.add).then_inc(var_ready, 1)

                f_red = s.sem("f_red")

                def step(at):
                    if g := at(3):
                        rstd_of(g)
                        weigh(g)
                    if g := at(-2):
                        s.stage_idx(v, g)
                    if g := at(2):
                        biased(g)
                    if g := at(0):
                        sum_first(g)
                        flux_part(g)
                    if g := at(2):
                        variance(g)
                    if g := at(-1):
                        s.compare(v, g)
                ticks(v, step)

            @block.tensor
            def _(pe):
                def expand(g):
                    pe.wait_ge(s.same_ready, done(g))
                    pe.wait_ge(s.put_in[g.slot(2)], g.turn(2) * 16 + 16)
                    prior(pe, z_ready, g, 1)
                    for j in range(G):
                        mm = pe.matmul(bank[0][:, j * D:(j + 1) * D], same[g.slot(4)][:, j, :], putr[g.slot(2)][:, j, :],
                                       start=True, stop=True)
                    mm.then_inc(expanded, 1)

                def turn_z(g):
                    pe.wait_ge(z_ready, done(g))
                    prior(pe, h1, g, 1)
                    for j in range(4):
                        mm = pe.transpose(bank[1][:, j * P:(j + 1) * P],
                                          zb[:, 2 * j:2 * j + 2, :].rearrange("p a d -> p (a d)"), ident[:, :])
                    mm.then_inc(turned, 1)

                def hidden(g, i, ready, used, out):
                    pe.wait_ge(ready, done(g))
                    prior(pe, used, g, 1)
                    pe.matmul(bank[2 + i][:, :], abd[i][:, :], (h1b, h2b)[i], start=True, stop=True).then_inc(out, 1)

                def last(g):
                    pe.wait_ge(h3, done(g))
                    prior(pe, yb_ready, g, 1)
                    for j in range(4):
                        mm = pe.matmul(bank[4][:, j * P:(j + 1) * P], h3b[:, j * P:(j + 1) * P], abd[2][:, :],
                                       start=True, stop=True)
                    mm.then_inc(y, 1)

                def sums_of(g):
                    pe.wait_ge(v_ready, done(g))
                    prior(pe, s.out_ready, g, 1)
                    for c, a, b in lanes:
                        for j in range(a, b):
                            mm = pe.matmul(bank[c][:, (j - a) * W2:(j - a + 1) * W2], same[g.slot(4)][:, j, :],
                                           vals[g.slot(2)][:, j, :], start=True, stop=True)
                    mm.then_inc(s.summed, 1)

                def step(at):
                    if g := at(1):
                        hidden(g, 0, h1, h2, m1)
                    if g := at(0):
                        expand(g)
                    if g := at(1):
                        hidden(g, 1, h2, h3, m2)
                    if g := at(0):
                        turn_z(g)
                    if g := at(3):
                        sums_of(g)
                    if g := at(1):
                        last(g)
                ticks(pe, step)

            @block.scalar
            def _(act):
                def relu(g, i, src_bank, to, ready, used, out):
                    act.wait_ge(ready, done(g))
                    prior(act, used, g, 1)
                    act.activation(to, bank[src_bank][:, :], ACT.Relu, bias=ab[:, i:i + 1]).then_inc(out, 1)

                def square(g):
                    act.wait_ge(yb_ready, done(g))
                    prior(act, var1, g, 1)
                    act.activation(sq, ysb[g.slot(2)].rearrange("p g d -> p (g d)"), ACT.Square).then_inc(squared, 1)

                def keep_wx(g):
                    s.rows_here(act, g)
                    prior(act, u_ready, g, 4)
                    act.copy(wxb[g.slot(4)], s.rows[g.slot(2)][:, :, D:2 * D]).then_inc(wx_ready, 1)

                def sqrt(g):
                    act.wait_ge(var_ready, done(g))
                    prior(act, rstd_ready, g, 1)
                    act.activation(sd, var, ACT.Sqrt).then_inc(root, 1)

                def evict(g):
                    act.wait_ge(s.summed, done(g))
                    prior_dma(act, s.stored[g.slot(2)], g, 2)
                    for c, a, b in lanes:
                        ins = act.copy(s.out[g.slot(2)][:, a * W2:b * W2], bank[c][:, 0:(b - a) * W2])
                    ins.then_inc(s.out_ready, 1)

                def step(at):
                    if g := at(1):
                        relu(g, 1, 2, h2b, m1, m2, h2)
                    if g := at(2):
                        square(g)
                    if g := at(0):
                        keep_wx(g)
                    if g := at(1):
                        relu(g, 2, 3, h3b, m2, y, h3)
                    if g := at(0):
                        relu(g, 0, 1, h1b, turned, m1, h1)
                    if g := at(2):
                        sqrt(g)
                    if g := at(3):
                        evict(g)
                ticks(act, step)

    flux_pass()
    collect("p2", W2)
    with nc.Block() as block:
        @block.vector
        def _(v):
            wide = [NP, NB, D]
            nv = r_last[:, :, 2 * D:W2].unsqueeze(2).to_broadcast([NP, NB, D, 2])
            f4 = fx[:, :, :].rearrange("p b (c d) -> p b c d", d=2)
            dve(v, v.tensor_tensor(f4, f4, nv, ALU.mult))
            dve(v, v.tensor_reduce(hid[:, :, :], f4, X, ALU.add))
            dve(v, v.tensor_tensor(agg[:, :, :], agg[:, :, :], hid[:, :, :], ALU.add))
            t = r_last[:, :, D:2 * D]
            dve(v, v.tensor_tensor(t, t, tab[:, :, 0:D], ALU.mult))
            dve(v, v.tensor_tensor(hid[:, :, :], tab[:, :, D:2 * D], deg[:, :].unsqueeze(2).to_broadcast(wide), ALU.mult))
            dve(v, v.tensor_tensor(t, t, hid[:, :, :], ALU.add))
            dve(v, v.tensor_tensor(agg[:, :, :], agg[:, :, :], t, ALU.subtract))
            dve(v, v.tensor_tensor(agg[:, :, :], agg[:, :, :], xs[:, :, :], ALU.add))
    residual(agg[:, :, :])

    turn_nodes(xs, featT)
    qs = hid[:, :, :]
    for n, to in (("k", tab[:, :, 0:D]), ("v", tab[:, :, D:2 * D]), ("q", qs)):
        project(featT, D + 1, wts[n][:, :], D)
        with nc.Block() as block:
            @block.vector
            def _(v):
                for view, b, m in by_bank(D):
                    v.tensor_copy(to[:, b:b + m, :], view)
    kv = dram("kv", [N, 2 * D])
    publish([(nodes(kv), tab[:, :, :]), (nodes(table), qs)], qs, table)

    def reverse(ap_tensor, rows, n):
        a = ap_tensor
        return bass.AP(tensor=a.tensor, offset=a.offset + n - 1, ap=[list(a.ap[0]), [-1, n]])

    def attention_pass():
        s = Pass("p3", kv, 2 * D, W3, 4)
        names = "expanded qk reduced scored turned f1 flagged scanned mx back dif_ready e_ready v_ready"
        expanded, qk, reduced, scored, turned, f1, flagged, scanned, mx, back, dif_ready, e_ready, v_ready = (
            s.sem(n) for n in names.split())
        heads_in = [s.sem(f"heads_in{u}") for u in range(2)]
        GH = G * H
        prod = carve(0, (G, D))
        sc = [carve(512 + 32 * u, (GH,)) for u in range(4)]
        mb = [carve(640 + 32 * u, (GH,)) for u in range(4)]
        dif = carve(800, (GH,))
        flags = carve(1024, (2 * P,), parts=GH)
        run_f, run_b, smax = (carve(1280 + P * k, (P,), parts=GH) for k in range(3))
        vals3 = [vals[u].rearrange("p g w -> p (g w)")[:, 0:G * (D + H)].rearrange("p (g w) -> p g w", w=D + H)
                 for u in range(2)]
        lanes = ((4, 0, 4), (5, 4, 8))

        with nc.Block() as block:
            @block.gpsimd
            def _(pool):
                s.gather(pool, v_ready)

            @block.sync
            def _(sp):
                def step(at):
                    if g := at(-2):
                        s.load_rows(sp, g)
                    if g := at(-1):
                        s.load_put(sp, g, expanded)
                    if g := at(0):
                        prior(sp, f1, g, 2)
                        sp.dma_start(rows32[g.slot(2)][:, :],
                                     head_groups[bass.ds(g.n, 1), :, :].rearrange("a j c -> (a j) c")
                                     ).then_inc(heads_in[g.slot(2)], 16)
                    if g := at(4):
                        s.store(sp, g)
                ticks(sp, step)
                s.all_stored(sp)

            @block.vector
            def _(v):
                vec_done.by(v.memset(flags, 0.0))
                vec_done.all(v)

                def score(g):
                    s.rows_here(v, g)
                    v.wait_ge(expanded, done(g))
                    prior(v, reduced, g, 1)
                    v.tensor_tensor(prod, bank[0][:, :].rearrange("p (g d) -> p g d", g=G), s.rows[g.slot(4)][:, :, 0:D],
                                    ALU.mult).then_inc(qk, 1)
                    v.wait_ge(qk, done(g))
                    prior(v, dif_ready, g, 4)
                    a = sc[g.slot(4)]
                    v.tensor_reduce(a, prod.rearrange("p g (h d) -> p (g h) d", h=H), X, ALU.add).then_inc(reduced, 1)
                    v.wait_ge(reduced, done(g))
                    a = a.rearrange("p (g h) -> p g h", h=H)
                    v.tensor_tensor(a, a, ebias[:, bass.ds(g.n * G, G), :], ALU.add).then_inc(scored, 1)

                def flag(g):
                    r = rows32[g.slot(2)]
                    v.wait_ge(heads_in[g.slot(2)], g.turn(2) * 16 + 16)
                    prior(v, scanned, g, 1)
                    v.tensor_tensor(flags[:, 1:P], r[:, 1:P], r[:, 0:P - 1], ALU.not_equal).then_inc(f1, 1)
                    v.wait_ge(f1, done(g))
                    v.tensor_scalar(flags[:, 1:P], flags[:, 1:P], NEG, None, ALU.mult).then_inc(flagged, 1)

                def scan(g):
                    v.wait_ge(flagged, done(g))
                    v.wait_ge(turned, done(g))
                    prior(v, mx, g, 1)
                    t = bank[2][0:GH, 0:P]
                    v.tensor_tensor_scan(run_f, flags[:, 0:P], t, NEG, ALU.add, ALU.max)
                    v.tensor_tensor_scan(reverse(run_b, GH, P), reverse(flags[:, 1:P + 1], GH, P), reverse(t, GH, P),
                                         NEG, ALU.add, ALU.max).then_inc(scanned, 1)
                    v.wait_ge(scanned, done(g))
                    prior(v, back, g, 1)
                    v.tensor_tensor(smax, run_f, run_b, ALU.max).then_inc(mx, 1)

                def differ(g):
                    v.wait_ge(back, done(g))
                    prior(v, e_ready, g, 1)
                    prior(v, s.out_ready, g, 4)
                    v.tensor_copy(mb[g.slot(4)], bank[3][:, 0:GH])
                    v.tensor_tensor(dif, sc[g.slot(4)], bank[3][:, 0:GH], ALU.subtract).then_inc(dif_ready, 1)

                def weigh(g):
                    v.wait_ge(e_ready, done(g))
                    out = vals3[g.slot(2)]
                    v.tensor_tensor(out[:, :, 0:D].rearrange("p g (h d) -> p g h d", h=H),
                                    s.rows[g.slot(4)][:, :, D:2 * D].rearrange("p g (h d) -> p g h d", h=H),
                                    out[:, :, D:D + H].unsqueeze(3).to_broadcast([P, G, H, HD]), ALU.mult
                                    ).then_inc(v_ready, 1)

                def step(at):
                    if g := at(-2):
                        s.stage_idx(v, g)
                    if g := at(2):
                        differ(g)
                    if g := at(1):
                        flag(g)
                    if g := at(2):
                        weigh(g)
                    if g := at(-1):
                        s.compare(v, g)
                    if g := at(1):
                        scan(g)
                    if g := at(0):
                        score(g)
                ticks(v, step)

            @block.tensor
            def _(pe):
                def expand(g):
                    pe.wait_ge(s.same_ready, done(g))
                    pe.wait_ge(s.put_in[g.slot(2)], g.turn(2) * 16 + 16)
                    prior(pe, qk, g, 1)
                    for j in range(G):
                        mm = pe.matmul(bank[0][:, j * D:(j + 1) * D], same[g.slot(4)][:, j, :], putr[g.slot(2)][:, j, :],
                                       start=True, stop=True)
                    mm.then_inc(expanded, 1)

                def step(at):
                    if g := at(3):
                        pe.wait_ge(v_ready, done(g))
                        prior(pe, s.out_ready, g, 1)
                        for c, a, b in lanes:
                            for j in range(a, b):
                                mm = pe.matmul(bank[c][:, (j - a) * P:(j - a) * P + D + H], same[g.slot(4)][:, j, :],
                                               vals3[g.slot(2)][:, j, :], start=True, stop=True)
                        mm.then_inc(s.summed, 1)
                    if g := at(1):
                        pe.wait_ge(scored, done(g))
                        prior(pe, scanned, g, 1)
                        pe.transpose(bank[2][0:GH, 0:P], sc[g.slot(4)], ident[:, :]).then_inc(turned, 1)
                    if g := at(0):
                        expand(g)
                    if g := at(1):
                        pe.wait_ge(mx, done(g))
                        prior(pe, dif_ready, g, 1)
                        pe.matmul(bank[3][:, 0:GH], smax, ident[0:GH, 0:GH], start=True, stop=True).then_inc(back, 1)
                ticks(pe, step)

            @block.scalar
            def _(act):
                def step(at):
                    if g := at(2):
                        act.wait_ge(dif_ready, done(g))
                        prior(act, s.summed, g, 2)
                        act.activation(vals3[g.slot(2)][:, :, D:D + H], dif.rearrange("p (g h) -> p g h", h=H),
                                       ACT.Exp).then_inc(e_ready, 1)
                    if g := at(3):
                        act.wait_ge(s.summed, done(g))
                        prior_dma(act, s.stored[g.slot(2)], g, 2)
                        to = s.out[g.slot(2)].rearrange("p (g w) -> p g w", w=W3)
                        act.copy(to[:, :, D + H:W3], mb[g.slot(4)].rearrange("p (g h) -> p g h", h=H))
                        for c, a, b in lanes:
                            ins = act.copy(to[:, a:b, 0:D + H],
                                           bank[c][:, :].rearrange("p (g w) -> p g w", g=4)[:, :, 0:D + H])
                        ins.then_inc(s.out_ready, 1)
                ticks(act, step)

    attention_pass()
    tmid = pick(W3)

    with when_mids("mids"):
        mT, flT, runT, runB = (gath[0:H, 896 * k:896 * k + T] for k in range(4))
        with nc.Block() as block:
            @block.tensor
            def _(pe):
                for k in range(TK):
                    pe.transpose(bank[k // 4][0:H, (k % 4) * P:(k % 4 + 1) * P], tmid[:, k, D + H:W3], ident[:, :])

        with nc.Block() as block:
            @block.vector
            def _(v):
                for k in range(TK):
                    w = min(P, T - k * P)
                    v.tensor_copy(mT[:, k * P:k * P + w], bank[k // 4][0:H, (k % 4) * P:(k % 4) * P + w])
                dve(v, v.memset(gath[0:H, 896:896 + T + 1], 0.0))
                dve(v, v.tensor_tensor(flT[:, 1:T], midrow[:, 1:T], midrow[:, 0:T - 1], ALU.not_equal))
                dve(v, v.tensor_scalar(flT[:, 1:T], flT[:, 1:T], NEG, None, ALU.mult))
                flR = gath[0:H, 897:897 + T]
                dve(v, v.tensor_tensor_scan(runT, flT, mT, NEG, ALU.add, ALU.max))
                dve(v, v.tensor_tensor_scan(reverse(runB, H, T), reverse(flR, H, T), reverse(mT, H, T), NEG, ALU.add, ALU.max))
                dve(v, v.tensor_tensor(runT, runT, runB, ALU.max))

        gcol = carve(600, (TK, H))
        mw = carve(640, (TK, H))
        ismid = carve(680, (TK,))
        tm3 = carve(1024, (TK, W3 + 1))
        with nc.Block() as block:
            @block.tensor
            def _(pe):
                for k in range(TK):
                    w = min(P, T - k * P)
                    pe.transpose(bank[0][0:w, k * H:(k + 1) * H], runT[:, k * P:k * P + w], ident[0:H, 0:H])

            @block.vector
            def _(v):
                v.memset(gcol, 0.0)

        with nc.Block() as block:
            @block.vector
            def _(v):
                g0 = bank[0][:, 0:TK * H].rearrange("p (k h) -> p k h", h=H)
                v.tensor_copy(gcol[:, 0:TK - 1, :], g0[:, 0:TK - 1, :])
                dve(v, v.tensor_copy(gcol[0:TL, TK - 1, :], g0[0:TL, TK - 1, :]))
                dve(v, v.tensor_tensor(mw, tmid[:, :, D + H:W3], gcol, ALU.subtract))
                dve(v, v.tensor_scalar(ismid, midnode[:, :], 0.0, None, ALU.is_ge))

        with nc.Block() as block:
            @block.scalar
            def _(act):
                act.activation(mw, mw, ACT.Exp)

        W4 = W3 + 1
        with nc.Block() as block:
            @block.vector
            def _(v):
                dve(v, v.tensor_tensor(mw, mw, ismid.unsqueeze(2).to_broadcast([P, TK, H]), ALU.mult))
                for k in range(TK):
                    v.tensor_tensor(tm3[:, k, 0:D].rearrange("p (h d) -> p h d", h=H),
                                    tmid[:, k, 0:D].rearrange("p (h d) -> p h d", h=H),
                                    mw[:, k, :].unsqueeze(2).to_broadcast([P, H, HD]), ALU.mult)
                v.tensor_tensor(tm3[:, :, D:D + H], tmid[:, :, D:D + H], mw, ALU.mult)
                v.tensor_tensor(tm3[:, :, D + H:W3], gcol, midlast[:, :].unsqueeze(2).to_broadcast([P, TK, H]), ALU.mult)
                dve(v, v.tensor_copy(tm3[:, :, W3:W4], midlast[:, :].unsqueeze(2)))
        r_mid = mids("p3", tm3, W4)
        top2 = carve(128, (NB, H), parts=NP)
        m_f, m_m = carve(256, (NB, H), parts=NP), carve(384, (NB, H), parts=NP)
        none = carve(700, (NB, 1), parts=NP)

        def scale_rows(v, r, by):
            for b in range(NB):
                a = r[:, b, 0:D].rearrange("p (h d) -> p h d", h=H)
                v.tensor_tensor(a, a, by[:, b, :].unsqueeze(2).to_broadcast([NP, H, HD]), ALU.mult)
            dve(v, v.tensor_tensor(r[:, :, D:D + H], r[:, :, D:D + H], by, ALU.mult))

        with nc.Block() as block:
            @block.vector
            def _(v):
                dve(v, v.tensor_scalar(none, r_mid[:, :, W3:W4], -1.0, -NEG, ALU.add, ALU.mult))
                mm = r_mid[:, :, D + H:W3]
                dve(v, v.tensor_tensor(mm, mm, none.to_broadcast([NP, NB, H]), ALU.add))
                dve(v, v.tensor_tensor(top2, r_first[:, :, D + H:W3], mm, ALU.max))
                v.tensor_tensor(m_f, r_first[:, :, D + H:W3], top2, ALU.subtract)
                dve(v, v.tensor_tensor(m_m, mm, top2, ALU.subtract))

        with nc.Block() as block:
            @block.scalar
            def _(act):
                act.activation(m_f, m_f, ACT.Exp)
                act.activation(m_m, m_m, ACT.Exp)

        with nc.Block() as block:
            @block.vector
            def _(v):
                scale_rows(v, r_first, m_f)
                scale_rows(v, r_mid, m_m)
                dve(v, v.tensor_tensor(r_first[:, :, 0:D + H], r_first[:, :, 0:D + H], r_mid[:, :, 0:D + H], ALU.add))
                dve(v, v.tensor_copy(r_first[:, :, D + H:W3], top2))
    ms = [carve(128 * k, (NB, H), parts=NP) for k in range(5)]
    with nc.Block() as block:
        @block.vector
        def _(v):
            top = ms[3]
            dve(v, v.tensor_tensor(top, r_last[:, :, D + H:W3], r_first[:, :, D + H:W3], ALU.max))
            dve(v, v.tensor_scalar(top, top, -1.0e9, None, ALU.max))
            for k, r in enumerate((r_last, r_first)):
                ins = v.tensor_tensor(ms[k], r[:, :, D + H:W3], top, ALU.subtract)
            dve(v, ins)

    with nc.Block() as block:
        @block.scalar
        def _(act):
            for k in range(2):
                act.activation(ms[k], ms[k], ACT.Exp)

    with nc.Block() as block:
        @block.vector
        def _(v):
            for k, r in enumerate((r_last, r_first)):
                v.tensor_tensor(r[:, :, 0:D].rearrange("p b (h d) -> p b h d", h=H),
                                r[:, :, 0:D].rearrange("p b (h d) -> p b h d", h=H),
                                ms[k].unsqueeze(3).to_broadcast([NP, NB, H, HD]), ALU.mult)
                dve(v, v.tensor_tensor(r[:, :, D:D + H], r[:, :, D:D + H], ms[k], ALU.mult))
            S = D + H
            dve(v, v.tensor_tensor(r_last[:, :, 0:S], r_last[:, :, 0:S], r_first[:, :, 0:S], ALU.add))
            dve(v, v.tensor_scalar(ms[4], r_last[:, :, D:S], 1e-12, None, ALU.add))
            dve(v, v.reciprocal(ms[3], ms[4]))
            dve(v, v.tensor_tensor(agg[:, :, :].rearrange("p b (h d) -> p b h d", h=H),
                                   r_last[:, :, 0:D].rearrange("p b (h d) -> p b h d", h=H),
                                   ms[3].unsqueeze(3).to_broadcast([NP, NB, H, HD]), ALU.mult))
    turn_nodes(agg, featT)
    project(featT, D + 1, wts["o"][:, :], D)
    with nc.Block() as block:
        @block.vector
        def _(v):
            for view, b, m in by_bank(D):
                v.tensor_copy(agg[:, b:b + m, :], view)
    residual(agg[:, :, :])
    with nc.Block() as block:
        @block.sync
        def _(sp):
            sp_io.by(sp.dma_start(nodes(out), xs[:, :, :]), 16)
            sp_io.all(sp)


_INS = ["x", "src", "dst", "edge_attr_2", "edge_type_4", "L0_gnn_W1", "L0_gnn_b1", "L0_gnn_W2", "L0_gnn_b2",
        "L2_gnn_flux_Wh", "L2_gnn_flux_bh", "L2_gnn_flux_Wo", "L2_gnn_flux_bo", "L2_gnn_flux_ln_w",
        "L2_gnn_flux_ln_b", "L2_gnn_a_Wh", "L2_gnn_a_bh", "L2_gnn_a_Wo", "L2_gnn_a_bo", "L2_gnn_a_ln_w",
        "L2_gnn_a_ln_b", "L3_gnn_Wq", "L3_gnn_bq", "L3_gnn_Wk", "L3_gnn_bk", "L3_gnn_Wv", "L3_gnn_bv",
        "L3_gnn_Wo", "L3_gnn_bo", "L3_gnn_edge_bias"]


def kernel(**inputs):
    import numpy as _np
    import concourse.bacc as _bacc
    from concourse import mybir as _mybir
    from concourse.bass_utils import run_bass_kernel_spmd as _run

    nc = _bacc.Bacc("TRN2", target_bir_lowering=False, num_devices=1)
    arrays, args = {}, []
    for name in _INS:
        a = _np.ascontiguousarray(inputs[name])
        arrays[f"in_{name}"] = a
        args.append(nc.dram_tensor(f"in_{name}", a.shape, _mybir.dt.from_np(a.dtype), kind="ExternalInput").ap())
    out = nc.dram_tensor("out_0", (N, D), F32, kind="ExternalOutput").ap()
    build(nc, *args, out)
    r = _run(nc, [arrays], core_ids=[0])
    return r.results[0]["out_0"]
```
